# Optimizing a Trainium2 kernel written in Bass

```python
import numpy as np
import jax
import jax.numpy as jnp

def _softmax(x, axis=-1):
    return jax.nn.softmax(x, axis=axis)

def _gelu(x):
    return jax.nn.gelu(x, approximate=True)

def _silu(x):
    return jax.nn.silu(x)

def _sigmoid(x):
    return jax.nn.sigmoid(x)

def _layernorm(x, axis=-1, eps=1e-05):
    m = jnp.mean(x, axis=axis, keepdims=True)
    v = jnp.var(x, axis=axis, keepdims=True)
    return (x - m) / jnp.sqrt(v + eps)

def _scatter_add(tgt, idx, src, axis=0):
    return tgt.at[idx].add(src)

def _segment_sum(src, seg, n):
    return jax.ops.segment_sum(src, seg, n)
kernel_name = 'mk_gnn_resnorm_d4_gnn_r32_598217'

def setup_inputs(seed: int=0):
    np.random.seed(seed)
    _w = jnp.asarray

    def _rec_inputs():
        import jax
        import jax.numpy as jnp
        _gk = jax.random.key(seed)
        x = -0.000202 + 1 * jax.random.normal(jax.random.fold_in(_gk, 1), (3125, 128), jnp.float32)
        src = jax.random.randint(jax.random.fold_in(_gk, 2), (50000,), 0, 3125, jnp.int32)
        dst = jax.random.randint(jax.random.fold_in(_gk, 3), (50000,), 0, 3125, jnp.int32)
        _o = jnp.argsort(dst, stable=True)
        src = src[_o]
        dst = dst[_o]
        edge_attr_10 = 0.000254407 + 0.99978 * jax.random.normal(jax.random.fold_in(_gk, 12), (50000, 10), jnp.float32)
        edge_attr_128 = -4.21973e-05 + 0.999841 * jax.random.normal(jax.random.fold_in(_gk, 13), (50000, 128), jnp.float32)
        return (x, src, dst, edge_attr_10, edge_attr_128)
    x, src, dst, edge_attr_10, edge_attr_128 = _rec_inputs()

    def _L0_gnn_setup():
        import jax, jax.numpy as jnp
        import numpy as np
        N_NODES = 50000
        N_EDGES = 18750
        DIM_H = 128
        LN_EPS = 1e-05

        def _layer_norm(x, gamma, beta):
            mu = jnp.mean(x, axis=-1, keepdims=True)
            var = jnp.mean(jnp.square(x - mu), axis=-1, keepdims=True)
            return gamma * (x - mu) * jax.lax.rsqrt(var + LN_EPS) + beta
        key = jax.random.key(seed)
        ks = jax.random.split(key, 8)
        s = 1.0 / np.sqrt(DIM_H)
        return {'nodes': jax.random.normal(ks[0], (N_NODES, DIM_H), jnp.float32), 'W_msg': jax.random.normal(ks[1], (DIM_H, DIM_H), jnp.float32) * s, 'b_msg': jnp.zeros((DIM_H,), jnp.float32), 'w_ih': jax.random.normal(ks[2], (3 * DIM_H, DIM_H), jnp.float32) * s, 'w_hh': jax.random.normal(ks[3], (3 * DIM_H, DIM_H), jnp.float32) * s, 'b_ih': jnp.zeros((3 * DIM_H,), jnp.float32), 'b_hh': jnp.zeros((3 * DIM_H,), jnp.float32), 'ln_gamma': jnp.ones((DIM_H,), jnp.float32), 'ln_beta': jnp.zeros((DIM_H,), jnp.float32), 'edge_src': jax.random.randint(ks[4], (N_EDGES,), 0, N_NODES, jnp.int32), 'edge_dst': jax.random.randint(ks[5], (N_EDGES,), 0, N_NODES, jnp.int32)}
    _L0_gnn_all = _L0_gnn_setup()
    _L0_gnn_in = {k: v for k, v in _L0_gnn_all.items() if k in ('W_msg', 'b_msg', 'w_ih', 'w_hh', 'b_ih', 'b_hh', 'ln_gamma', 'ln_beta')}
    del _L0_gnn_all

    def _L1_gnn_setup():
        import jax, jax.numpy as jnp
        import numpy as np
        N = 50000
        E = 25000
        D = 128
        H = 8
        C = D // H
        ED = 10
        FF = 4 * D

        def _layer(x, edge_index, edge_attr, Wq, bq, Wk, bk, Wv, bv, We, Wskip, bskip, Wbeta, gn_w, gn_b, gn_ms, W1, b1, W2, b2):
            n = x.shape[0]
            src, dst = (edge_index[0], edge_index[1])
            q = (x @ Wq + bq).reshape(n, H, C)
            k = (x @ Wk + bk).reshape(n, H, C)
            v = (x @ Wv + bv).reshape(n, H, C)
            e = (edge_attr @ We).reshape(-1, H, C)
            k_j = k[src] + e
            alpha = jnp.einsum('ehc,ehc->eh', q[dst], k_j) / jnp.sqrt(jnp.float32(C))
            amax = jax.ops.segment_max(alpha, dst, num_segments=n)
            ex = jnp.exp(alpha - amax[dst])
            denom = jax.ops.segment_sum(ex, dst, num_segments=n)
            alpha = ex / (denom[dst] + 1e-16)
            msg = (v[src] + e) * alpha[:, :, None]
            out = jax.ops.segment_sum(msg.reshape(-1, H * C), dst, num_segments=n)
            x_r = x @ Wskip + bskip
            beta = jax.nn.sigmoid(jnp.concatenate([out, x_r, out - x_r], axis=-1) @ Wbeta)
            x_att = beta * x_r + (1.0 - beta) * out
            h = x + x_att
            mean = h.mean(axis=0)
            hc = h - gn_ms * mean
            var = (hc * hc).mean(axis=0)
            h = hc / jnp.sqrt(var + 1e-05) * gn_w + gn_b
            ffn = jax.nn.gelu(h @ W1 + b1, approximate=False) @ W2 + b2
            return h + ffn
        key = jax.random.key(seed)
        ks = jax.random.split(key, 20)
        s = 0.05
        p = lambda k, shape: jax.random.normal(k, shape, jnp.float32) * s
        return {'x': jax.random.normal(ks[0], (N, D), jnp.float32), 'edge_index': jax.random.randint(ks[1], (2, E), 0, N), 'edge_attr': jax.random.normal(ks[2], (E, ED), jnp.float32), 'Wq': p(ks[3], (D, D)), 'bq': jnp.zeros((D,), jnp.float32), 'Wk': p(ks[4], (D, D)), 'bk': jnp.zeros((D,), jnp.float32), 'Wv': p(ks[5], (D, D)), 'bv': jnp.zeros((D,), jnp.float32), 'We': p(ks[6], (ED, D)), 'Wskip': p(ks[7], (D, D)), 'bskip': jnp.zeros((D,), jnp.float32), 'Wbeta': p(ks[8], (3 * D, 1)), 'gn_w': jnp.ones((D,), jnp.float32), 'gn_b': jnp.zeros((D,), jnp.float32), 'gn_ms': jnp.ones((D,), jnp.float32), 'W1': p(ks[9], (D, FF)), 'b1': jnp.zeros((FF,), jnp.float32), 'W2': p(ks[10], (FF, D)), 'b2': jnp.zeros((D,), jnp.float32)}
    _L1_gnn_all = _L1_gnn_setup()
    _L1_gnn_in = {k: v for k, v in _L1_gnn_all.items() if k in ('Wq', 'bq', 'Wk', 'bk', 'Wv', 'bv', 'We', 'Wskip', 'bskip', 'Wbeta', 'gn_w', 'gn_b', 'gn_ms', 'W1', 'b1', 'W2', 'b2')}
    del _L1_gnn_all

    def _L2_gnn_setup():
        import jax, jax.numpy as jnp
        import numpy as np
        EPS = 1e-07
        BETA = 1.0
        MSG_SCALE = 1.0
        N_NODES = 50000
        N_EDGES = 18750
        D = 128
        key = jax.random.key(seed)
        k1, k2, k3, k4, k5 = jax.random.split(key, 5)
        node_feats = jax.random.normal(k1, (N_NODES, D), dtype=jnp.float32)
        edge_feats = jax.random.normal(k2, (N_EDGES, D), dtype=jnp.float32)
        mlp_w = jax.random.normal(k3, (D, D), dtype=jnp.float32) / np.sqrt(D)
        mlp_b = jnp.zeros((D,), dtype=jnp.float32)
        src = jax.random.randint(k4, (N_EDGES,), 0, N_NODES)
        dst = jax.random.randint(k5, (N_EDGES,), 0, N_NODES)
        return {'node_feats': node_feats, 'edge_feats': edge_feats, 'mlp_w': mlp_w, 'mlp_b': mlp_b, 'src': src, 'dst': dst}
    _L2_gnn_all = _L2_gnn_setup()
    _L2_gnn_in = {k: v for k, v in _L2_gnn_all.items() if k in ('mlp_w', 'mlp_b')}
    del _L2_gnn_all

    def _L3_gnn_setup():
        import jax, jax.numpy as jnp
        import numpy as np
        N, E, F_IN, H, C = (50000, 25000, 128, 2, 64)
        NEG_SLOPE = 0.2

        def gat_conv(x, W, att_src, att_dst, b, src, dst):
            n = x.shape[0]
            h = (x @ W).reshape(n, H, C)
            loops = jnp.arange(n, dtype=src.dtype)
            s = jnp.concatenate([src, loops])
            d = jnp.concatenate([dst, loops])
            a_s = jnp.einsum('nhc,hc->nh', h, att_src)
            a_d = jnp.einsum('nhc,hc->nh', h, att_dst)
            e = jax.nn.leaky_relu(a_s[s] + a_d[d], NEG_SLOPE)
            m = jax.ops.segment_max(e, d, num_segments=n)
            p = jnp.exp(e - m[d])
            denom = jax.ops.segment_sum(p, d, num_segments=n)
            alpha = p / (denom[d] + 1e-16)
            out = jax.ops.segment_sum(h[s] * alpha[:, :, None], d, num_segments=n)
            return out.reshape(n, H * C) + b
        key = jax.random.key(seed)
        ks = jax.random.split(key, 16)
        rn = lambda k, shape, s=0.1: jax.random.normal(k, shape, jnp.float32) * s
        return {'x': jax.random.normal(ks[0], (N, F_IN), jnp.float32), 'src': jax.random.randint(ks[1], (E,), 0, N, jnp.int32), 'dst': jax.random.randint(ks[2], (E,), 0, N, jnp.int32), 'W1': rn(ks[3], (F_IN, H * C)), 'att_src1': rn(ks[4], (H, C)), 'att_dst1': rn(ks[5], (H, C)), 'b1': rn(ks[6], (H * C,)), 'Wsk1': rn(ks[7], (F_IN, H * C)), 'bsk1': rn(ks[8], (H * C,)), 'W2': rn(ks[9], (H * C, H * C)), 'att_src2': rn(ks[10], (H, C)), 'att_dst2': rn(ks[11], (H, C)), 'b2': rn(ks[12], (H * C,)), 'Wsk2': rn(ks[13], (H * C, H * C)), 'bsk2': rn(ks[14], (H * C,))}
    _L3_gnn_all = _L3_gnn_setup()
    _L3_gnn_in = {k: v for k, v in _L3_gnn_all.items() if k in ('W1', 'att_src1', 'att_dst1', 'b1', 'Wsk1', 'bsk1', 'W2', 'att_src2', 'att_dst2', 'b2', 'Wsk2', 'bsk2')}
    del _L3_gnn_all
    return {'x': x, 'src': src, 'dst': dst, 'edge_attr_10': edge_attr_10, 'edge_attr_128': edge_attr_128, 'L0_gnn_W_msg': _L0_gnn_in['W_msg'], 'L0_gnn_b_msg': _L0_gnn_in['b_msg'], 'L0_gnn_w_ih': _L0_gnn_in['w_ih'], 'L0_gnn_w_hh': _L0_gnn_in['w_hh'], 'L0_gnn_b_ih': _L0_gnn_in['b_ih'], 'L0_gnn_b_hh': _L0_gnn_in['b_hh'], 'L0_gnn_ln_gamma': _L0_gnn_in['ln_gamma'], 'L0_gnn_ln_beta': _L0_gnn_in['ln_beta'], 'L1_gnn_Wq': _L1_gnn_in['Wq'], 'L1_gnn_bq': _L1_gnn_in['bq'], 'L1_gnn_Wk': _L1_gnn_in['Wk'], 'L1_gnn_bk': _L1_gnn_in['bk'], 'L1_gnn_Wv': _L1_gnn_in['Wv'], 'L1_gnn_bv': _L1_gnn_in['bv'], 'L1_gnn_We': _L1_gnn_in['We'], 'L1_gnn_Wskip': _L1_gnn_in['Wskip'], 'L1_gnn_bskip': _L1_gnn_in['bskip'], 'L1_gnn_Wbeta': _L1_gnn_in['Wbeta'], 'L1_gnn_gn_w': _L1_gnn_in['gn_w'], 'L1_gnn_gn_b': _L1_gnn_in['gn_b'], 'L1_gnn_gn_ms': _L1_gnn_in['gn_ms'], 'L1_gnn_W1': _L1_gnn_in['W1'], 'L1_gnn_b1': _L1_gnn_in['b1'], 'L1_gnn_W2': _L1_gnn_in['W2'], 'L1_gnn_b2': _L1_gnn_in['b2'], 'L2_gnn_mlp_w': _L2_gnn_in['mlp_w'], 'L2_gnn_mlp_b': _L2_gnn_in['mlp_b'], 'L3_gnn_W1': _L3_gnn_in['W1'], 'L3_gnn_att_src1': _L3_gnn_in['att_src1'], 'L3_gnn_att_dst1': _L3_gnn_in['att_dst1'], 'L3_gnn_b1': _L3_gnn_in['b1'], 'L3_gnn_Wsk1': _L3_gnn_in['Wsk1'], 'L3_gnn_bsk1': _L3_gnn_in['bsk1'], 'L3_gnn_W2': _L3_gnn_in['W2'], 'L3_gnn_att_src2': _L3_gnn_in['att_src2'], 'L3_gnn_att_dst2': _L3_gnn_in['att_dst2'], 'L3_gnn_b2': _L3_gnn_in['b2'], 'L3_gnn_Wsk2': _L3_gnn_in['Wsk2'], 'L3_gnn_bsk2': _L3_gnn_in['bsk2']}

def reference(x, src, dst, edge_attr_10, edge_attr_128, L0_gnn_W_msg, L0_gnn_b_msg, L0_gnn_w_ih, L0_gnn_w_hh, L0_gnn_b_ih, L0_gnn_b_hh, L0_gnn_ln_gamma, L0_gnn_ln_beta, L1_gnn_Wq, L1_gnn_bq, L1_gnn_Wk, L1_gnn_bk, L1_gnn_Wv, L1_gnn_bv, L1_gnn_We, L1_gnn_Wskip, L1_gnn_bskip, L1_gnn_Wbeta, L1_gnn_gn_w, L1_gnn_gn_b, L1_gnn_gn_ms, L1_gnn_W1, L1_gnn_b1, L1_gnn_W2, L1_gnn_b2, L2_gnn_mlp_w, L2_gnn_mlp_b, L3_gnn_W1, L3_gnn_att_src1, L3_gnn_att_dst1, L3_gnn_b1, L3_gnn_Wsk1, L3_gnn_bsk1, L3_gnn_W2, L3_gnn_att_src2, L3_gnn_att_dst2, L3_gnn_b2, L3_gnn_Wsk2, L3_gnn_bsk2):
    import jax
    import jax.numpy as jnp

    def _L0_gnn_ref(nodes, W_msg, b_msg, w_ih, w_hh, b_ih, b_hh, ln_gamma, ln_beta, edge_src, edge_dst):
        import jax, jax.numpy as jnp
        import numpy as np
        N_NODES = 50000
        N_EDGES = 18750
        DIM_H = 128
        LN_EPS = 1e-05

        def _layer_norm(x, gamma, beta):
            mu = jnp.mean(x, axis=-1, keepdims=True)
            var = jnp.mean(jnp.square(x - mu), axis=-1, keepdims=True)
            return gamma * (x - mu) * jax.lax.rsqrt(var + LN_EPS) + beta
        n_nodes = nodes.shape[0]
        msg_e = nodes[edge_src] @ W_msg.T + b_msg
        messages = jax.ops.segment_sum(msg_e, edge_dst, num_segments=n_nodes)
        msg = messages + jnp.mean(nodes, axis=0)
        gi = msg @ w_ih.T + b_ih
        gh = nodes @ w_hh.T + b_hh
        i_r, i_z, i_n = jnp.split(gi, 3, axis=-1)
        h_r, h_z, h_n = jnp.split(gh, 3, axis=-1)
        r = jax.nn.sigmoid(i_r + h_r)
        z = jax.nn.sigmoid(i_z + h_z)
        n = jnp.tanh(i_n + r * h_n)
        h_next = (1.0 - z) * n + z * nodes
        out = _layer_norm(h_next, ln_gamma, ln_beta)
        out = out + messages
        return out

    def _L1_gnn_ref(x, edge_index, edge_attr, Wq, bq, Wk, bk, Wv, bv, We, Wskip, bskip, Wbeta, gn_w, gn_b, gn_ms, W1, b1, W2, b2):
        import jax, jax.numpy as jnp
        import numpy as np
        N = 50000
        E = 25000
        D = 128
        H = 8
        C = D // H
        ED = 10
        FF = 4 * D

        def _layer(x, edge_index, edge_attr, Wq, bq, Wk, bk, Wv, bv, We, Wskip, bskip, Wbeta, gn_w, gn_b, gn_ms, W1, b1, W2, b2):
            n = x.shape[0]
            src, dst = (edge_index[0], edge_index[1])
            q = (x @ Wq + bq).reshape(n, H, C)
            k = (x @ Wk + bk).reshape(n, H, C)
            v = (x @ Wv + bv).reshape(n, H, C)
            e = (edge_attr @ We).reshape(-1, H, C)
            k_j = k[src] + e
            alpha = jnp.einsum('ehc,ehc->eh', q[dst], k_j) / jnp.sqrt(jnp.float32(C))
            amax = jax.ops.segment_max(alpha, dst, num_segments=n)
            ex = jnp.exp(alpha - amax[dst])
            denom = jax.ops.segment_sum(ex, dst, num_segments=n)
            alpha = ex / (denom[dst] + 1e-16)
            msg = (v[src] + e) * alpha[:, :, None]
            out = jax.ops.segment_sum(msg.reshape(-1, H * C), dst, num_segments=n)
            x_r = x @ Wskip + bskip
            beta = jax.nn.sigmoid(jnp.concatenate([out, x_r, out - x_r], axis=-1) @ Wbeta)
            x_att = beta * x_r + (1.0 - beta) * out
            h = x + x_att
            mean = h.mean(axis=0)
            hc = h - gn_ms * mean
            var = (hc * hc).mean(axis=0)
            h = hc / jnp.sqrt(var + 1e-05) * gn_w + gn_b
            ffn = jax.nn.gelu(h @ W1 + b1, approximate=False) @ W2 + b2
            return h + ffn
        return _layer(x, edge_index, edge_attr, Wq, bq, Wk, bk, Wv, bv, We, Wskip, bskip, Wbeta, gn_w, gn_b, gn_ms, W1, b1, W2, b2)

    def _L2_gnn_ref(node_feats, edge_feats, mlp_w, mlp_b, src, dst):
        import jax, jax.numpy as jnp
        import numpy as np
        EPS = 1e-07
        BETA = 1.0
        MSG_SCALE = 1.0
        N_NODES = 50000
        N_EDGES = 18750
        D = 128
        n = node_feats.shape[0]
        m = jax.nn.relu(node_feats[src] + edge_feats) + EPS
        logits = m * BETA
        seg_max = jax.ops.segment_max(logits, dst, num_segments=n)
        ex = jnp.exp(logits - seg_max[dst])
        denom = jax.ops.segment_sum(ex, dst, num_segments=n)
        a = ex / denom[dst]
        agg = jax.ops.segment_sum(m * a, dst, num_segments=n)
        msg = agg / jnp.maximum(jnp.linalg.norm(agg, axis=-1, keepdims=True), 1e-12)
        feat_norm = jnp.linalg.norm(node_feats, axis=-1, keepdims=True)
        feats = node_feats + msg * feat_norm * MSG_SCALE
        return feats @ mlp_w + mlp_b

    def _L3_gnn_ref(x, W1, att_src1, att_dst1, b1, Wsk1, bsk1, W2, att_src2, att_dst2, b2, Wsk2, bsk2, src, dst):
        import jax, jax.numpy as jnp
        import numpy as np
        N, E, F_IN, H, C = (50000, 25000, 128, 2, 64)
        NEG_SLOPE = 0.2

        def gat_conv(x, W, att_src, att_dst, b, src, dst):
            n = x.shape[0]
            h = (x @ W).reshape(n, H, C)
            loops = jnp.arange(n, dtype=src.dtype)
            s = jnp.concatenate([src, loops])
            d = jnp.concatenate([dst, loops])
            a_s = jnp.einsum('nhc,hc->nh', h, att_src)
            a_d = jnp.einsum('nhc,hc->nh', h, att_dst)
            e = jax.nn.leaky_relu(a_s[s] + a_d[d], NEG_SLOPE)
            m = jax.ops.segment_max(e, d, num_segments=n)
            p = jnp.exp(e - m[d])
            denom = jax.ops.segment_sum(p, d, num_segments=n)
            alpha = p / (denom[d] + 1e-16)
            out = jax.ops.segment_sum(h[s] * alpha[:, :, None], d, num_segments=n)
            return out.reshape(n, H * C) + b
        h = gat_conv(x, W1, att_src1, att_dst1, b1, src, dst) + x @ Wsk1 + bsk1
        h = jax.nn.relu(h)
        out = gat_conv(h, W2, att_src2, att_dst2, b2, src, dst) + h @ Wsk2 + bsk2
        return out
    edge_index = jnp.stack([src, dst])
    x = _layernorm(x + _L0_gnn_ref(x, L0_gnn_W_msg, L0_gnn_b_msg, L0_gnn_w_ih, L0_gnn_w_hh, L0_gnn_b_ih, L0_gnn_b_hh, L0_gnn_ln_gamma, L0_gnn_ln_beta, src, dst), axis=-1)
    x = _layernorm(x + _L1_gnn_ref(x, edge_index, edge_attr_10, L1_gnn_Wq, L1_gnn_bq, L1_gnn_Wk, L1_gnn_bk, L1_gnn_Wv, L1_gnn_bv, L1_gnn_We, L1_gnn_Wskip, L1_gnn_bskip, L1_gnn_Wbeta, L1_gnn_gn_w, L1_gnn_gn_b, L1_gnn_gn_ms, L1_gnn_W1, L1_gnn_b1, L1_gnn_W2, L1_gnn_b2), axis=-1)
    x = _layernorm(x + _L2_gnn_ref(x, edge_attr_128, L2_gnn_mlp_w, L2_gnn_mlp_b, src, dst), axis=-1)
    x = _layernorm(x + _L3_gnn_ref(x, L3_gnn_W1, L3_gnn_att_src1, L3_gnn_att_dst1, L3_gnn_b1, L3_gnn_Wsk1, L3_gnn_bsk1, L3_gnn_W2, L3_gnn_att_src2, L3_gnn_att_dst2, L3_gnn_b2, L3_gnn_Wsk2, L3_gnn_bsk2, src, dst), axis=-1)
    return x

_drawn_inputs = setup_inputs


def setup_inputs(seed=0):
    import zlib

    import numpy as np

    out = dict(_drawn_inputs(seed))
    spreads = {'L0_gnn_b_msg': (0.0, 0.1),
     'L0_gnn_b_ih': (0.0, 0.8),
     'L0_gnn_b_hh': (0.0, 0.8),
     'L0_gnn_ln_gamma': (1.0, 0.541),
     'L0_gnn_ln_beta': (0.0, 0.553),
     'L1_gnn_bq': (0.0, 0.8),
     'L1_gnn_bk': (0.0, 0.8),
     'L1_gnn_bv': (0.0, 0.8),
     'L1_gnn_bskip': (0.0, 0.8),
     'L1_gnn_gn_w': (1.0, 0.2),
     'L1_gnn_gn_b': (0.0, 0.1),
     'L1_gnn_gn_ms': (1.0, 0.2),
     'L1_gnn_b1': (0.0, 0.1),
     'L1_gnn_b2': (0.0, 0.1),
     'L2_gnn_mlp_b': (0.0, 0.1)}
    factors = {'edge_attr_10': 5.645, 'L1_gnn_Wq': 5.684, 'L1_gnn_Wk': 5.837, 'L1_gnn_We': 5.803}
    for name, (base, spread) in spreads.items():
        noise = np.random.default_rng([zlib.crc32(name.encode()), seed]).standard_normal(out[name].shape)
        drawn = base * np.exp(spread * noise) if base else spread * noise
        out[name] = jnp.asarray(drawn.astype(out[name].dtype))
    for name, factor in factors.items():
        out[name] = (out[name] * factor).astype(out[name].dtype)
    return out
```

```python
from contextlib import ExitStack

import numpy as np

import concourse.bass as bass
from concourse import mybir

F32 = mybir.dt.float32
BF16 = mybir.dt.bfloat16
I32 = mybir.dt.int32
U32 = mybir.dt.uint32
ALU = mybir.AluOpType
ACT = mybir.ActivationFunctionType
AX = mybir.AxisListType.X

NODES, EDGES, D, EDGE_D = 3125, 50000, 128, 10
P = 128
TILES = -(-NODES // P)
NP = TILES * P
GE = 512
CH = GE // P
GROUPS = -(-EDGES // GE)
EP = GROUPS * GE
CHUNKS = EP // P
PAIRS = GROUPS // 2
LOW = -3.0e38
BANK = 512

HEADS1, HEADS3 = 8, 2
KINDS = {
    "e0": dict(kind="sum", row=D, out=D),
    "e1": dict(kind="attn", row=2 * D, out=D + HEADS1),
    "e2": dict(kind="soft", row=D, out=2 * D),
    "e3": dict(kind="gat", row=2 * D, out=D + 3 * HEADS3),
    "e4": dict(kind="gat", row=2 * D, out=D + 3 * HEADS3),
}

WEIGHTS = [("w_msg", 128), ("w_ih", 384), ("w_hh", 384), ("wq", 128), ("wk", 128), ("wv", 128), ("wskip", 128),
           ("ffn1", 512), ("ffn2", 512), ("mlp", 128), ("g1", 128), ("g1s", 128), ("g2", 128), ("g2s", 128),
           ("ident", 128), ("ones", 128), ("avg", 128), ("upper", 128), ("strict", 128),
           ("heads8", 128), ("heads2", 128), ("pick8", HEADS1), ("pick2", HEADS3), ("iota", 128), ("part", 1),
           ("node", TILES), ("beta", 3),
           ("b_ih", 3), ("b_hh", 3), ("gamma0", 1), ("beta0", 1), ("bskip", 1), ("gn_w", 1), ("gn_b", 1),
           ("gn_ms", 1), ("fb1", 4), ("fb2", 1), ("mlp_b", 1),
           ("att_s1", 1), ("att_d1", 1), ("g1b", 1), ("g1sb", 1),
           ("att_s2", 1), ("att_d2", 1), ("g2b", 1), ("g2sb", 1)]
ROWS = [("b_msg", 128), ("bq", 128), ("bk", 128), ("bv", 128), ("one", 128)]


def columns(spec):
    at, out = 0, {}
    for name, n in spec:
        out[name] = (at, n)
        at += n
    return out, at


WCOL, WIDTH = columns(WEIGHTS)
RCOL, RWIDTH = columns(ROWS)



def norm_steps(p):
    return [(f"{p}.mean", 1), (f"{p}.center", 1), (f"{p}.square", 1), (f"{p}.var", 1), (f"{p}.std", 1),
            (f"{p}.inv", 1), (f"{p}.scale", 1)]


def gat_steps(p):
    return [(f"{p}.hT", 1), (f"{p}.hT_out", 1), (f"{p}.att", 2), (f"{p}.h", 1), (f"{p}.h_out", 2),
            (f"{p}.as", 1), (f"{p}.as_out", 1), (f"{p}.ad", 1), (f"{p}.ad_out", 1),
            (f"{p}.self_z", 1), (f"{p}.self", 1),
            (f"{p}.table", 16), (f"{p}.spread", 1), (f"{p}.edges", 0), (f"{p}.ends", 1),
            (f"{p}.m", 1), (f"{p}.m_live", 1), (f"{p}.m_mask", 1), (f"{p}.m_all", 1), (f"{p}.we_x", 1), (f"{p}.ws_x", 1),
            (f"{p}.we", 1), (f"{p}.ws", 1), (f"{p}.we_live", 1), (f"{p}.den", 1), (f"{p}.den2", 1), (f"{p}.den3", 1),
            (f"{p}.rden", 1), (f"{p}.we_n", 1), (f"{p}.ws_n", 1), (f"{p}.num", 1), (f"{p}.hs", 1), (f"{p}.agg", 1),
            (f"{p}.bias", 1), (f"{p}.sum", 1), (f"{p}.act", 1)]


STEPS = (
    [("load", 16 * 12)]
    + [("s.start", 1), ("s.keep", 1), ("s.next", 1), ("s.reset", 1), ("s.count", 1), ("s.before", 1), ("s.rho", 1),
       ("s.first", 1), ("s.rank", 1), ("s.save", 16 * 4), ("s.first_row", 16),
       ("s.lo", 1), ("s.hi", 1), ("s.lof", 1), ("s.hif", 1), ("s.deg", 0), ("s.deg_out", 1), ("s.live", 1),
       ("s.within", 2), ("s.total", 2), ("s.total_out", 1), ("s.run", 1), ("s.end", 1), ("s.end2", 1), ("s.end3", 1),
       ("s.nrun", 1), ("s.nlive", 1), ("s.nlive2", 1), ("s.nlive3", 1), ("s.empty", 1), ("s.empty2", 1),
       ("s.slot", 1), ("s.slot2", 1), ("s.slot3", 1),
       ("s.deg_save", 16), ("s.deg_row", 16)]
    + [("e0.edges", 0), ("e0.ends", 1), ("e0.mask", 1), ("e0.turn", 1), ("e0.turned", 1), ("msg", 1),
       ("msg_out", 1), ("mean", 1), ("mean2", 1), ("msg_mean", 1), ("gb", 1), ("r", 1), ("r_out", 1), ("z", 1), ("z_out", 1),
       ("hn", 1), ("hn_out", 1), ("in", 1), ("in_out", 1), ("n", 1), ("h1", 1), ("h2", 1), ("h3", 1)]
    + norm_steps("ln0") + [("y0a", 1), ("y0b", 1), ("y0c", 1)] + norm_steps("n0")
    + [("k", 1), ("k_out", 1), ("v", 1), ("v_out", 1), ("q", 1), ("q_out", 1), ("kv_table", 16),
       ("q_spread", 1), ("e1.edges", 0), ("e1.ends", 1),
       ("a.den", 1), ("a.rden", 1), ("a.live", 1), ("a.norm", 1), ("a.turn", 1), ("a.turned", 1),
       ("skip", 1), ("skip_out", 1), ("a.diff", 1), ("a.wb", 3), ("a.gate", 1), ("a.gate_out", 1),
       ("a.mix", 1), ("a.att", 1), ("a.h", 1), ("gn.sum", 1), ("gn.mean", 1), ("gn.center", 1), ("gn.sq", 1),
       ("gn.var", 1), ("gn.std", 1), ("gn.inv", 1), ("gn.gain", 1), ("gn.out", 1)]
    + [(f"ffn{c}{o}", 1) for c in range(4) for o in ("", "_out")]
    + [("ffn", 1), ("ffn_out", 1), ("y1", 1)] + norm_steps("n1")
    + [("x2", 1), ("x2_out", 1), ("x2_table", 16), ("e2.edges", 0), ("e2.ends", 1),
       ("c.rden", 1), ("c.norm", 1), ("c.mask", 1), ("c.turn", 1), ("c.turned", 1), ("c.sqa", 1), ("c.na", 1),
       ("c.maxa", 1), ("c.roota", 1), ("c.inva", 1), ("c.sqx", 1), ("c.nx", 1), ("c.maxx", 1), ("c.rootx", 1),
       ("c.unit", 1), ("c.scaled", 1), ("c.feat", 1), ("c.mlp", 1), ("c.mlp_out", 1), ("y2", 1)] + norm_steps("n2")
    + gat_steps("e3") + gat_steps("e4") + norm_steps("n3") + [("y", 1), ("y_out", 1), ("y_save", 16)]
)
BEFORE = {}
_at = 0
for _name, _n in STEPS:
    assert _name not in BEFORE, _name
    BEFORE[_name] = _at
    _at += _n
ALL_STEPS = _at


def gnn(nc, t):
    with ExitStack() as ctx:
        def sb(name, shape, dt=F32):
            return ctx.enter_context(nc.sbuf_tensor(name, shape, dt))

        def sem(name):
            return ctx.enter_context(nc.semaphore(name))

        def dram(name, shape, dt=F32):
            return nc.dram_tensor(name, shape, dt, kind="Internal").ap()

        rank_d = dram("rank_d", [EP], BF16)
        reset_d = dram("reset_d", [EP], BF16)
        keep_d = dram("keep_d", [EP], BF16)
        first_d = dram("first_d", [1, CHUNKS], I32)
        deg_d = dram("deg_d", [NP])
        window_d = {e: dram(f"{e}_window", [NP + P, D]) for e in ("e1", "e3", "e4")}
        table_d = {"e0": t["x"]}
        for e in ("e1", "e2", "e3", "e4"):
            table_d[e] = dram(f"{e}_table", [NP, KINDS[e]["row"]])
        out_d = {e: dram(f"{e}_out", [EP, KINDS[e]["out"]]) for e in KINDS}

        W = sb("W", [P, WIDTH])
        rows = sb("rows", [1, RWIDTH])

        def w(name, lo=0, n=None, p=P):
            a, k = WCOL[name]
            return W[0:p, a + lo:a + (k if n is None else lo + n)]

        def row(name):
            a, k = RCOL[name]
            return rows[0:1, a:a + k]

        src = sb("src", [P, CHUNKS], U32)
        live = sb("live", [P, TILES])
        slot = sb("slot", [P, TILES], U32)
        last = sb("last", [P, TILES], U32)
        X = sb("X", [P, NP])
        A = sb("A", [P, NP])
        B = sb("B", [P, NP])
        C = sb("C", [P, NP])
        S1 = sb("S1", [P, NP])
        R = sb("R", [P, TILES, 2 * D])
        R2 = R[:, :, :].rearrange("p t d -> p (t d)")
        G4 = [A, B, R2[:, 0:NP], R2[:, NP:2 * NP]]
        s8 = sb("s8", [P, 8, TILES, HEADS1])
        eps = sb("eps", [P, 1])
        col = sb("col", [P, 8])
        attm = sb("attm", [P, 2, P])

        MAXROW = 2 * D
        rows_in = sb("rows_in", [P, 2, CH, MAXROW])
        idx = sb("idx", [P, 2, CH], U32)
        rank_b = sb("rank_b", [P, 2, GE], BF16)
        flag_b = sb("flag_b", [P, 2, GE], BF16)
        ea = sb("ea", [P, 2, GE])
        win = sb("win", [P, 2, CH, D])
        one_hot = sb("one_hot", [P, 2, GE])
        qx = sb("qx", [P, GE])
        prod = sb("prod", [P, GE])
        score = sb("score", [P, 2, GE])
        U = sb("U", [P, 2, GE + 1])
        xd = sb("xd", [P, 2, GE])
        clip = sb("clip", [P, 2, GE])
        pw = sb("pw", [P, 2, GE])
        rw = sb("rw", [P, 2, GE])
        pv = sb("pv", [P, GE])
        den = sb("den", [P, 2, GE])
        num = sb("num", [P, 2, GE])
        rows_out = sb("rows_out", [P, 2, CH, MAXROW])

        PS = ctx.enter_context(nc.psum_tensor("PS", [P, 8 * BANK], F32))
        PN = PS[:, 0:NP]
        PM = PS[:, 7 * BANK:8 * BANK]

        def bank(b, n=BANK):
            return PS[:, b * BANK:b * BANK + n]

        V_BANK, K_BANK, Q_BANK, A_BANK = 0, 2, 3, 4
        OUT_BANK = {"sum": 5, "attn": 5, "soft": 5, "gat": 3}

        node_step = sem("node_step")
        moved = sem("moved")
        moved_tiles = [0]

        def moves_done(pool):
            moved_tiles[0] += TILES
            pool.wait_ge(moved, 16 * moved_tiles[0])
            pool.sem_inc(node_step, 1)

        gate_pool = sem("gate_pool")
        gate_sp = sem("gate_sp")
        deg_hot = sem("deg_hot")
        deg_mm = sem("deg_mm")
        SEM = {}
        for e in KINDS:
            for n in ("idx_here", "k_ready", "q_ready", "expanded", "one_hot", "q_copied", "product", "scored", "u", "u_head", "x", "clipped",
                      "weights", "pv", "den", "num", "turned", "evac"):
                if not (KINDS[e]["kind"] == "sum" and n in ("k_ready", "q_ready", "one_hot", "q_copied", "product", "scored", "u", "u_head",
                                                            "x", "clipped", "weights", "pv", "den")):
                    SEM[e, n] = sem(f"{e}_{n}")
            for n in ("rows_here", "rank_here", "flag_here", "edge_here", "attr_here", "stored"):
                for s in range(2):
                    SEM[e, n, s] = sem(f"{e}_{n}{s}")

        def turn(eng, name):
            eng.wait_ge(node_step, BEFORE[name])

        def need(eng, s, value):
            if not isinstance(value, int) or value > 0:
                eng.wait_ge(s, value)

        def past(g, n):
            return not isinstance(g, int) or g >= n

        def below(g, n):
            return not isinstance(g, int) or g < n

        def stream(eng, body):
            for g in range(4):
                body(g, g % 2, g // 2)
            with eng.Fori(2, PAIRS - 1) as i:
                for s in range(2):
                    body(2 * i + s, s, i)
            for g in (GROUPS - 2, GROUPS - 1):
                body(g, g % 2, g // 2)

        def prev(u, s):
            return u if s == 0 else u + 1

        L = GROUPS
        dst_i = A[0:L, 0:3 * GE].bitcast(I32).rearrange("p (n e) -> p n e", n=3)
        dst_line = [dst_i[:, n, :] for n in range(3)]
        start_l = B[0:L, 0:GE]
        count_l = B[0:L, GE:2 * GE]
        rho_l = B[0:L, 2 * GE:3 * GE]
        next_l = B[0:L, 3 * GE:4 * GE]
        one_l = B[0:L, 4 * GE:5 * GE]
        rank_l = one_hot[0:L, 0, 0:GE // 2].bitcast(BF16)
        reset_l = one_hot[0:L, 0, GE // 2:GE].bitcast(BF16)
        keep_l = one_hot[0:L, 1, 0:GE // 2].bitcast(BF16)
        first_l = one_hot[0:L, 1, GE // 2:GE // 2 + CH].bitcast(I32)
        dst_col = S1[:, 0:CHUNKS].bitcast(I32)
        lo_i = S1[:, CHUNKS:2 * CHUNKS].bitcast(I32)
        hi_i = S1[:, 2 * CHUNKS:3 * CHUNKS].bitcast(I32)
        lo_f = S1[:, 3 * CHUNKS:4 * CHUNKS]
        hi_f = S1[:, 4 * CHUNKS:5 * CHUNKS]
        lo_hot = pv[:, 0:P].bitcast(BF16).rearrange("p (s n) -> p s n", s=2)
        hi_hot = pv[:, P:P + 32].bitcast(BF16).rearrange("p (s n) -> p s n", s=2)[:, :, 0:TILES]
        deg = sb("deg", [P, TILES])
        first_s = sb("first_s", [1, CHUNKS], I32)
        z = [sb(f"z{k}", [P, TILES]) for k in range(8)]
        wb3 = sb("wb3", [P, P])
        We = sb("We", [EDGE_D, D])
        Wrow = {"e1": C[:, :].rearrange("p (t d) -> p t d", d=D)}
        Wrow["e3"] = Wrow["e4"] = Wrow["e1"]


        def edges_sync(sp, e):
            kind = KINDS[e]["kind"]
            turn(sp, f"{e}.edges")
            flag = keep_d if kind == "sum" else reset_d

            def load_flag(g, s, u):
                if past(g, 2):
                    sp.wait_ge(SEM[e, "num" if kind == "sum" else "u"], g - 1)
                sp.sem_inc(gate_sp, 1)
                sp.dma_start(flag_b[:, s, :], flag[bass.ds(g * GE, GE)].partition_broadcast(P)).then_inc(
                    SEM[e, "flag_here", s], 16)

            def body(g, s, u):
                if kind in ("attn", "gat"):
                    if past(g, 2):
                        sp.wait_ge(SEM[e, "one_hot"], g - 1)
                    sp.dma_start(rank_b[:, s, :], rank_d[bass.ds(g * GE, GE)].partition_broadcast(P)).then_inc(
                        SEM[e, "rank_here", s], 16)
                    if past(g, 2):
                        sp.wait_ge(SEM[e, "q_ready"], g - 1)
                    sp.sem_inc(gate_sp, 1)
                    _, firsts = nc.values_load_multi_w_load_instructions(
                        first_s[0:1, bass.ds(g * CH, CH)], engines=[mybir.EngineType.SP], min_val=0, max_val=NP - 1)
                    for j in range(CH):
                        sp.dma_start(win[:, s, j, :], window_d[e][bass.ds(firsts[j], P), :]).then_inc(
                            SEM[e, "edge_here", s], 16)
                if kind in ("attn", "soft"):
                    if past(g, 2):
                        sp.wait_ge(SEM[e, "expanded"], g - 1)
                    sp.sem_inc(gate_sp, 1)
                if kind == "attn":
                    sp.dma_start(ea[0:EDGE_D, s, :], t["ea10"][:, bass.ds(g * GE, GE)]).then_inc(
                        SEM[e, "attr_here", s], 16)
                if kind == "soft":
                    sp.dma_start(ea[:, s, :].rearrange("p (c d) -> p c d", c=CH),
                                 t["ea128"][bass.ds(g * GE, GE), :].rearrange("(c p) d -> p c d", p=P)).then_inc(
                        SEM[e, "attr_here", s], 16)
                if past(g, 1):
                    load_flag(g - 1, 1 - s, prev(u, s) - 1)

            stream(sp, body)
            load_flag(GROUPS - 1, 1, PAIRS - 1)

        def spread(pool, e, name):
            turn(pool, name)
            for i in range(TILES):
                pool.indirect_dma_start(window_d[e], bass.IndirectOffsetOnAxis(ap=slot[:, i:i + 1], axis=0),
                                        Wrow[e][:, i, :], None).then_inc(moved, 16)
            moves_done(pool)

        def edges_gpsimd(pool, e):
            k = KINDS[e]["row"]

            def body(g, s, u):
                if past(g, 2):
                    pool.wait_ge(SEM[e, "expanded"], g - 1)
                pool.wait_ge(SEM[e, "idx_here"], g + 1)
                pool.sem_inc(gate_pool, 1)
                for j in range(CH):
                    pool.indirect_dma_start(rows_in[:, s, j, 0:k], None, table_d[e], bass.IndirectOffsetOnAxis(
                        ap=idx[:, s, j:j + 1], axis=0)).then_inc(SEM[e, "rows_here", s], 16)

            stream(pool, body)

        def linear(pe, name, terms):
            turn(pe, name)
            for lo in range(0, NP, BANK):
                n = min(BANK, NP - lo)
                for k, (lhsT, rhs) in enumerate(terms):
                    mm = pe.matmul(PN[:, lo:lo + n], lhsT, rhs[:, lo:lo + n], start=k == 0, stop=k == len(terms) - 1)
            mm.then_inc(node_step, 1)

        def row_linear(pe, name, xT, weight, bias):
            turn(pe, name)
            for i in range(TILES):
                out = PN[:, i * P:(i + 1) * P]
                mm = pe.matmul(out, xT[:, i * P:(i + 1) * P], weight, start=True, stop=bias is None)
                if bias is not None:
                    mm = pe.matmul(out, row("one"), bias, start=False, stop=True)
            mm.then_inc(node_step, 1)

        def rows_to_features(pe, name, R_):
            turn(pe, name)
            for i in range(TILES):
                mm = pe.transpose(PN[:, i * P:(i + 1) * P], R_[:, i, :], w("ident"))
            mm.then_inc(node_step, 1)

        def norm_tensor(pe, p, x, c, q):
            linear(pe, f"{p}.mean", [(w("avg"), x)])
            linear(pe, f"{p}.var", [(w("avg"), q)])

        def structure_tensor(pe):
            turn(pe, "s.before")
            pe.matmul(PM[0:GROUPS, 0:1], w("strict", 0, GROUPS, GROUPS), count_l[:, GE - 1:GE], start=True,
                      stop=True).then_inc(node_step, 1)
            turn(pe, "s.deg")

            def degree(c, s, first, last_):
                pe.wait_ge(deg_hot, c + 1)
                pe.matmul(PS[:, 0:TILES], lo_hot[:, s, :], hi_hot[:, s, :], start=first, stop=last_,
                          skip_group_check=True).then_inc(deg_mm, 1)

            degree(0, 0, True, False)
            degree(1, 1, False, False)
            with pe.Fori(1, CHUNKS // 2 - 1) as i:
                for s in range(2):
                    degree(2 * i + s, s, False, False)
            degree(CHUNKS - 2, 0, False, False)
            degree(CHUNKS - 1, 1, False, True)
            turn(pe, "s.within")
            pe.matmul(PS[:, BANK:BANK + TILES], w("upper"), deg[:, :], start=True, stop=True).then_inc(node_step, 1)
            pe.matmul(PS[:, 2 * BANK:2 * BANK + TILES], w("upper"), live[:, :], start=True, stop=True).then_inc(
                node_step, 1)
            turn(pe, "s.total")
            pe.matmul(PS[:, 3 * BANK:3 * BANK + TILES], w("ones"), deg[:, :], start=True, stop=True).then_inc(
                node_step, 1)
            pe.matmul(PS[:, 4 * BANK:4 * BANK + TILES], w("ones"), live[:, :], start=True, stop=True).then_inc(
                node_step, 1)

        def edges_tensor(pe, e):
            kind = KINDS[e]["kind"]
            turn(pe, f"{e}.edges")

            def expand(g, s, u, queries=False):
                if kind != "attn":
                    pe.wait_ge(SEM[e, "rows_here", s], 16 * CH * (u + 1))
                if past(g, 2) and kind != "attn":
                    if kind == "soft":
                        pe.wait_ge(SEM[e, "scored"], g - 1)
                    else:
                        pe.wait_ge(SEM[e, "num" if kind == "sum" else "pv"], g - 1)
                V = bank(V_BANK + s)
                if kind == "sum":
                    for j in range(CH):
                        mm = pe.transpose(V[:, j * P:(j + 1) * P], rows_in[:, s, j, 0:D], w("ident"))
                    mm.then_inc(SEM[e, "expanded"], 1)
                    return
                if kind == "soft":
                    pe.wait_ge(SEM[e, "attr_here", s], 16 * (u + 1))
                    for j in range(CH):
                        o = V[:, j * P:(j + 1) * P]
                        pe.matmul(o, rows_in[:, s, j, 0:D], w("ident"), start=True, stop=False, is_transpose=True)
                        mm = pe.matmul(o, ea[:, s, j * P:(j + 1) * P], w("ident"), start=False, stop=True)
                    mm.then_inc(SEM[e, "expanded"], 1)
                    return
                K = bank(K_BANK)
                if queries or kind == "gat":
                    pe.wait_ge(SEM[e, "edge_here", s], 16 * (u + 1) * CH)
                    pe.wait_ge(SEM[e, "one_hot"], g + 1)
                if queries:
                    if past(g, 1):
                        pe.wait_ge(SEM[e, "q_copied"], g)
                    for j in range(CH):
                        mm = pe.matmul(bank(Q_BANK)[:, j * P:(j + 1) * P], win[:, s, j, :],
                                       one_hot[:, s, j * P:(j + 1) * P], start=True, stop=True)
                    mm.then_inc(SEM[e, "q_ready"], 1)
                    return
                if kind == "attn":
                    pe.wait_ge(SEM[e, "rows_here", s], 16 * CH * (u + 1))
                    if past(g, 2):
                        pe.wait_ge(SEM[e, "pv"], g - 1)
                    pe.wait_ge(SEM[e, "attr_here", s], 16 * (u + 1))
                    if past(g, 1):
                        pe.wait_ge(SEM[e, "product"], g)
                    for out, at, done in ((K, 0, "k_ready"), (V, D, "expanded")):
                        for j in range(CH):
                            o = out[:, j * P:(j + 1) * P]
                            pe.matmul(o, rows_in[:, s, j, at:at + D], w("ident"), start=True, stop=False,
                                      is_transpose=True)
                            mm = pe.matmul(o, We[:, :], ea[0:EDGE_D, s, j * P:(j + 1) * P], start=False, stop=True)
                        mm.then_inc(SEM[e, done], 1)
                if kind == "gat":
                    if past(g, 1):
                        pe.wait_ge(SEM[e, "scored"], g)
                    for j in range(CH):
                        o = K[:, j * P:(j + 1) * P]
                        pe.matmul(o, rows_in[:, s, j, D:2 * D], w("ident"), start=True, stop=False,
                                  is_transpose=True)
                        mm = pe.matmul(o, win[:, s, j, :], one_hot[:, s, j * P:(j + 1) * P], start=False, stop=True)
                    mm.then_inc(SEM[e, "q_ready"], 1)
                    for j in range(CH):
                        mm = pe.transpose(V[:, j * P:(j + 1) * P], rows_in[:, s, j, 0:D], w("ident"))
                    mm.then_inc(SEM[e, "expanded"], 1)

            def heads(g, s, u):
                pe.wait_ge(SEM[e, "product"], g + 1)
                if past(g, 1):
                    pe.wait_ge(SEM[e, "x"], g)
                pe.matmul(bank(A_BANK), w("heads8"), prod[:, :], start=True, stop=True).then_inc(SEM[e, "scored"], 1)

            def turn_back(g, s, u):
                pe.wait_ge(SEM[e, "num"], g + 1)
                if kind != "sum":
                    pe.wait_ge(SEM[e, "den"], g + 1)
                if past(g, 1):
                    pe.wait_ge(SEM[e, "evac"], 2 * g if kind != "sum" else g)
                back = [num[:, s, :]] + ([den[:, s, :]] if kind != "sum" else [])
                if kind == "gat":
                    back += [U[:, s, 0:GE], score[:, s, :]]
                for k, x in enumerate(back):
                    for j in range(CH):
                        mm = pe.transpose(bank(OUT_BANK[kind] + k)[:, j * P:(j + 1) * P], x[:, j * P:(j + 1) * P],
                                          w("ident"))
                mm.then_inc(SEM[e, "turned"], 1)

            if kind == "attn":
                expand(0, 0, 0, queries=True)
            expand(0, 0, 0)

            def body(g, s, u):
                if kind == "attn":
                    if below(g, GROUPS - 1):
                        expand(g + 1, 1 - s, prev(u, s), queries=True)
                    heads(g, s, u)
                if below(g, GROUPS - 1):
                    expand(g + 1, 1 - s, prev(u, s))
                if past(g, 1):
                    turn_back(g - 1, 1 - s, prev(u, s) - 1)

            stream(pe, body)
            turn_back(GROUPS - 1, 1, PAIRS - 1)

        def norm_vector(dve, p, x, c, q, out):
            turn(dve, f"{p}.center")
            nc.vector.tensor_tensor(c[:, :], x[:, :], PN, ALU.subtract).then_inc(node_step, 1)
            turn(dve, f"{p}.inv")
            nc.vector.reciprocal(q[:, :], q[:, :]).then_inc(node_step, 1)
            turn(dve, f"{p}.scale")
            nc.vector.tensor_tensor(out[:, :], c[:, :], q[:, :], ALU.mult).then_inc(node_step, 1)

        def structure_vector(dve):
            def step(name):
                turn(dve, name)
                return nc.vector

            nc.vector.memset(eps[:, :], 1e-5)
            nc.vector.memset(one_l, 1.0)
            step("s.start").tensor_tensor(start_l, dst_line[1], dst_line[0], ALU.not_equal).then_inc(node_step, 1)
            step("s.keep").tensor_tensor(keep_l, dst_line[1], dst_line[0], ALU.is_equal).then_inc(node_step, 1)
            step("s.next").tensor_tensor(next_l, dst_line[1], dst_line[2], ALU.not_equal).then_inc(node_step, 1)
            step("s.reset").tensor_scalar(reset_l, next_l, LOW, None, ALU.mult).then_inc(node_step, 1)
            step("s.count").tensor_tensor_scan(count_l, one_l, start_l, 0.0, ALU.mult, ALU.add).then_inc(node_step, 1)
            step("s.rho").tensor_scalar(rho_l, count_l, PM[0:L, 0:1], -1.0, ALU.add, ALU.add).then_inc(node_step, 1)
            rho_c = rho_l.rearrange("p (c e) -> p c e", c=CH)
            step("s.first").tensor_copy(first_l, rho_c[:, :, 0]).then_inc(node_step, 1)
            step("s.rank").tensor_tensor(rank_l.rearrange("p (c e) -> p c e", c=CH), rho_c,
                                         rho_c[:, :, 0:1].to_broadcast([L, CH, P]), ALU.subtract).then_inc(
                node_step, 1)
            step("s.lo").tensor_scalar(lo_i, dst_col, P - 1, None, ALU.bitwise_and).then_inc(node_step, 1)
            step("s.hi").tensor_scalar(hi_i, dst_col, 7, None, ALU.logical_shift_right).then_inc(node_step, 1)
            step("s.lof").tensor_copy(lo_f, lo_i).then_inc(node_step, 1)
            step("s.hif").tensor_copy(hi_f, hi_i).then_inc(node_step, 1)
            turn(dve, "s.deg")

            def hot(c, s):
                if past(c, 2):
                    dve.wait_ge(deg_mm, c - 1)
                nc.vector.tensor_scalar(lo_hot[:, s, :], w("iota"), lo_f[:, bass.ds(c, 1)], None, ALU.is_equal)
                nc.vector.tensor_scalar(hi_hot[:, s, :], w("iota", 0, TILES), hi_f[:, bass.ds(c, 1)], None,
                                        ALU.is_equal).then_inc(deg_hot, 1)

            hot(0, 0)
            hot(1, 1)
            with dve.Fori(1, CHUNKS // 2) as i:
                for s in range(2):
                    hot(2 * i + s, s)
            dve.wait_ge(deg_mm, CHUNKS)
            step("s.deg_out").tensor_copy(deg[:, :], PS[:, 0:TILES]).then_inc(node_step, 1)
            step("s.live").tensor_scalar(live[:, :], deg[:, :], 0.0, None, ALU.is_gt).then_inc(node_step, 1)
            ones = w("ones", 0, TILES)
            step("s.total_out").tensor_copy(z[0][:, :], PS[:, 3 * BANK:3 * BANK + TILES]).then_inc(node_step, 1)
            step("s.run").tensor_tensor_scan(z[1][:, :], ones, z[0][:, :], 0.0, ALU.mult, ALU.add).then_inc(
                node_step, 1)
            step("s.end").tensor_tensor(z[2][:, :], z[1][:, :], z[0][:, :], ALU.subtract).then_inc(node_step, 1)
            step("s.end2").scalar_tensor_tensor(z[3][:, :], PS[:, BANK:BANK + TILES], -1.0, z[2][:, :], ALU.add,
                                                ALU.add).then_inc(node_step, 1)
            step("s.end3").tensor_scalar(last[:, :], z[3][:, :], 0.0, None, ALU.max).then_inc(node_step, 1)
            step("s.nrun").tensor_copy(z[4][:, :], PS[:, 4 * BANK:4 * BANK + TILES]).then_inc(node_step, 1)
            step("s.nlive").tensor_tensor_scan(z[5][:, :], ones, z[4][:, :], 0.0, ALU.mult, ALU.add).then_inc(
                node_step, 1)
            step("s.nlive2").tensor_tensor(z[6][:, :], z[5][:, :], z[4][:, :], ALU.subtract).then_inc(node_step, 1)
            step("s.nlive3").tensor_tensor(z[7][:, :], PS[:, 2 * BANK:2 * BANK + TILES], z[6][:, :],
                                           ALU.add).then_inc(node_step, 1)
            step("s.empty").tensor_tensor(z[6][:, :], z[7][:, :], live[:, :], ALU.subtract).then_inc(node_step, 1)
            step("s.empty2").scalar_tensor_tensor(z[7][:, :], w("node"), z[5][:, TILES - 1:TILES], z[6][:, :],
                                                  ALU.add, ALU.subtract).then_inc(node_step, 1)
            step("s.slot").tensor_tensor(z[6][:, :], z[6][:, :], z[7][:, :], ALU.subtract).then_inc(node_step, 1)
            step("s.slot2").tensor_tensor(z[6][:, :], z[6][:, :], live[:, :], ALU.mult).then_inc(node_step, 1)
            step("s.slot3").tensor_tensor(slot[:, :], z[6][:, :], z[7][:, :], ALU.add).then_inc(node_step, 1)

        def edges_vector(dve, e):
            kind = KINDS[e]["kind"]
            turn(dve, f"{e}.edges")

            def copy_idx(g, s, u):
                if past(g, 2):
                    dve.wait_ge(SEM[e, "rows_here", s], 16 * CH * u)
                nc.vector.tensor_copy(idx[:, s, :], src[:, bass.ds(g * CH, CH)]).then_inc(SEM[e, "idx_here"], 1)

            def sums(g, s, u):
                dve.wait_ge(SEM[e, "expanded"], g + 1)
                dve.wait_ge(SEM[e, "flag_here", s], 16 * (u + 1))
                if past(g, 1):
                    dve.wait_ge(SEM[e, "num"], g)
                if past(g, 2):
                    dve.wait_ge(SEM[e, "turned"], g - 1)
                init = num[:, 1 - s, GE - 1:GE] if past(g, 1) else 0.0
                nc.vector.tensor_tensor_scan(num[:, s, :], flag_b[:, s, :], bank(V_BANK + s), init, ALU.mult,
                                             ALU.add).then_inc(SEM[e, "num"], 1)

            def hot(g, s, u):
                dve.wait_ge(SEM[e, "rank_here", s], 16 * (u + 1))
                if past(g, 2):
                    dve.wait_ge(SEM[e, "q_ready"], g - 1)
                nc.vector.tensor_scalar(one_hot[:, s, :], rank_b[:, s, :], w("part"), None, ALU.is_equal).then_inc(
                    SEM[e, "one_hot"], 1)

            def product(g, s, u):
                dve.wait_ge(SEM[e, "q_copied"], g + 1)
                dve.wait_ge(SEM[e, "k_ready"], g + 1)
                if past(g, 1):
                    dve.wait_ge(SEM[e, "scored"], g)
                nc.vector.tensor_tensor(prod[:, :], bank(K_BANK), qx[:, :], ALU.mult).then_inc(SEM[e, "product"], 1)

            def messages(g, s, u):
                dve.wait_ge(SEM[e, "expanded"], g + 1)
                if past(g, 2):
                    dve.wait_ge(SEM[e, "x"], g - 1)
                    dve.wait_ge(SEM[e, "pv"], g - 1)
                nc.vector.tensor_scalar(score[:, s, :], bank(V_BANK + s), 0.0, 1e-7, ALU.max, ALU.add).then_inc(
                    SEM[e, "scored"], 1)

            def leaky(g, s, u):
                dve.wait_ge(SEM[e, "q_ready"], g + 1)
                if past(g, 2):
                    dve.wait_ge(SEM[e, "turned"], g - 1)
                dve.wait_ge(SEM[e, "q_copied"], g + 1)
                nc.vector.tensor_tensor(score[:, s, :], bank(K_BANK), qx[:, :], ALU.max).then_inc(
                    SEM[e, "scored"], 1)

            def running_max(g, s, u):
                dve.wait_ge(SEM[e, "scored"], g + 1)
                dve.wait_ge(SEM[e, "flag_here", s], 16 * (u + 1))
                a = bank(A_BANK) if kind == "attn" else score[:, s, :]
                if past(g, 1):
                    dve.wait_ge(SEM[e, "u"], g)
                    dve.wait_ge(SEM[e, "x"], g)
                if past(g, 2):
                    if kind == "gat":
                        dve.wait_ge(SEM[e, "turned"], g - 1)
                if past(g, 1):
                    nc.vector.tensor_copy(U[:, s, 0:1], U[:, 1 - s, GE:GE + 1]).then_inc(SEM[e, "u_head"], 1)
                else:
                    nc.vector.memset(U[:, s, 0:1], LOW).then_inc(SEM[e, "u_head"], 1)
                dve.wait_ge(SEM[e, "u_head"], g + 1)
                nc.vector.tensor_tensor_scan(U[:, s, 1:GE + 1], a, flag_b[:, s, :], U[:, s, 0:1], ALU.max,
                                             ALU.add).then_inc(SEM[e, "u"], 1)
                dve.wait_ge(SEM[e, "u"], g + 1)
                if past(g, 2):
                    dve.wait_ge(SEM[e, "clipped"], 2 * (g - 1))
                nc.vector.tensor_tensor(xd[:, s, :], U[:, s, 0:GE], a, ALU.subtract).then_inc(SEM[e, "x"], 1)

            def softmax_sums(g, s, u):
                dve.wait_ge(SEM[e, "weights"], 2 * g + 1)
                dve.wait_ge(SEM[e, "scored" if kind == "soft" else "expanded"], g + 1)
                if past(g, 1):
                    dve.wait_ge(SEM[e, "num"], g)
                value = score[:, s, :] if kind == "soft" else bank(V_BANK + s)
                nc.vector.tensor_tensor(pv[:, :], value, pw[:, s, :], ALU.mult).then_inc(SEM[e, "pv"], 1)
                dve.wait_ge(SEM[e, "weights"], 2 * g + 2)
                if past(g, 1):
                    dve.wait_ge(SEM[e, "den"], g)
                if past(g, 2):
                    dve.wait_ge(SEM[e, "turned"], g - 1)
                for out, x, n in ((den, pw[:, s, :], "den"), (num, pv[:, :], "num")):
                    init = out[:, 1 - s, GE - 1:GE] if past(g, 1) else 0.0
                    if n == "num":
                        dve.wait_ge(SEM[e, "pv"], g + 1)
                    nc.vector.tensor_tensor_scan(out[:, s, :], rw[:, s, :], x, init, ALU.mult, ALU.add).then_inc(
                        SEM[e, n], 1)

            copy_idx(0, 0, 0)
            copy_idx(1, 1, 0)
            if kind in ("attn", "gat"):
                hot(0, 0, 0)
                hot(1, 1, 0)

            def body(g, s, u):
                if below(g, GROUPS - 2):
                    copy_idx(g + 2, s, u + 1)
                if kind == "sum":
                    sums(g, s, u)
                    return
                if kind == "attn":
                    product(g, s, u)
                if kind == "soft":
                    messages(g, s, u)
                if kind == "gat":
                    leaky(g, s, u)
                if past(g, 1):
                    softmax_sums(g - 1, 1 - s, prev(u, s) - 1)
                if kind in ("attn", "gat") and below(g, GROUPS - 2):
                    hot(g + 2, s, u + 1)
                running_max(g, s, u)

            stream(dve, body)
            if kind != "sum":
                softmax_sums(GROUPS - 1, 1, PAIRS - 1)

        def edges_scalar(act, e):
            kind = KINDS[e]["kind"]
            k = KINDS[e]["out"]
            turn(act, f"{e}.edges")

            def copy_q(g, s, u):
                act.wait_ge(SEM[e, "q_ready"], g + 1)
                if past(g, 1):
                    act.wait_ge(SEM[e, "product" if kind == "attn" else "scored"], g)
                if kind == "attn":
                    nc.scalar.activation(qx[:, :], bank(Q_BANK), ACT.Copy).then_inc(SEM[e, "q_copied"], 1)
                else:
                    nc.scalar.activation(qx[:, :], bank(K_BANK), ACT.Copy, scale=0.2).then_inc(SEM[e, "q_copied"], 1)

            def weights(g, s, u):
                act.wait_ge(SEM[e, "x"], g + 1)
                if past(g, 2):
                    act.wait_ge(SEM[e, "num"], g - 1)
                    act.wait_ge(SEM[e, "den"], g - 1)
                for n, (out, sign) in enumerate(((pw, 1.0), (rw, -1.0))):
                    if past(g, 1):
                        act.wait_ge(SEM[e, "weights"], 2 * g)
                    nc.scalar.activation(clip[:, n, :], xd[:, s, :], ACT.Relu, scale=sign).then_inc(
                        SEM[e, "clipped"], 1)
                    act.wait_ge(SEM[e, "clipped"], 2 * g + n + 1)
                    nc.scalar.activation(out[:, s, :], clip[:, n, :], ACT.Exp, scale=-1.0).then_inc(
                        SEM[e, "weights"], 1)

            def store(g, s, u):
                act.wait_ge(SEM[e, "turned"], g + 1)
                if past(g, 2):
                    act.wait_ge(SEM[e, "stored", s], 16 * u)
                b = OUT_BANK[kind]
                nc.scalar.activation(rows_out[:, s, :, 0:D], bank(b).rearrange("p (c d) -> p c d", d=D),
                                     ACT.Copy).then_inc(SEM[e, "evac"], 1)
                n = 1 if kind == "sum" else 2
                if kind == "gat":
                    small = PS[:, (b + 1) * BANK:(b + 4) * BANK].rearrange("p (k c h x) -> p k c h x", k=3, c=CH,
                                                                           h=HEADS3)[:, :, :, :, 0]
                    to = rows_out[:, s, :, D:k].rearrange("p c (k h) -> p k c h", k=3)
                else:
                    h = HEADS1 if kind == "attn" else D
                    small = bank(b + 1).rearrange("p (c h x) -> p c h x", c=CH, h=h)[:, :, :, 0]
                    to = rows_out[:, s, :, D:k]
                if kind != "sum":
                    nc.scalar.activation(to, small, ACT.Copy).then_inc(SEM[e, "evac"], 1)
                act.wait_ge(SEM[e, "evac"], n * (g + 1))
                act.dma_start(out_d[e][bass.ds(g * GE, GE), :].rearrange("(c p) d -> p c d", p=P),
                              rows_out[:, s, :, 0:k]).then_inc(SEM[e, "stored", s], 16)

            def body(g, s, u):
                if past(g, 2):
                    store(g - 2, s, u - 1)
                if kind in ("attn", "gat") and below(g, GROUPS - 1):
                    copy_q(g + 1, 1 - s, prev(u, s))
                if kind != "sum":
                    weights(g, s, u)

            if kind in ("attn", "gat"):
                copy_q(0, 0, 0)
            stream(act, body)
            store(GROUPS - 2, 0, PAIRS - 1)
            store(GROUPS - 1, 1, PAIRS - 1)

        block = ctx.enter_context(nc.Block())

        @block.sync
        def _(sp):
            sp.dma_start(W[:, :], t["weights"]).then_inc(node_step, 16)
            sp.dma_start(rows[:, :], t["rows"]).then_inc(node_step, 16)
            sp.dma_start(X[:, :], t["xT"]).then_inc(node_step, 16)
            sp.dma_start(src[:, :], t["src"]).then_inc(node_step, 16)
            for n in range(3):
                sp.dma_start(dst_line[n], t["dst_line"][n:n + EP].rearrange("(g e) -> g e", e=GE)).then_inc(
                    node_step, 16)
            sp.dma_start(dst_col, t["dst_col"]).then_inc(node_step, 16)
            sp.dma_start(We[:, :], t["We"]).then_inc(node_step, 16)
            for e in ("e1", "e3", "e4"):
                sp.dma_start(window_d[e][NP:NP + P, :], t["zero"]).then_inc(node_step, 16)
            turn(sp, "s.save")
            sp.dma_start(rank_d.rearrange("(g e) -> g e", e=GE), rank_l[:, :]).then_inc(node_step, 16)
            sp.dma_start(reset_d.rearrange("(g e) -> g e", e=GE), reset_l[:, :]).then_inc(node_step, 16)
            sp.dma_start(keep_d.rearrange("(g e) -> g e", e=GE), keep_l[:, :]).then_inc(node_step, 16)
            sp.dma_start(first_d.rearrange("a (g c) -> (a g) c", c=CH), first_l[:, :]).then_inc(node_step, 16)
            turn(sp, "s.first_row")
            sp.dma_start(first_s[:, :], first_d).then_inc(node_step, 16)
            turn(sp, "s.deg_save")
            with nc.allow_non_contiguous_dma(reason="3200 degrees, once"):
                sp.dma_start(deg_d.rearrange("(t p) -> p t", p=P), deg[:, :]).then_inc(node_step, 16)
            turn(sp, "s.deg_row")
            sp.dma_start(C[0:1, :], deg_d.rearrange("(a n) -> a n", a=1)).then_inc(node_step, 16)
            edges_sync(sp, "e0")
            turn(sp, "kv_table")
            sp.dma_start(table_d["e1"].rearrange("(t p) d -> p t d", p=P), R[:, :, :]).then_inc(node_step, 16)
            edges_sync(sp, "e1")
            turn(sp, "x2_table")
            sp.dma_start(table_d["e2"].rearrange("(t p) d -> p t d", p=P), R[:, :, 0:D]).then_inc(node_step, 16)
            edges_sync(sp, "e2")
            for e in ("e3", "e4"):
                turn(sp, f"{e}.table")
                sp.dma_start(table_d[e].rearrange("(t p) d -> p t d", p=P), R[:, :, :]).then_inc(node_step, 16)
                edges_sync(sp, e)
            turn(sp, "y_save")
            sp.dma_start(t["out"].rearrange("(t p) d -> p t d", p=P), R[:, :, 0:D]).then_inc(node_step, 16)
            sp.wait_ge(node_step, ALL_STEPS)

        @block.gpsimd
        def _(pool):
            for e in KINDS:
                if e == "e1":
                    spread(pool, "e1", "q_spread")
                if e in ("e3", "e4"):
                    spread(pool, e, f"{e}.spread")
                turn(pool, f"{e}.edges")
                edges_gpsimd(pool, e)
                for s in range(2):
                    pool.wait_ge(SEM[e, "stored", s], 16 * PAIRS)
                turn(pool, f"{e}.ends")
                k = KINDS[e]["out"]
                for i in range(TILES):
                    pool.indirect_dma_start(R[:, i, 0:k], None, out_d[e], bass.IndirectOffsetOnAxis(
                        ap=last[:, i:i + 1], axis=0)).then_inc(moved, 16)
                moves_done(pool)

        @block.tensor
        def _(pe):
            structure_tensor(pe)
            edges_tensor(pe, "e0")
            rows_to_features(pe, "e0.turn", R[:, :, 0:D])
            linear(pe, "msg", [(w("w_msg"), A), (row("b_msg"), C[0:1, :])])
            linear(pe, "r", [(w("w_ih", 0, D), S1), (w("w_hh", 0, D), X)])
            linear(pe, "z", [(w("w_ih", D, D), S1), (w("w_hh", D, D), X)])
            linear(pe, "hn", [(w("w_hh", 2 * D, D), X)])
            linear(pe, "in", [(w("w_ih", 2 * D, D), S1)])
            norm_tensor(pe, "ln0", B, S1, C)
            norm_tensor(pe, "n0", A, S1, C)
            row_linear(pe, "k", X, w("wk"), row("bk"))
            row_linear(pe, "v", X, w("wv"), row("bv"))
            row_linear(pe, "q", X, w("wq"), row("bq"))
            edges_tensor(pe, "e1")
            rows_to_features(pe, "a.turn", R[:, :, 0:D])
            linear(pe, "skip", [(w("wskip"), X)])
            linear(pe, "a.gate", [(attm[:, 0, :], A), (attm[:, 1, :], B), (wb3[:, :], C)])
            for c in range(4):
                linear(pe, f"ffn{c}", [(w("ffn1", c * D, D), C)])
            linear(pe, "ffn", [(w("ffn2", c * D, D), G4[c]) for c in range(4)])
            norm_tensor(pe, "n1", A, S1, C)
            row_linear(pe, "x2", X, w("ident"), None)
            edges_tensor(pe, "e2")
            rows_to_features(pe, "c.turn", R[:, :, 0:D])
            linear(pe, "c.na", [(w("ones"), B)])
            linear(pe, "c.nx", [(w("ones"), C)])
            linear(pe, "c.mlp", [(w("mlp"), A)])
            norm_tensor(pe, "n2", A, S1, C)
            for e, stream_in, g, gs in (("e3", X, "g1", "g1s"), ("e4", B, "g2", "g2s")):
                linear(pe, f"{e}.hT", [(w(g), stream_in)])
                row_linear(pe, f"{e}.h", stream_in, w(g), None)
                row_linear(pe, f"{e}.as", A, attm[:, 0, :], None)
                row_linear(pe, f"{e}.ad", A, attm[:, 1, :], None)
                edges_tensor(pe, e)
                turn(pe, f"{e}.sum")
                for i in range(TILES):
                    o = PN[:, i * P:(i + 1) * P]
                    pe.matmul(o, w(gs), stream_in[:, i * P:(i + 1) * P], start=True, stop=False)
                    mm = pe.matmul(o, R[:, i, 0:D], w("ident"), start=False, stop=True)
                mm.then_inc(node_step, 1)
            norm_tensor(pe, "n3", A, S1, C)
            row_linear(pe, "y", X, w("ident"), None)

        @block.vector
        def _(dve):
            structure_vector(dve)
            edges_vector(dve, "e0")
            live_rows = live[:, :].rearrange("p (t o) -> p t o", o=1).to_broadcast([P, TILES, D])
            X_real = X[:, 0:NODES]

            def step(name):
                turn(dve, name)
                return nc.vector

            step("e0.mask").tensor_tensor(R[:, :, 0:D], R[:, :, 0:D], live_rows, ALU.mult).then_inc(node_step, 1)
            step("mean").tensor_reduce(col[:, 0:1], X_real, AX, ALU.add).then_inc(node_step, 1)
            step("mean2").tensor_scalar(col[:, 1:2], col[:, 0:1], 1.0 / NODES, None, ALU.mult).then_inc(node_step, 1)
            step("msg_mean").tensor_scalar(S1[:, :], A[:, :], col[:, 1:2], None, ALU.add).then_inc(node_step, 1)
            step("gb").tensor_tensor(col[:, 2:4], w("b_ih", 0, 2), w("b_hh", 0, 2), ALU.add).then_inc(node_step, 1)
            step("hn_out").scalar_tensor_tensor(B[:, :], PN, w("b_hh", 2, 1), B[:, :], ALU.add, ALU.mult).then_inc(
                node_step, 1)
            step("in_out").tensor_tensor(B[:, :], PN, B[:, :], ALU.add).then_inc(node_step, 1)
            step("h1").tensor_tensor(S1[:, :], X[:, :], B[:, :], ALU.subtract).then_inc(node_step, 1)
            step("h2").tensor_tensor(S1[:, :], S1[:, :], C[:, :], ALU.mult).then_inc(node_step, 1)
            step("h3").tensor_tensor(B[:, :], S1[:, :], B[:, :], ALU.add).then_inc(node_step, 1)
            norm_vector(dve, "ln0", B, S1, C, B)
            step("y0a").tensor_scalar(B[:, :], B[:, :], w("gamma0"), w("beta0"), ALU.mult, ALU.add).then_inc(
                node_step, 1)
            step("y0b").tensor_tensor(A[:, :], A[:, :], B[:, :], ALU.add).then_inc(node_step, 1)
            step("y0c").tensor_tensor(A[:, :], A[:, :], X[:, :], ALU.add).then_inc(node_step, 1)
            norm_vector(dve, "n0", A, S1, C, X)

            edges_vector(dve, "e1")
            dn = R[:, :, D:D + HEADS1]
            step("a.den").tensor_scalar(s8[:, 0, :, :], dn, 1e-16, None, ALU.add).then_inc(node_step, 1)
            step("a.rden").reciprocal(s8[:, 1, :, :], s8[:, 0, :, :]).then_inc(node_step, 1)
            live8 = live[:, :].rearrange("p (t o) -> p t o", o=1).to_broadcast([P, TILES, HEADS1])
            step("a.live").tensor_tensor(s8[:, 0, :, :], s8[:, 1, :, :], live8, ALU.mult).then_inc(node_step, 1)
            turn(dve, "a.norm")
            for h in range(HEADS1):
                c = D // HEADS1
                mul = s8[:, 0, :, h:h + 1].to_broadcast([P, TILES, c])
                x = R[:, :, h * c:(h + 1) * c]
                op = nc.vector.tensor_tensor(x, x, mul, ALU.mult)
            op.then_inc(node_step, 1)
            step("a.diff").tensor_tensor(C[:, :], A[:, :], B[:, :], ALU.subtract).then_inc(node_step, 1)
            turn(dve, "a.wb")
            nc.vector.tensor_scalar(attm[:, 0, :], w("ones"), w("beta", 0, 1), None, ALU.mult).then_inc(node_step, 1)
            nc.vector.tensor_scalar(attm[:, 1, :], w("ones"), w("beta", 1, 1), None, ALU.mult).then_inc(node_step, 1)
            nc.vector.tensor_scalar(wb3[:, :], w("ones"), w("beta", 2, 1), None, ALU.mult).then_inc(node_step, 1)
            step("a.mix").tensor_tensor(C[:, :], C[:, :], S1[:, :], ALU.mult).then_inc(node_step, 1)
            step("a.att").tensor_tensor(A[:, :], A[:, :], C[:, :], ALU.subtract).then_inc(node_step, 1)
            step("a.h").tensor_tensor(A[:, :], A[:, :], X[:, :], ALU.add).then_inc(node_step, 1)
            step("gn.sum").tensor_reduce(col[:, 0:1], A[:, 0:NODES], AX, ALU.add).then_inc(node_step, 1)
            step("gn.mean").tensor_scalar(col[:, 1:2], col[:, 0:1], 1.0 / NODES, w("gn_ms"), ALU.mult,
                                          ALU.mult).then_inc(node_step, 1)
            step("gn.center").tensor_scalar(S1[:, :], A[:, :], col[:, 1:2], None, ALU.subtract).then_inc(node_step, 1)
            step("gn.var").tensor_reduce(col[:, 2:3], B[:, 0:NODES], AX, ALU.add).then_inc(node_step, 1)
            step("gn.inv").reciprocal(col[:, 4:5], col[:, 3:4]).then_inc(node_step, 1)
            step("gn.gain").tensor_tensor(col[:, 5:6], col[:, 4:5], w("gn_w"), ALU.mult).then_inc(node_step, 1)
            step("gn.out").tensor_scalar(C[:, :], S1[:, :], col[:, 5:6], w("gn_b"), ALU.mult, ALU.add).then_inc(
                node_step, 1)
            step("ffn_out").scalar_tensor_tensor(A[:, :], PN, w("fb2"), C[:, :], ALU.add, ALU.add).then_inc(
                node_step, 1)
            step("y1").tensor_tensor(A[:, :], A[:, :], X[:, :], ALU.add).then_inc(node_step, 1)
            norm_vector(dve, "n1", A, S1, C, X)

            edges_vector(dve, "e2")
            step("c.rden").reciprocal(R[:, :, D:2 * D], R[:, :, D:2 * D]).then_inc(node_step, 1)
            step("c.norm").tensor_tensor(R[:, :, 0:D], R[:, :, 0:D], R[:, :, D:2 * D], ALU.mult).then_inc(
                node_step, 1)
            step("c.mask").tensor_tensor(R[:, :, 0:D], R[:, :, 0:D], live_rows, ALU.mult).then_inc(node_step, 1)
            step("c.maxa").tensor_scalar(B[:, :], PN, 1e-24, None, ALU.max).then_inc(node_step, 1)
            step("c.inva").reciprocal(S1[:, :], B[:, :]).then_inc(node_step, 1)
            step("c.maxx").tensor_scalar(B[:, :], PN, 1e-30, None, ALU.max).then_inc(node_step, 1)
            step("c.unit").tensor_tensor(A[:, :], A[:, :], S1[:, :], ALU.mult).then_inc(node_step, 1)
            step("c.scaled").tensor_tensor(A[:, :], A[:, :], C[:, :], ALU.mult).then_inc(node_step, 1)
            step("c.feat").tensor_tensor(A[:, :], A[:, :], X[:, :], ALU.add).then_inc(node_step, 1)
            step("c.mlp_out").tensor_scalar(A[:, :], PN, w("mlp_b"), None, ALU.add).then_inc(node_step, 1)
            step("y2").tensor_tensor(A[:, :], A[:, :], X[:, :], ALU.add).then_inc(node_step, 1)
            norm_vector(dve, "n2", A, S1, C, X)

            H2 = HEADS3
            small = [s8[:, k, :, 0:H2] for k in range(8)]
            live2 = live[:, :].rearrange("p (t o) -> p t o", o=1).to_broadcast([P, TILES, H2])
            hrow = S1[:, :].rearrange("p (t d) -> p t d", d=D)
            adrow = C[:, :].rearrange("p (t d) -> p t d", d=D)
            for e, n, gb, gsb in (("e3", "1", "g1b", "g1sb"), ("e4", "2", "g2b", "g2sb")):
                turn(dve, f"{e}.att")
                nc.vector.tensor_scalar(attm[:, 0, :], w("heads2"), w(f"att_s{n}"), None, ALU.mult).then_inc(
                    node_step, 1)
                nc.vector.tensor_scalar(attm[:, 1, :], w("heads2"), w(f"att_d{n}"), None, ALU.mult).then_inc(
                    node_step, 1)
                step(f"{e}.self_z").tensor_tensor(small[0], R[:, :, D::D // H2], adrow[:, :, 0::D // H2],
                                                  ALU.add).then_inc(node_step, 1)
                step(f"{e}.self").scalar_tensor_tensor(small[1], small[0], 0.2, small[0], ALU.mult,
                                                       ALU.max).then_inc(node_step, 1)
                edges_vector(dve, e)
                dn, un, sn = (R[:, :, D + k * H2:D + (k + 1) * H2] for k in range(3))
                step(f"{e}.m").tensor_tensor(small[2], un, sn, ALU.max).then_inc(node_step, 1)
                step(f"{e}.m_live").tensor_tensor(small[3], small[2], live2, ALU.mult).then_inc(node_step, 1)
                step(f"{e}.m_mask").tensor_scalar(small[4], live2, 1.0, -LOW, ALU.subtract, ALU.mult).then_inc(
                    node_step, 1)
                step(f"{e}.m_all").tensor_tensor(small[2], small[3], small[4], ALU.add).then_inc(node_step, 1)
                step(f"{e}.we_x").tensor_tensor(small[3], small[2], small[1], ALU.max).then_inc(node_step, 1)
                turn(dve, f"{e}.ws_x")
                nc.vector.tensor_tensor(small[4], small[2], small[3], ALU.subtract)
                nc.vector.tensor_tensor(small[5], small[1], small[3], ALU.subtract).then_inc(node_step, 1)
                step(f"{e}.we_live").tensor_tensor(small[3], small[6], live2, ALU.mult).then_inc(node_step, 1)
                step(f"{e}.den").tensor_tensor(small[4], dn, small[3], ALU.mult).then_inc(node_step, 1)
                step(f"{e}.den2").tensor_tensor(small[5], small[4], small[7], ALU.add).then_inc(node_step, 1)
                step(f"{e}.den3").tensor_scalar(small[4], small[5], 1e-16, None, ALU.add).then_inc(node_step, 1)
                step(f"{e}.rden").reciprocal(small[5], small[4]).then_inc(node_step, 1)
                step(f"{e}.we_n").tensor_tensor(small[4], small[3], small[5], ALU.mult).then_inc(node_step, 1)
                step(f"{e}.ws_n").tensor_tensor(small[6], small[7], small[5], ALU.mult).then_inc(node_step, 1)
                for name, rows_, k in (("num", R[:, :, 0:D], 4), ("hs", hrow, 6)):
                    turn(dve, f"{e}.{name}")
                    for h in range(H2):
                        c = D // H2
                        mul = s8[:, k, :, h:h + 1].to_broadcast([P, TILES, c])
                        x = rows_[:, :, h * c:(h + 1) * c]
                        op = nc.vector.tensor_tensor(x, x, mul, ALU.mult)
                    op.then_inc(node_step, 1)
                step(f"{e}.agg").tensor_tensor(R[:, :, 0:D], R[:, :, 0:D], hrow, ALU.add).then_inc(node_step, 1)
                step(f"{e}.bias").tensor_tensor(col[:, 0:1], w(gb), w(gsb), ALU.add).then_inc(node_step, 1)
                if e == "e3":
                    step(f"{e}.act").tensor_scalar(B[:, :], PN, col[:, 0:1], 0.0, ALU.add, ALU.max).then_inc(
                        node_step, 1)
                else:
                    step(f"{e}.act").scalar_tensor_tensor(A[:, :], PN, col[:, 0:1], X[:, :], ALU.add,
                                                          ALU.add).then_inc(node_step, 1)
            norm_vector(dve, "n3", A, S1, C, X)

        @block.scalar
        def _(act):
            edges_scalar(act, "e0")

            def step(name):
                turn(act, name)
                return nc.scalar

            def out_of_psum(name, out, func=ACT.Copy, **k):
                step(name).activation(out, PN, func, **k).then_inc(node_step, 1)

            def table(name, at):
                step(name).activation(R[:, :, at:at + D], PN.rearrange("p (t d) -> p t d", d=D), ACT.Copy).then_inc(
                    node_step, 1)

            def norm_scalar(p, c, q):
                step(f"{p}.square").activation(q[:, :], c[:, :], ACT.Square).then_inc(node_step, 1)
                step(f"{p}.std").activation(q[:, :], PN, ACT.Sqrt, bias=eps[:, 0:1]).then_inc(node_step, 1)

            out_of_psum("e0.turned", A[:, :])
            out_of_psum("msg_out", A[:, :])
            out_of_psum("r_out", B[:, :], ACT.Sigmoid, bias=col[:, 2:3])
            out_of_psum("z_out", C[:, :], ACT.Sigmoid, bias=col[:, 3:4])
            step("n").activation(B[:, :], B[:, :], ACT.Tanh, bias=w("b_ih", 2, 1)).then_inc(node_step, 1)
            norm_scalar("ln0", S1, C)
            norm_scalar("n0", S1, C)
            table("k_out", 0)
            table("v_out", D)
            out_of_psum("q_out", C[:, :])
            edges_scalar(act, "e1")
            out_of_psum("a.turned", A[:, :])
            out_of_psum("skip_out", B[:, :], ACT.Identity, bias=w("bskip"))
            out_of_psum("a.gate_out", S1[:, :], ACT.Sigmoid)
            step("gn.sq").activation(B[:, :], S1[:, :], ACT.Square).then_inc(node_step, 1)
            step("gn.std").activation(col[:, 3:4], col[:, 2:3], ACT.Sqrt, bias=eps[:, 0:1],
                                      scale=1.0 / NODES).then_inc(node_step, 1)
            for c in range(4):
                out_of_psum(f"ffn{c}_out", G4[c][:, :], ACT.Gelu, bias=w("fb1", c, 1))
            norm_scalar("n1", S1, C)
            table("x2_out", 0)
            edges_scalar(act, "e2")
            out_of_psum("c.turned", A[:, :])
            step("c.sqa").activation(B[:, :], A[:, :], ACT.Square).then_inc(node_step, 1)
            step("c.roota").activation(B[:, :], B[:, :], ACT.Sqrt).then_inc(node_step, 1)
            step("c.sqx").activation(C[:, :], X[:, :], ACT.Square).then_inc(node_step, 1)
            step("c.rootx").activation(C[:, :], B[:, :], ACT.Sqrt).then_inc(node_step, 1)
            norm_scalar("n2", S1, C)
            for e in ("e3", "e4"):
                out_of_psum(f"{e}.hT_out", A[:, :])
                out_of_psum(f"{e}.h_out", S1[:, :])
                nc.scalar.activation(R[:, :, 0:D], PN.rearrange("p (t d) -> p t d", d=D), ACT.Copy).then_inc(
                    node_step, 1)
                table(f"{e}.as_out", D)
                out_of_psum(f"{e}.ad_out", C[:, :])
                edges_scalar(act, e)
                step(f"{e}.we").activation(s8[:, 6, :, 0:HEADS3], s8[:, 4, :, 0:HEADS3], ACT.Exp).then_inc(
                    node_step, 1)
                step(f"{e}.ws").activation(s8[:, 7, :, 0:HEADS3], s8[:, 5, :, 0:HEADS3], ACT.Exp).then_inc(
                    node_step, 1)
            norm_scalar("n3", S1, C)
            step("y_out").activation(R[:, :, 0:D], PN.rearrange("p (t d) -> p t d", d=D), ACT.Copy).then_inc(
                node_step, 1)


def host_arrays(a):
    f = np.float32

    def padded(x, n):
        return np.concatenate([x, np.zeros((n - x.shape[0],) + x.shape[1:], x.dtype)])

    def fill(n, value):
        return np.full(n, value, np.int32)

    x = padded(a["x"], NP)
    dst = np.concatenate([a["dst"], fill(EP - EDGES, NP - 1)])
    k = np.arange(P)

    def same(heads):
        return (k[:, None] * heads // D == k[None, :] * heads // D).astype(f)

    def pick(heads):
        return (k[:, None] == np.arange(heads)[None, :] * (D // heads)).astype(f)

    parts = {
        "w_msg": a["L0_gnn_W_msg"].T, "w_ih": a["L0_gnn_w_ih"].T, "w_hh": a["L0_gnn_w_hh"].T,
        "wq": a["L1_gnn_Wq"], "wk": a["L1_gnn_Wk"], "wv": a["L1_gnn_Wv"], "wskip": a["L1_gnn_Wskip"],
        "ffn1": a["L1_gnn_W1"], "ffn2": a["L1_gnn_W2"].reshape(4, D, D).transpose(1, 0, 2).reshape(D, 4 * D),
        "mlp": a["L2_gnn_mlp_w"],
        "g1": a["L3_gnn_W1"], "g1s": a["L3_gnn_Wsk1"], "g2": a["L3_gnn_W2"], "g2s": a["L3_gnn_Wsk2"],
        "ident": np.eye(P, dtype=f), "ones": np.ones((P, P), f), "avg": np.full((P, P), 1.0 / D, f),
        "upper": np.triu(np.ones((P, P), f)), "strict": np.triu(np.ones((P, P), f), 1),
        "heads8": same(HEADS1) * f((D // HEADS1) ** -0.5), "heads2": same(HEADS3),
        "pick8": pick(HEADS1), "pick2": pick(HEADS3),
        "iota": np.tile(k.astype(f), (P, 1)), "part": k.astype(f)[:, None],
        "node": (np.arange(TILES)[None, :] * P + k[:, None]).astype(f),
        "beta": a["L1_gnn_Wbeta"].reshape(3, D).T,
        "b_ih": a["L0_gnn_b_ih"].reshape(3, D).T, "b_hh": a["L0_gnn_b_hh"].reshape(3, D).T,
        "fb1": a["L1_gnn_b1"].reshape(4, D).T,
    }
    for name, key in (("gamma0", "L0_gnn_ln_gamma"), ("beta0", "L0_gnn_ln_beta"), ("bskip", "L1_gnn_bskip"),
                      ("gn_w", "L1_gnn_gn_w"), ("gn_b", "L1_gnn_gn_b"), ("gn_ms", "L1_gnn_gn_ms"),
                      ("fb2", "L1_gnn_b2"), ("mlp_b", "L2_gnn_mlp_b"),
                      ("att_s1", "L3_gnn_att_src1"), ("att_d1", "L3_gnn_att_dst1"), ("g1b", "L3_gnn_b1"),
                      ("g1sb", "L3_gnn_bsk1"), ("att_s2", "L3_gnn_att_src2"), ("att_d2", "L3_gnn_att_dst2"),
                      ("g2b", "L3_gnn_b2"), ("g2sb", "L3_gnn_bsk2")):
        parts[name] = a[key].reshape(D, 1)
    lines = {"b_msg": a["L0_gnn_b_msg"], "bq": a["L1_gnn_bq"], "bk": a["L1_gnn_bk"], "bv": a["L1_gnn_bv"],
             "one": np.ones(P, f)}
    return {
        "weights": np.concatenate([parts[n] for n, _ in WEIGHTS], axis=1),
        "rows": np.concatenate([lines[n] for n, _ in ROWS])[None, :],
        "x": x, "xT": np.ascontiguousarray(x.T),
        "src": np.ascontiguousarray(np.concatenate([a["src"], fill(EP - EDGES, 0)]).reshape(CHUNKS, P).T).view(
            np.uint32),
        "dst_line": np.concatenate([fill(1, -1), dst, fill(1, NP)]),
        "dst_col": np.ascontiguousarray(dst.reshape(CHUNKS, P).T),
        "We": a["L1_gnn_We"],
        "zero": np.zeros((P, D), f),
        "ea10": np.ascontiguousarray(padded(a["edge_attr_10"], EP).T),
        "ea128": padded(a["edge_attr_128"], EP),
    }


def kernel(**inputs):
    import concourse.bacc as bacc
    from concourse.bass_utils import run_bass_kernel_spmd

    arrays = host_arrays({k: np.asarray(v) for k, v in inputs.items()})
    nc = bacc.Bacc("TRN2", target_bir_lowering=False, num_devices=1)
    t = {k: nc.dram_tensor(f"in_{k}", v.shape, mybir.dt.from_np(v.dtype), kind="ExternalInput").ap()
         for k, v in arrays.items()}
    t["out"] = nc.dram_tensor("out", [NP, D], F32, kind="ExternalOutput").ap()
    gnn(nc, t)
    r = run_bass_kernel_spmd(nc, [{f"in_{k}": v for k, v in arrays.items()}], core_ids=[0])
    return r.results[0]["out"][:NODES]
```

```python
from contextlib import ExitStack

import numpy as np

import concourse.bass as bass
from concourse import mybir

F32 = mybir.dt.float32
BF16 = mybir.dt.bfloat16
I32 = mybir.dt.int32
U32 = mybir.dt.uint32
ALU = mybir.AluOpType
ACT = mybir.ActivationFunctionType
AX = mybir.AxisListType.X

NODES, EDGES, D, EDGE_D = 3125, 50000, 128, 10
P = 128
TILES = -(-NODES // P)
NP = TILES * P
GE = 512
CH = GE // P
GROUPS = -(-EDGES // GE)
EP = GROUPS * GE
CHUNKS = EP // P
PAIRS = GROUPS // 2
LOW = -3.0e38
BANK = 512

HEADS1, HEADS3 = 8, 2
KINDS = {
    "e0": dict(kind="sum", row=D, out=D),
    "e1": dict(kind="attn", row=2 * D, out=D + HEADS1),
    "e2": dict(kind="soft", row=D, out=2 * D),
    "e3": dict(kind="gat", row=2 * D, out=D + 3 * HEADS3),
    "e4": dict(kind="gat", row=2 * D, out=D + 3 * HEADS3),
}

WEIGHTS = [("w_msg", 128), ("w_ih", 384), ("w_hh", 384), ("wq", 128), ("wk", 128), ("wv", 128), ("wskip", 128),
           ("ffn1", 512), ("ffn2", 512), ("mlp", 128), ("g1", 128), ("g1s", 128), ("g1T", 128), ("g2", 128), ("g2s", 128), ("g2T", 128),
           ("ident", 128), ("ones", 128), ("avg", 128), ("upper", 128), ("strict", 128),
           ("heads8", 128), ("head2", HEADS3), ("iota", 128), ("part", 1),
           ("node", TILES), ("beta", 3),
           ("b_ih", 3), ("b_hh", 3), ("b_msg", 1), ("gamma0", 1), ("beta0", 1), ("bq", 1), ("bskip", 1), ("gn_w", 1), ("gn_b", 1),
           ("gn_ms", 1), ("fb1", 4), ("fb2", 1), ("mlp_b", 1),
           ("att_s1", 1), ("att_d1", 1), ("g1b", 1), ("g1sb", 1),
           ("att_s2", 1), ("att_d2", 1), ("g2b", 1), ("g2sb", 1)]


def columns(spec):
    at, out = 0, {}
    for name, n in spec:
        out[name] = (at, n)
        at += n
    return out, at


WCOL, WIDTH = columns(WEIGHTS)

PARTS = [(lo, min(lo + BANK // P, TILES)) for lo in range(0, TILES, BANK // P)]
WHOLE = "whole"


def norm_steps(p):
    return [f"{p}.mean", f"{p}.center", f"{p}.square", f"{p}.var", f"{p}.inv", f"{p}.scale"]


def gat_steps(p):
    return [f"{p}.terms", (f"{p}.terms_out", 1, WHOLE), f"{p}.ad_row", (f"{p}.spread", 0, None), f"{p}.as_row", f"{p}.h", f"{p}.h_row",
            (f"{p}.table", 0, None), f"{p}.h_out",
            (f"{p}.self_z", 1, WHOLE), (f"{p}.self", 1, WHOLE), (f"{p}.edges", 0, WHOLE), f"{p}.ends",
            (f"{p}.m", 1, WHOLE), (f"{p}.m_live", 1, WHOLE), (f"{p}.m_mask", 1, WHOLE), (f"{p}.m_all", 1, WHOLE),
            (f"{p}.we_x", 1, WHOLE), (f"{p}.ws_x", 1, WHOLE), (f"{p}.we", 1, WHOLE), (f"{p}.ws", 1, WHOLE),
            (f"{p}.we_live", 1, WHOLE), (f"{p}.den", 1, WHOLE), (f"{p}.den2", 1, WHOLE), (f"{p}.den3", 1, WHOLE),
            (f"{p}.rden", 1, WHOLE), (f"{p}.we_n", 1, WHOLE), (f"{p}.ws_n", 1, WHOLE),
            f"{p}.num", f"{p}.hs", f"{p}.agg", f"{p}.sum", f"{p}.act"]


STEPS = (
    [(n, k, WHOLE) for n, k in (
        ("s.start", 1), ("s.keep", 1), ("s.next", 1), ("s.reset", 1), ("s.count", 1), ("s.before", 1), ("s.rho", 1),
        ("s.first", 1), ("s.rank", 1), ("s.save", 16 * 4), ("s.first_row", 16),
        ("s.lo", 1), ("s.hi", 1), ("s.lof", 1), ("s.hif", 1), ("mean", 1), ("mean2", 1), ("gb", 1), ("a.wb", 4),
        ("g.att", 4), ("g.comp", 1), ("g.comp_out", 1), ("g.bias", 2), ("e0.edges", 0),
        ("s.deg_out", 1), ("s.live", 1),
        ("s.within", 2), ("s.total", 2), ("s.total_out", 1), ("s.run", 1), ("s.end", 1), ("s.end2", 1), ("s.end3", 1),
        ("s.nrun", 1), ("s.nlive", 1), ("s.nlive2", 1), ("s.nlive3", 1), ("s.empty", 1), ("s.empty2", 1),
        ("s.slot", 1), ("s.slot2", 1), ("s.slot3", 1))]
    + ["e0.ends", "e0.mask", "e0.turn", "e0.turned", "msg", "msg_out", "msg_mean", "r", "r_out", "z", "z_out",
       "hn", "hn_out", "in", "in_out", "n", "h1", "h2", "h3"]
    + norm_steps("ln0") + ["y0a", "y0b", "y0c"] + norm_steps("n0")
    + ["q", "q_row", ("q_spread", 0, None), "k", "k_row", "v", "v_row", ("kv_table", 0, None), ("e1.edges", 0, WHOLE), "e1.ends",
       "a.den", "a.rden", "a.live", "a.norm", "a.turn", "a.turned", "skip", "skip_out", "a.gate", "a.gate_out", "a.diff",
       "a.mix", "a.att", "a.h", "gn.sum", ("gn.all", 1, WHOLE), ("gn.mean", 1, WHOLE), "gn.center", "gn.sq",
       "gn.sqsum", ("gn.var", 1, WHOLE), ("gn.std", 1, WHOLE), ("gn.inv", 1, WHOLE), ("gn.gain", 1, WHOLE), "gn.out"]
    + [f"ffn{c}{o}" for c in range(4) for o in ("", "_out")]
    + ["ffn", "ffn_out", "y1"] + norm_steps("n1")
    + ["x2", "x2_row", ("x2_table", 0, None), ("e2.edges", 0, WHOLE), "e2.ends",
       "c.den2", "c.rden", "c.norm", "c.mask", "c.turn", "c.turned", "c.sqa", "c.na", "c.maxa", "c.inva",
       "c.sqx", "c.nx", "c.rootx", "c.unit", "c.scaled", "c.feat", "c.mlp", "y2"] + norm_steps("n2")
    + gat_steps("e3") + gat_steps("e4") + norm_steps("n3") + ["y", "y_row", ("y_save", 0, None)]
)
LOADS = {"src": 16, "dst": 16 * 4, "weights": 16 * 7}
PART_BEFORE, WHOLE_BEFORE = {}, {}
_part = _whole = 0
for _s in STEPS:
    _name, _n, _kind = (_s, 1, None) if isinstance(_s, str) else _s
    assert _name not in PART_BEFORE, _name
    PART_BEFORE[_name], WHOLE_BEFORE[_name] = _part, _whole
    if _kind == WHOLE:
        _whole += _n
    else:
        _part += _n


def gnn(nc, t):
    with ExitStack() as ctx:
        def sb(name, shape, dt=F32):
            return ctx.enter_context(nc.sbuf_tensor(name, shape, dt))

        def sem(name):
            return ctx.enter_context(nc.semaphore(name))

        def dram(name, shape, dt=F32):
            return nc.dram_tensor(name, shape, dt, kind="Internal").ap()

        rank_d = dram("rank_d", [EP], BF16)
        reset_d = dram("reset_d", [EP], BF16)
        keep_d = dram("keep_d", [EP], BF16)
        first_d = dram("first_d", [1, CHUNKS], I32)
        deg_d = dram("deg_d", [NP])
        window_d = {e: dram(f"{e}_window", [NP + P, D]) for e in ("e1", "e3", "e4")}
        table_d = {"e0": t["x"]}
        for e in ("e1", "e2", "e3", "e4"):
            table_d[e] = dram(f"{e}_table", [NP, KINDS[e]["row"]])
        out_d = {e: dram(f"{e}_out", [EP, KINDS[e]["out"]]) for e in KINDS}

        W = sb("W", [P, WIDTH])

        def w(name, lo=0, n=None, p=P):
            a, k = WCOL[name]
            return W[0:p, a + lo:a + (k if n is None else lo + n)]

        src = sb("src", [P, CHUNKS], U32)
        live = sb("live", [P, TILES])
        slot = sb("slot", [P, TILES], U32)
        last = sb("last", [P, TILES], U32)
        X = sb("X", [P, NP])
        A = sb("A", [P, NP])
        B = sb("B", [P, NP])
        C = sb("C", [P, NP])
        S1 = sb("S1", [P, NP])
        R = sb("R", [P, TILES, 2 * D])
        R2 = R[:, :, :].rearrange("p t d -> p (t d)")
        G4 = [A, B, R2[:, 0:NP], R2[:, NP:2 * NP]]
        s8 = sb("s8", [P, 8, TILES, HEADS1])
        eps = sb("eps", [P, 1])
        col = sb("col", [P, 16])
        part_sum = sb("part_sum", [P, 2, len(PARTS)])
        gate_w = sb("gate_w", [P, 2, P])
        beta_sum = sb("beta_sum", [P, 2])
        att = sb("att", [P, 2, 2 * HEADS3])
        comp = sb("comp", [P, 2, 2 * HEADS3])
        terms = sb("terms", [P, TILES, 2 * HEADS3])
        gat_bias = sb("gat_bias", [P, 2])

        MAXROW = 2 * D
        rows_in = sb("rows_in", [P, 2, CH, MAXROW])
        idx = sb("idx", [P, 2, CH], U32)
        rank_b = sb("rank_b", [P, 2, GE], BF16)
        flag_b = sb("flag_b", [P, 2, GE], BF16)
        ea = sb("ea", [P, 2, GE])
        win = sb("win", [P, 2, CH, D])
        one_hot = sb("one_hot", [P, 2, GE])
        qx = sb("qx", [P, GE])
        prod = sb("prod", [P, GE])
        score = sb("score", [P, 2, GE])
        U = sb("U", [P, 2, GE + 1])
        xd = sb("xd", [P, 2, GE])
        clip = sb("clip", [P, 2, GE])
        pw = sb("pw", [P, 2, GE])
        rw = sb("rw", [P, 2, GE])
        pv = sb("pv", [P, GE])
        den = sb("den", [P, 2, GE])
        num = sb("num", [P, 2, GE])
        rows_out = sb("rows_out", [P, 2, CH, MAXROW])

        PS = ctx.enter_context(nc.psum_tensor("PS", [P, 8 * BANK], F32))
        PN = PS[:, 0:NP]
        PM = PS[:, 7 * BANK:8 * BANK]

        def bank(b, n=BANK):
            return PS[:, b * BANK:b * BANK + n]

        V_BANK, K_BANK, Q_BANK, A_BANK = 0, 2, 3, 4
        OUT_BANK = {"sum": 5, "attn": 5, "soft": 5, "gat": 3}

        loaded = {n: sem(f"loaded_{n}") for n in ("src", "dst", "weights")}
        part_done = [sem(f"part_done{b}") for b in range(len(PARTS))]
        whole_done = sem("whole_done")
        moved = [sem(f"moved{b}") for b in range(len(PARTS))]
        moves = [0]
        table_saved = sem("table_saved")
        degrees_here = sem("degrees_here")
        out_saved = sem("out_saved")
        TABLES = len(PARTS) * 16

        gate_pool = sem("gate_pool")
        gate_sp = sem("gate_sp")
        deg_hot = sem("deg_hot")
        deg_mm = sem("deg_mm")
        SEM = {}
        SOFTMAX = ["scored", "u", "u_head", "x", "clipped", "weights", "pv", "den"]
        QUERY = ["q_ready", "one_hot", "q_copied"]
        USED = {"sum": [], "attn": ["k_ready", "product"] + QUERY + SOFTMAX, "soft": SOFTMAX,
                "gat": QUERY + SOFTMAX}
        HERE = {"sum": [], "attn": ["rank_here", "edge_here", "attr_here"], "soft": ["attr_here"],
                "gat": ["rank_here", "edge_here"]}
        for e in KINDS:
            kind = KINDS[e]["kind"]
            for n in ["idx_here", "expanded", "num", "turned", "evac"] + USED[kind]:
                SEM[e, n] = sem(f"{e}_{n}")
            for n in ["rows_here", "flag_here", "stored"] + HERE[kind]:
                for s in range(2):
                    SEM[e, n, s] = sem(f"{e}_{n}{s}")

        def turn(eng, name, b=None):
            if WHOLE_BEFORE[name]:
                eng.wait_ge(whole_done, WHOLE_BEFORE[name])
            if PART_BEFORE[name]:
                for s in part_done if b is None else part_done[b:b + 1]:
                    eng.wait_ge(s, PART_BEFORE[name])

        def turns(eng, name):
            for b, (lo, hi) in enumerate(PARTS):
                turn(eng, name, b)
                yield b, slice(lo * P, hi * P), slice(lo, hi)

        def past(g, n):
            return not isinstance(g, int) or g >= n

        def below(g, n):
            return not isinstance(g, int) or g < n

        def stream(eng, body):
            for g in range(4):
                body(g, g % 2, g // 2)
            with eng.Fori(2, PAIRS - 1) as i:
                for s in range(2):
                    body(2 * i + s, s, i)
            for g in (GROUPS - 2, GROUPS - 1):
                body(g, g % 2, g // 2)

        def prev(u, s):
            return u if s == 0 else u + 1

        L = GROUPS
        dst_i = A[0:L, 0:3 * GE].bitcast(I32).rearrange("p (n e) -> p n e", n=3)
        dst_line = [dst_i[:, n, :] for n in range(3)]
        start_l = B[0:L, 0:GE]
        count_l = B[0:L, GE:2 * GE]
        rho_l = B[0:L, 2 * GE:3 * GE]
        next_l = B[0:L, 3 * GE:4 * GE]
        one_l = B[0:L, 4 * GE:5 * GE]
        rank_l = one_hot[0:L, 0, 0:GE // 2].bitcast(BF16)
        reset_l = one_hot[0:L, 0, GE // 2:GE].bitcast(BF16)
        keep_l = one_hot[0:L, 1, 0:GE // 2].bitcast(BF16)
        first_l = one_hot[0:L, 1, GE // 2:GE // 2 + CH].bitcast(I32)
        dst_col = S1[:, 0:CHUNKS].bitcast(I32)
        lo_i = S1[:, CHUNKS:2 * CHUNKS].bitcast(I32)
        hi_i = S1[:, 2 * CHUNKS:3 * CHUNKS].bitcast(I32)
        lo_f = S1[:, 3 * CHUNKS:4 * CHUNKS]
        hi_f = S1[:, 4 * CHUNKS:5 * CHUNKS]
        lo_hot = [pw[:, s, 0:CH * P // 2].bitcast(BF16).rearrange("p (c n) -> p c n", c=CH) for s in range(2)]
        hi_hot = [rw[:, s, 0:CH * 16].bitcast(BF16).rearrange("p (c n) -> p c n", c=CH)[:, :, 0:TILES]
                  for s in range(2)]
        DEG_BANK = 7
        deg = sb("deg", [P, TILES])
        first_s = sb("first_s", [1, CHUNKS], I32)
        z = [sb(f"z{k}", [P, TILES]) for k in range(8)]
        We_k = sb("We_k", [EDGE_D + 1, D])
        We_v = sb("We_v", [EDGE_D + 1, D])
        C_rows = C[:, :].rearrange("p (t d) -> p t d", d=D)


        def edges_sync(sp, e):
            kind = KINDS[e]["kind"]
            if kind == "sum":
                turn(sp, "s.first_row")
            if kind in ("attn", "gat"):
                for b, (lo, hi) in enumerate(PARTS):
                    sp.wait_ge(moved[b], 16 * (hi - lo) * (2, 5, 7)[("e1", "e3", "e4").index(e)])
            turn(sp, f"{e}.edges" if kind != "sum" else "s.first_row")
            flag = keep_d if kind == "sum" else reset_d

            def load_flag(g, s, u):
                if past(g, 2):
                    sp.wait_ge(SEM[e, "num" if kind == "sum" else "u"], g - 1)
                sp.sem_inc(gate_sp, 1)
                sp.dma_start(flag_b[:, s, :], flag[bass.ds(g * GE, GE)].partition_broadcast(P)).then_inc(
                    SEM[e, "flag_here", s], 16)

            def body(g, s, u):
                if kind in ("attn", "gat"):
                    if past(g, 2):
                        sp.wait_ge(SEM[e, "one_hot"], g - 1)
                    sp.dma_start(rank_b[:, s, :], rank_d[bass.ds(g * GE, GE)].partition_broadcast(P)).then_inc(
                        SEM[e, "rank_here", s], 16)
                    if past(g, 2):
                        sp.wait_ge(SEM[e, "q_ready"], g - 1)
                    sp.sem_inc(gate_sp, 1)
                    _, firsts = nc.values_load_multi_w_load_instructions(
                        first_s[0:1, bass.ds(g * CH, CH)], engines=[mybir.EngineType.SP], min_val=0, max_val=NP - 1)
                    for j in range(CH):
                        sp.dma_start(win[:, s, j, :], window_d[e][bass.ds(firsts[j], P), :]).then_inc(
                            SEM[e, "edge_here", s], 16)
                if kind in ("attn", "soft"):
                    if past(g, 2):
                        sp.wait_ge(SEM[e, "expanded"], g - 1)
                    sp.sem_inc(gate_sp, 1)
                if kind == "attn":
                    sp.dma_start(ea[0:EDGE_D + 1, s, :], t["ea11"][:, bass.ds(g * GE, GE)]).then_inc(
                        SEM[e, "attr_here", s], 16)
                if kind == "soft":
                    sp.dma_start(ea[:, s, :].rearrange("p (c d) -> p c d", c=CH),
                                 t["ea128"][bass.ds(g * GE, GE), :].rearrange("(c p) d -> p c d", p=P)).then_inc(
                        SEM[e, "attr_here", s], 16)
                if past(g, 1):
                    load_flag(g - 1, 1 - s, prev(u, s) - 1)

            stream(sp, body)
            load_flag(GROUPS - 1, 1, PAIRS - 1)

        def spread(pool, e, name):
            for b, c, tiles in turns(pool, name):
                for i in range(tiles.start, tiles.stop):
                    pool.indirect_dma_start(window_d[e], bass.IndirectOffsetOnAxis(ap=slot[:, i:i + 1], axis=0),
                                            C_rows[:, i, :], None).then_inc(moved[b], 16)
            moves[0] += 1

        def gather_ends(pool, e):
            for s in range(2):
                pool.wait_ge(SEM[e, "stored", s], 16 * PAIRS)
            k = KINDS[e]["out"]
            for b, c, tiles in turns(pool, f"{e}.ends"):
                for i in range(tiles.start, tiles.stop):
                    pool.indirect_dma_start(R[:, i, 0:k], None, out_d[e], bass.IndirectOffsetOnAxis(
                        ap=last[:, i:i + 1], axis=0)).then_inc(moved[b], 16)
            moves[0] += 1
            for b, (lo, hi) in enumerate(PARTS):
                pool.wait_ge(moved[b], 16 * (hi - lo) * moves[0])
                pool.sem_inc(part_done[b], 1)

        def edges_gpsimd(pool, e):
            k = KINDS[e]["row"]

            def body(g, s, u):
                if past(g, 2):
                    pool.wait_ge(SEM[e, "expanded"], g - 1)
                pool.wait_ge(SEM[e, "idx_here"], g + 1)
                pool.sem_inc(gate_pool, 1)
                for j in range(CH):
                    pool.indirect_dma_start(rows_in[:, s, j, 0:k], None, table_d[e], bass.IndirectOffsetOnAxis(
                        ap=idx[:, s, j:j + 1], axis=0)).then_inc(SEM[e, "rows_here", s], 16)

            stream(pool, body)

        def linear(pe, name, terms_):
            for b, c, tiles in turns(pe, name):
                for k, (lhsT, rhs) in enumerate(terms_):
                    mm = pe.matmul(PN[:, c], lhsT, rhs[:, c], start=k == 0, stop=k == len(terms_) - 1)
                mm.then_inc(part_done[b], 1)

        def row_linear(pe, name, xT, weight):
            for b, c, tiles in turns(pe, name):
                for i in range(tiles.start, tiles.stop):
                    mm = pe.matmul(PN[:, i * P:(i + 1) * P], xT[:, i * P:(i + 1) * P], weight, start=True, stop=True)
                mm.then_inc(part_done[b], 1)

        def rows_to_features(pe, name, R_):
            for b, c, tiles in turns(pe, name):
                for i in range(tiles.start, tiles.stop):
                    mm = pe.transpose(PN[:, i * P:(i + 1) * P], R_[:, i, :], w("ident"))
                mm.then_inc(part_done[b], 1)

        def features_to_rows(pe, name, x):
            rows_to_features(pe, name, x[:, :].rearrange("p (t d) -> p t d", d=P))

        def norm_tensor(pe, p, x, c, q):
            linear(pe, f"{p}.mean", [(w("avg"), x)])
            linear(pe, f"{p}.var", [(w("avg"), q)])

        def structure_tensor(pe):
            pe.wait_ge(loaded["weights"], LOADS["weights"])
            turn(pe, "s.before")
            pe.matmul(PM[0:GROUPS, 0:1], w("strict", 0, GROUPS, GROUPS), count_l[:, GE - 1:GE], start=True,
                      stop=True).then_inc(whole_done, 1)
            turn(pe, "g.comp")
            for n, g in enumerate(("g1T", "g2T")):
                mm = pe.matmul(PM[:, n * 2 * HEADS3:(n + 1) * 2 * HEADS3], w(g), att[:, n, :], start=True, stop=True)
            mm.then_inc(whole_done, 1)

        def counts_tensor(pe):
            turn(pe, "s.within")
            pe.matmul(PS[:, BANK:BANK + TILES], w("upper"), deg[:, :], start=True, stop=True).then_inc(whole_done, 1)
            pe.matmul(PS[:, 2 * BANK:2 * BANK + TILES], w("upper"), live[:, :], start=True, stop=True).then_inc(
                whole_done, 1)
            turn(pe, "s.total")
            pe.matmul(PS[:, 3 * BANK:3 * BANK + TILES], w("ones"), deg[:, :], start=True, stop=True).then_inc(
                whole_done, 1)
            pe.matmul(PS[:, 4 * BANK:4 * BANK + TILES], w("ones"), live[:, :], start=True, stop=True).then_inc(
                whole_done, 1)

        def edges_tensor(pe, e):
            kind = KINDS[e]["kind"]
            turn(pe, f"{e}.edges")

            def expand(g, s, u, queries=False):
                if kind != "attn":
                    pe.wait_ge(SEM[e, "rows_here", s], 16 * CH * (u + 1))
                if past(g, 2) and kind != "attn":
                    if kind == "soft":
                        pe.wait_ge(SEM[e, "scored"], g - 1)
                    else:
                        pe.wait_ge(SEM[e, "num" if kind == "sum" else "pv"], g - 1)
                V = bank(V_BANK + s)
                if kind == "sum":
                    for j in range(CH):
                        mm = pe.transpose(V[:, j * P:(j + 1) * P], rows_in[:, s, j, 0:D], w("ident"))
                    mm.then_inc(SEM[e, "expanded"], 1)
                    return
                if kind == "soft":
                    pe.wait_ge(SEM[e, "attr_here", s], 16 * (u + 1))
                    for j in range(CH):
                        o = V[:, j * P:(j + 1) * P]
                        pe.matmul(o, rows_in[:, s, j, 0:D], w("ident"), start=True, stop=False, is_transpose=True)
                        mm = pe.matmul(o, ea[:, s, j * P:(j + 1) * P], w("ident"), start=False, stop=True)
                    mm.then_inc(SEM[e, "expanded"], 1)
                    return
                K = bank(K_BANK)
                if queries or kind == "gat":
                    pe.wait_ge(SEM[e, "edge_here", s], 16 * (u + 1) * CH)
                    pe.wait_ge(SEM[e, "one_hot"], g + 1)
                if queries:
                    if past(g, 1):
                        pe.wait_ge(SEM[e, "q_copied"], g)
                    for j in range(CH):
                        mm = pe.matmul(bank(Q_BANK)[:, j * P:(j + 1) * P], win[:, s, j, :],
                                       one_hot[:, s, j * P:(j + 1) * P], start=True, stop=True)
                    mm.then_inc(SEM[e, "q_ready"], 1)
                    return
                if kind == "attn":
                    pe.wait_ge(SEM[e, "rows_here", s], 16 * CH * (u + 1))
                    if past(g, 2):
                        pe.wait_ge(SEM[e, "pv"], g - 1)
                    pe.wait_ge(SEM[e, "attr_here", s], 16 * (u + 1))
                    if past(g, 1):
                        pe.wait_ge(SEM[e, "product"], g)
                    for out, at, We, done in ((K, 0, We_k, "k_ready"), (V, D, We_v, "expanded")):
                        for j in range(CH):
                            o = out[:, j * P:(j + 1) * P]
                            pe.matmul(o, rows_in[:, s, j, at:at + D], w("ident"), start=True, stop=False,
                                      is_transpose=True)
                            mm = pe.matmul(o, We[:, :], ea[0:EDGE_D + 1, s, j * P:(j + 1) * P], start=False, stop=True)
                        mm.then_inc(SEM[e, done], 1)
                if kind == "gat":
                    if past(g, 1):
                        pe.wait_ge(SEM[e, "scored"], g)
                    for j in range(CH):
                        o = K[:, j * P:(j + 1) * P]
                        pe.matmul(o, rows_in[:, s, j, D:2 * D], w("ident"), start=True, stop=False,
                                  is_transpose=True)
                        mm = pe.matmul(o, win[:, s, j, :], one_hot[:, s, j * P:(j + 1) * P], start=False, stop=True)
                    mm.then_inc(SEM[e, "q_ready"], 1)
                    for j in range(CH):
                        mm = pe.transpose(V[:, j * P:(j + 1) * P], rows_in[:, s, j, 0:D], w("ident"))
                    mm.then_inc(SEM[e, "expanded"], 1)

            def heads(g, s, u):
                pe.wait_ge(SEM[e, "product"], g + 1)
                if past(g, 1):
                    pe.wait_ge(SEM[e, "x"], g)
                pe.matmul(bank(A_BANK), w("heads8"), prod[:, :], start=True, stop=True).then_inc(SEM[e, "scored"], 1)

            def turn_back(g, s, u):
                pe.wait_ge(SEM[e, "num"], g + 1)
                if kind != "sum":
                    pe.wait_ge(SEM[e, "den"], g + 1)
                if past(g, 1):
                    pe.wait_ge(SEM[e, "evac"], 2 * g if kind != "sum" else g)
                back = [num[:, s, :]] + ([den[:, s, :]] if kind != "sum" else [])
                if kind == "gat":
                    back += [U[:, s, 0:GE], score[:, s, :]]
                for k, x in enumerate(back):
                    for j in range(CH):
                        mm = pe.transpose(bank(OUT_BANK[kind] + k)[:, j * P:(j + 1) * P], x[:, j * P:(j + 1) * P],
                                          w("ident"))
                mm.then_inc(SEM[e, "turned"], 1)

            if kind == "attn":
                expand(0, 0, 0, queries=True)
            expand(0, 0, 0)

            def body(g, s, u):
                if kind == "attn":
                    if below(g, GROUPS - 1):
                        expand(g + 1, 1 - s, prev(u, s), queries=True)
                    heads(g, s, u)
                if below(g, GROUPS - 1):
                    expand(g + 1, 1 - s, prev(u, s))
                if past(g, 1):
                    turn_back(g - 1, 1 - s, prev(u, s) - 1)
                if kind == "sum":
                    pe.wait_ge(deg_hot, g + 1)
                    for j in range(CH):
                        mm = pe.matmul(bank(DEG_BANK, TILES), lo_hot[s][:, j, :], hi_hot[s][:, j, :],
                                       start=not past(g, 1) and j == 0,
                                       stop=isinstance(g, int) and g == GROUPS - 1 and j == CH - 1,
                                       skip_group_check=True)
                    mm.then_inc(deg_mm, 1)

            stream(pe, body)
            turn_back(GROUPS - 1, 1, PAIRS - 1)

        def norm_vector(dve, p, x, c, q, out):
            for b, n, _ in turns(dve, f"{p}.center"):
                nc.vector.tensor_tensor(c[:, n], x[:, n], PN[:, n], ALU.subtract).then_inc(part_done[b], 1)
            for b, n, _ in turns(dve, f"{p}.scale"):
                nc.vector.tensor_tensor(out[:, n], c[:, n], q[:, n], ALU.mult).then_inc(part_done[b], 1)

        def structure_vector(dve):
            def step(name):
                turn(dve, name)
                return nc.vector

            nc.vector.memset(eps[:, :], 1e-5)
            nc.vector.memset(one_l, 1.0)
            dve.wait_ge(loaded["src"], LOADS["src"])
            for s in range(2):
                nc.vector.tensor_copy(idx[:, s, :], src[:, s * CH:(s + 1) * CH]).then_inc(SEM["e0", "idx_here"], 1)
            dve.wait_ge(loaded["dst"], LOADS["dst"])
            step("s.start").tensor_tensor(start_l, dst_line[1], dst_line[0], ALU.not_equal).then_inc(whole_done, 1)
            step("s.keep").tensor_tensor(keep_l, dst_line[1], dst_line[0], ALU.is_equal).then_inc(whole_done, 1)
            step("s.next").tensor_tensor(next_l, dst_line[1], dst_line[2], ALU.not_equal).then_inc(whole_done, 1)
            step("s.reset").tensor_scalar(reset_l, next_l, LOW, None, ALU.mult).then_inc(whole_done, 1)
            step("s.count").tensor_tensor_scan(count_l, one_l, start_l, 0.0, ALU.mult, ALU.add).then_inc(
                whole_done, 1)
            step("s.rho").tensor_scalar(rho_l, count_l, PM[0:L, 0:1], -1.0, ALU.add, ALU.add).then_inc(whole_done, 1)
            rho_c = rho_l.rearrange("p (c e) -> p c e", c=CH)
            step("s.first").tensor_copy(first_l, rho_c[:, :, 0]).then_inc(whole_done, 1)
            step("s.rank").tensor_tensor(rank_l.rearrange("p (c e) -> p c e", c=CH), rho_c,
                                         rho_c[:, :, 0:1].to_broadcast([L, CH, P]), ALU.subtract).then_inc(
                whole_done, 1)
            step("s.lo").tensor_scalar(lo_i, dst_col, P - 1, None, ALU.bitwise_and).then_inc(whole_done, 1)
            step("s.hi").tensor_scalar(hi_i, dst_col, 7, None, ALU.logical_shift_right).then_inc(whole_done, 1)
            step("s.lof").tensor_copy(lo_f, lo_i).then_inc(whole_done, 1)
            step("s.hif").tensor_copy(hi_f, hi_i).then_inc(whole_done, 1)
            step("mean").tensor_reduce(col[:, 0:1], X[:, 0:NODES], AX, ALU.add).then_inc(whole_done, 1)
            step("mean2").tensor_scalar(col[:, 1:2], col[:, 0:1], 1.0 / NODES, None, ALU.mult).then_inc(
                whole_done, 1)
            step("gb").tensor_tensor(col[:, 2:4], w("b_ih", 0, 2), w("b_hh", 0, 2), ALU.add).then_inc(whole_done, 1)
            turn(dve, "a.wb")
            nc.vector.tensor_tensor(beta_sum[:, 0:1], w("beta", 0, 1), w("beta", 2, 1), ALU.add).then_inc(
                whole_done, 1)
            nc.vector.tensor_tensor(beta_sum[:, 1:2], w("beta", 1, 1), w("beta", 2, 1), ALU.subtract).then_inc(
                whole_done, 1)
            dve.wait_ge(whole_done, WHOLE_BEFORE["a.wb"] + 2)
            for n in range(2):
                nc.vector.tensor_scalar(gate_w[:, n, :], w("ones"), beta_sum[:, n:n + 1], None, ALU.mult).then_inc(
                    whole_done, 1)
            turn(dve, "g.att")
            for n in range(2):
                for k, a in enumerate((f"att_s{n + 1}", f"att_d{n + 1}")):
                    nc.vector.tensor_scalar(att[:, n, k * HEADS3:(k + 1) * HEADS3], w("head2"), w(a), None,
                                            ALU.mult).then_inc(whole_done, 1)
            step("g.comp_out").tensor_copy(comp[:, :, :], PM[:, 0:4 * HEADS3].rearrange(
                "p (n k) -> p n k", n=2)).then_inc(whole_done, 1)
            turn(dve, "g.bias")
            for n in range(2):
                nc.vector.tensor_tensor(gat_bias[:, n:n + 1], w(f"g{n + 1}b"), w(f"g{n + 1}sb"), ALU.add).then_inc(
                    whole_done, 1)

        def counts_vector(dve):
            def step(name):
                turn(dve, name)
                return nc.vector

            dve.wait_ge(deg_mm, GROUPS)
            step("s.deg_out").tensor_copy(deg[:, :], bank(DEG_BANK, TILES)).then_inc(whole_done, 1)
            step("s.live").tensor_scalar(live[:, :], deg[:, :], 0.0, None, ALU.is_gt).then_inc(whole_done, 1)
            ones = w("ones", 0, TILES)
            step("s.total_out").tensor_copy(z[0][:, :], PS[:, 3 * BANK:3 * BANK + TILES]).then_inc(whole_done, 1)
            step("s.run").tensor_tensor_scan(z[1][:, :], ones, z[0][:, :], 0.0, ALU.mult, ALU.add).then_inc(
                whole_done, 1)
            step("s.end").tensor_tensor(z[2][:, :], z[1][:, :], z[0][:, :], ALU.subtract).then_inc(whole_done, 1)
            step("s.end2").scalar_tensor_tensor(z[3][:, :], PS[:, BANK:BANK + TILES], -1.0, z[2][:, :], ALU.add,
                                                ALU.add).then_inc(whole_done, 1)
            step("s.end3").tensor_scalar(last[:, :], z[3][:, :], 0.0, None, ALU.max).then_inc(whole_done, 1)
            step("s.nrun").tensor_copy(z[4][:, :], PS[:, 4 * BANK:4 * BANK + TILES]).then_inc(whole_done, 1)
            step("s.nlive").tensor_tensor_scan(z[5][:, :], ones, z[4][:, :], 0.0, ALU.mult, ALU.add).then_inc(
                whole_done, 1)
            step("s.nlive2").tensor_tensor(z[6][:, :], z[5][:, :], z[4][:, :], ALU.subtract).then_inc(whole_done, 1)
            step("s.nlive3").tensor_tensor(z[7][:, :], PS[:, 2 * BANK:2 * BANK + TILES], z[6][:, :],
                                           ALU.add).then_inc(whole_done, 1)
            step("s.empty").tensor_tensor(z[6][:, :], z[7][:, :], live[:, :], ALU.subtract).then_inc(whole_done, 1)
            step("s.empty2").scalar_tensor_tensor(z[7][:, :], w("node"), z[5][:, TILES - 1:TILES], z[6][:, :],
                                                  ALU.add, ALU.subtract).then_inc(whole_done, 1)
            step("s.slot").tensor_tensor(z[6][:, :], z[6][:, :], z[7][:, :], ALU.subtract).then_inc(whole_done, 1)
            step("s.slot2").tensor_tensor(z[6][:, :], z[6][:, :], live[:, :], ALU.mult).then_inc(whole_done, 1)
            step("s.slot3").tensor_tensor(slot[:, :], z[6][:, :], z[7][:, :], ALU.add).then_inc(whole_done, 1)

        def edges_vector(dve, e):
            kind = KINDS[e]["kind"]
            turn(dve, f"{e}.edges")

            def copy_idx(g, s, u):
                if past(g, 2):
                    dve.wait_ge(SEM[e, "rows_here", s], 16 * CH * u)
                nc.vector.tensor_copy(idx[:, s, :], src[:, bass.ds(g * CH, CH)]).then_inc(SEM[e, "idx_here"], 1)

            def sums(g, s, u):
                dve.wait_ge(SEM[e, "expanded"], g + 1)
                dve.wait_ge(SEM[e, "flag_here", s], 16 * (u + 1))
                if past(g, 1):
                    dve.wait_ge(SEM[e, "num"], g)
                if past(g, 2):
                    dve.wait_ge(SEM[e, "turned"], g - 1)
                init = num[:, 1 - s, GE - 1:GE] if past(g, 1) else 0.0
                nc.vector.tensor_tensor_scan(num[:, s, :], flag_b[:, s, :], bank(V_BANK + s), init, ALU.mult,
                                             ALU.add).then_inc(SEM[e, "num"], 1)

            def hot(g, s, u):
                dve.wait_ge(SEM[e, "rank_here", s], 16 * (u + 1))
                if past(g, 2):
                    dve.wait_ge(SEM[e, "q_ready"], g - 1)
                nc.vector.tensor_scalar(one_hot[:, s, :], rank_b[:, s, :], w("part"), None, ALU.is_equal).then_inc(
                    SEM[e, "one_hot"], 1)

            def product(g, s, u):
                dve.wait_ge(SEM[e, "q_copied"], g + 1)
                dve.wait_ge(SEM[e, "k_ready"], g + 1)
                if past(g, 1):
                    dve.wait_ge(SEM[e, "scored"], g)
                nc.vector.tensor_tensor(prod[:, :], bank(K_BANK), qx[:, :], ALU.mult).then_inc(SEM[e, "product"], 1)

            def messages(g, s, u):
                dve.wait_ge(SEM[e, "expanded"], g + 1)
                if past(g, 2):
                    dve.wait_ge(SEM[e, "x"], g - 1)
                    dve.wait_ge(SEM[e, "pv"], g - 1)
                nc.vector.tensor_scalar(score[:, s, :], bank(V_BANK + s), 0.0, 1e-7, ALU.max, ALU.add).then_inc(
                    SEM[e, "scored"], 1)

            def leaky(g, s, u):
                dve.wait_ge(SEM[e, "q_ready"], g + 1)
                if past(g, 2):
                    dve.wait_ge(SEM[e, "turned"], g - 1)
                dve.wait_ge(SEM[e, "q_copied"], g + 1)
                nc.vector.tensor_tensor(score[:, s, :], bank(K_BANK), qx[:, :], ALU.max).then_inc(
                    SEM[e, "scored"], 1)

            def running_max(g, s, u):
                dve.wait_ge(SEM[e, "scored"], g + 1)
                dve.wait_ge(SEM[e, "flag_here", s], 16 * (u + 1))
                a = bank(A_BANK) if kind == "attn" else score[:, s, :]
                if past(g, 1):
                    dve.wait_ge(SEM[e, "u"], g)
                    dve.wait_ge(SEM[e, "x"], g)
                if past(g, 2):
                    if kind == "gat":
                        dve.wait_ge(SEM[e, "turned"], g - 1)
                if past(g, 1):
                    nc.vector.tensor_copy(U[:, s, 0:1], U[:, 1 - s, GE:GE + 1]).then_inc(SEM[e, "u_head"], 1)
                else:
                    nc.vector.memset(U[:, s, 0:1], LOW).then_inc(SEM[e, "u_head"], 1)
                dve.wait_ge(SEM[e, "u_head"], g + 1)
                nc.vector.tensor_tensor_scan(U[:, s, 1:GE + 1], a, flag_b[:, s, :], U[:, s, 0:1], ALU.max,
                                             ALU.add).then_inc(SEM[e, "u"], 1)
                dve.wait_ge(SEM[e, "u"], g + 1)
                if past(g, 2):
                    dve.wait_ge(SEM[e, "clipped"], 2 * (g - 1))
                nc.vector.tensor_tensor(xd[:, s, :], U[:, s, 0:GE], a, ALU.subtract).then_inc(SEM[e, "x"], 1)

            def softmax_sums(g, s, u):
                dve.wait_ge(SEM[e, "weights"], 2 * g + 1)
                dve.wait_ge(SEM[e, "scored" if kind == "soft" else "expanded"], g + 1)
                if past(g, 1):
                    dve.wait_ge(SEM[e, "num"], g)
                value = score[:, s, :] if kind == "soft" else bank(V_BANK + s)
                nc.vector.tensor_tensor(pv[:, :], value, pw[:, s, :], ALU.mult).then_inc(SEM[e, "pv"], 1)
                dve.wait_ge(SEM[e, "weights"], 2 * g + 2)
                if past(g, 1):
                    dve.wait_ge(SEM[e, "den"], g)
                if past(g, 2):
                    dve.wait_ge(SEM[e, "turned"], g - 1)
                for out, x, n in ((den, pw[:, s, :], "den"), (num, pv[:, :], "num")):
                    init = out[:, 1 - s, GE - 1:GE] if past(g, 1) else 0.0
                    if n == "num":
                        dve.wait_ge(SEM[e, "pv"], g + 1)
                    nc.vector.tensor_tensor_scan(out[:, s, :], rw[:, s, :], x, init, ALU.mult, ALU.add).then_inc(
                        SEM[e, n], 1)

            def degrees(g, s):
                if past(g, 2):
                    dve.wait_ge(deg_mm, g - 1)
                for hot_, n, x in ((lo_hot, P, lo_f), (hi_hot, TILES, hi_f)):
                    op = nc.vector.tensor_tensor(
                        hot_[s], w("iota", 0, n).rearrange("p (o n) -> p o n", o=1).to_broadcast([P, CH, n]),
                        x[:, bass.ds(g * CH, CH)].rearrange("p (c o) -> p c o", o=1).to_broadcast([P, CH, n]),
                        ALU.is_equal)
                op.then_inc(deg_hot, 1)

            if kind != "sum":
                copy_idx(0, 0, 0)
                copy_idx(1, 1, 0)
            if kind in ("attn", "gat"):
                hot(0, 0, 0)
                hot(1, 1, 0)

            def body(g, s, u):
                if below(g, GROUPS - 2):
                    copy_idx(g + 2, s, u + 1)
                if kind == "sum":
                    sums(g, s, u)
                    degrees(g, s)
                    return
                if kind == "attn":
                    product(g, s, u)
                if kind == "soft":
                    messages(g, s, u)
                if kind == "gat":
                    leaky(g, s, u)
                if past(g, 1):
                    softmax_sums(g - 1, 1 - s, prev(u, s) - 1)
                if kind in ("attn", "gat") and below(g, GROUPS - 2):
                    hot(g + 2, s, u + 1)
                running_max(g, s, u)

            stream(dve, body)
            if kind != "sum":
                softmax_sums(GROUPS - 1, 1, PAIRS - 1)

        def edges_scalar(act, e):
            kind = KINDS[e]["kind"]
            k = KINDS[e]["out"]
            turn(act, f"{e}.edges")

            def copy_q(g, s, u):
                act.wait_ge(SEM[e, "q_ready"], g + 1)
                if past(g, 1):
                    act.wait_ge(SEM[e, "product" if kind == "attn" else "scored"], g)
                if kind == "attn":
                    nc.scalar.activation(qx[:, :], bank(Q_BANK), ACT.Identity, bias=w("bq")).then_inc(SEM[e, "q_copied"], 1)
                else:
                    nc.scalar.activation(qx[:, :], bank(K_BANK), ACT.Copy, scale=0.2).then_inc(SEM[e, "q_copied"], 1)

            def weights(g, s, u):
                act.wait_ge(SEM[e, "x"], g + 1)
                if past(g, 2):
                    act.wait_ge(SEM[e, "num"], g - 1)
                    act.wait_ge(SEM[e, "den"], g - 1)
                for n, (out, sign) in enumerate(((pw, 1.0), (rw, -1.0))):
                    if past(g, 1):
                        act.wait_ge(SEM[e, "weights"], 2 * g)
                    nc.scalar.activation(clip[:, n, :], xd[:, s, :], ACT.Relu, scale=sign).then_inc(
                        SEM[e, "clipped"], 1)
                    act.wait_ge(SEM[e, "clipped"], 2 * g + n + 1)
                    nc.scalar.activation(out[:, s, :], clip[:, n, :], ACT.Exp, scale=-1.0).then_inc(
                        SEM[e, "weights"], 1)

            def store(g, s, u):
                act.wait_ge(SEM[e, "turned"], g + 1)
                if past(g, 2):
                    act.wait_ge(SEM[e, "stored", s], 16 * u)
                b = OUT_BANK[kind]
                nc.scalar.activation(rows_out[:, s, :, 0:D], bank(b).rearrange("p (c d) -> p c d", d=D),
                                     ACT.Copy).then_inc(SEM[e, "evac"], 1)
                n = 1 if kind == "sum" else 2
                if kind == "gat":
                    small = PS[:, (b + 1) * BANK:(b + 4) * BANK].rearrange("p (k c h x) -> p k c h x", k=3, c=CH,
                                                                           h=HEADS3)[:, :, :, :, 0]
                    to = rows_out[:, s, :, D:k].rearrange("p c (k h) -> p k c h", k=3)
                else:
                    h = HEADS1 if kind == "attn" else D
                    small = bank(b + 1).rearrange("p (c h x) -> p c h x", c=CH, h=h)[:, :, :, 0]
                    to = rows_out[:, s, :, D:k]
                if kind != "sum":
                    nc.scalar.activation(to, small, ACT.Copy).then_inc(SEM[e, "evac"], 1)
                act.wait_ge(SEM[e, "evac"], n * (g + 1))
                act.dma_start(out_d[e][bass.ds(g * GE, GE), :].rearrange("(c p) d -> p c d", p=P),
                              rows_out[:, s, :, 0:k]).then_inc(SEM[e, "stored", s], 16)

            def body(g, s, u):
                if past(g, 2):
                    store(g - 2, s, u - 1)
                if kind in ("attn", "gat") and below(g, GROUPS - 1):
                    copy_q(g + 1, 1 - s, prev(u, s))
                if kind != "sum":
                    weights(g, s, u)

            if kind in ("attn", "gat"):
                copy_q(0, 0, 0)
            stream(act, body)
            store(GROUPS - 2, 0, PAIRS - 1)
            store(GROUPS - 1, 1, PAIRS - 1)

        block = ctx.enter_context(nc.Block())

        @block.sync
        def _(sp):
            sp.dma_start(src[:, :], t["src"]).then_inc(loaded["src"], 16)
            for n in range(3):
                sp.dma_start(dst_line[n], t["dst_line"][n:n + EP].rearrange("(g e) -> g e", e=GE)).then_inc(
                    loaded["dst"], 16)
            sp.dma_start(dst_col, t["dst_col"]).then_inc(loaded["dst"], 16)
            sp.dma_start(W[:, :], t["weights"]).then_inc(loaded["weights"], 16)
            sp.dma_start(X[:, :], t["xT"]).then_inc(loaded["weights"], 16)
            sp.dma_start(We_k[:, :], t["We_k"]).then_inc(loaded["weights"], 16)
            sp.dma_start(We_v[:, :], t["We_v"]).then_inc(loaded["weights"], 16)
            for e in ("e1", "e3", "e4"):
                sp.dma_start(window_d[e][NP:NP + P, :], t["zero"]).then_inc(loaded["weights"], 16)
            turn(sp, "s.save")
            sp.dma_start(rank_d.rearrange("(g e) -> g e", e=GE), rank_l[:, :]).then_inc(whole_done, 16)
            sp.dma_start(reset_d.rearrange("(g e) -> g e", e=GE), reset_l[:, :]).then_inc(whole_done, 16)
            sp.dma_start(keep_d.rearrange("(g e) -> g e", e=GE), keep_l[:, :]).then_inc(whole_done, 16)
            sp.dma_start(first_d.rearrange("a (g c) -> (a g) c", c=CH), first_l[:, :]).then_inc(whole_done, 16)
            turn(sp, "s.first_row")
            sp.dma_start(first_s[:, :], first_d).then_inc(whole_done, 16)
            edges_sync(sp, "e0")
            turn(sp, "s.live")
            with nc.allow_non_contiguous_dma(reason="3200 degrees, once"):
                sp.dma_start(deg_d.rearrange("(t p) -> p t", p=P), deg[:, :]).then_inc(degrees_here, 16)
            sp.wait_ge(degrees_here, 16)
            sp.dma_start(C[:, :], deg_d.partition_broadcast(P)).then_inc(degrees_here, 16)

            def save_table(e, name):
                for b, _, tiles in turns(sp, name):
                    lo, hi = tiles.start * P, tiles.stop * P
                    sp.dma_start(table_d[e][lo:hi, :].rearrange("(t p) d -> p t d", p=P),
                                 R[:, tiles, 0:KINDS[e]["row"]]).then_inc(table_saved, 16)

            save_table("e1", "kv_table")
            edges_sync(sp, "e1")
            save_table("e2", "x2_table")
            edges_sync(sp, "e2")
            for e in ("e3", "e4"):
                save_table(e, f"{e}.table")
                edges_sync(sp, e)
            for b, _, tiles in turns(sp, "y_save"):
                sp.dma_start(t["out"][tiles.start * P:tiles.stop * P, :].rearrange("(t p) d -> p t d", p=P),
                             R[:, tiles, 0:D]).then_inc(out_saved, 16)
            sp.wait_ge(out_saved, 16 * len(PARTS))

        @block.gpsimd
        def _(pool):
            for n, e in enumerate(KINDS):
                if e == "e1":
                    spread(pool, "e1", "q_spread")
                if e in ("e3", "e4"):
                    spread(pool, e, f"{e}.spread")
                if e != "e0":
                    turn(pool, f"{e}.edges")
                    pool.wait_ge(table_saved, TABLES * n)
                edges_gpsimd(pool, e)
                gather_ends(pool, e)

        @block.tensor
        def _(pe):
            structure_tensor(pe)
            edges_tensor(pe, "e0")
            counts_tensor(pe)
            rows_to_features(pe, "e0.turn", R[:, :, 0:D])
            linear(pe, "msg", [(w("w_msg"), A)])
            linear(pe, "r", [(w("w_ih", 0, D), S1), (w("w_hh", 0, D), X)])
            linear(pe, "z", [(w("w_ih", D, D), S1), (w("w_hh", D, D), X)])
            linear(pe, "hn", [(w("w_hh", 2 * D, D), X)])
            linear(pe, "in", [(w("w_ih", 2 * D, D), S1)])
            norm_tensor(pe, "ln0", B, S1, C)
            norm_tensor(pe, "n0", A, S1, C)
            row_linear(pe, "q", X, w("wq"))
            row_linear(pe, "k", X, w("wk"))
            row_linear(pe, "v", X, w("wv"))
            edges_tensor(pe, "e1")
            rows_to_features(pe, "a.turn", R[:, :, 0:D])
            linear(pe, "skip", [(w("wskip"), X)])
            linear(pe, "a.gate", [(gate_w[:, 0, :], A), (gate_w[:, 1, :], B)])
            for c in range(4):
                linear(pe, f"ffn{c}", [(w("ffn1", c * D, D), C)])
            linear(pe, "ffn", [(w("ffn2", c * D, D), G4[c]) for c in range(4)])
            norm_tensor(pe, "n1", A, S1, C)
            features_to_rows(pe, "x2", X)
            edges_tensor(pe, "e2")
            rows_to_features(pe, "c.turn", R[:, :, 0:D])
            linear(pe, "c.na", [(w("ones"), B)])
            linear(pe, "c.nx", [(w("ones"), C)])
            linear(pe, "c.mlp", [(w("mlp"), A)])
            norm_tensor(pe, "n2", A, S1, C)
            for n, (e, x_in, g, gs) in enumerate((("e3", X, "g1", "g1s"), ("e4", B, "g2", "g2s"))):
                for b, _, tiles in turns(pe, f"{e}.terms"):
                    for i in range(tiles.start, tiles.stop):
                        mm = pe.matmul(PM[:, i * 2 * HEADS3:(i + 1) * 2 * HEADS3], x_in[:, i * P:(i + 1) * P],
                                       comp[:, n, :], start=True, stop=True)
                    mm.then_inc(part_done[b], 1)
                row_linear(pe, f"{e}.h", x_in, w(g))
                edges_tensor(pe, e)
                for b, _, tiles in turns(pe, f"{e}.sum"):
                    for i in range(tiles.start, tiles.stop):
                        o = PN[:, i * P:(i + 1) * P]
                        pe.matmul(o, w(gs), x_in[:, i * P:(i + 1) * P], start=True, stop=False)
                        mm = pe.matmul(o, R[:, i, 0:D], w("ident"), start=False, stop=True)
                    mm.then_inc(part_done[b], 1)
            norm_tensor(pe, "n3", A, S1, C)
            features_to_rows(pe, "y", X)

        @block.vector
        def _(dve):
            def two(name, out, x, y, op):
                for b, c, _ in turns(dve, name):
                    nc.vector.tensor_tensor(out[:, c], x[:, c], y[:, c], op).then_inc(part_done[b], 1)

            def live_rows(tiles, n):
                return live[:, tiles].rearrange("p (t o) -> p t o", o=1).to_broadcast([P, tiles.stop - tiles.start, n])

            def mask(name):
                for b, _, tiles in turns(dve, name):
                    nc.vector.tensor_tensor(R[:, tiles, 0:D], R[:, tiles, 0:D], live_rows(tiles, D),
                                            ALU.mult).then_inc(part_done[b], 1)

            def over_heads(name, rows_, k, heads):
                for b, _, tiles in turns(dve, name):
                    n = tiles.stop - tiles.start
                    x = rows_[:, tiles, 0:D].rearrange("p t (h c) -> p t h c", h=heads)
                    mul = s8[:, k, tiles, 0:heads].rearrange("p t (h o) -> p t h o", o=1).to_broadcast(
                        [P, n, heads, D // heads])
                    nc.vector.tensor_tensor(x, x, mul, ALU.mult).then_inc(part_done[b], 1)

            structure_vector(dve)
            edges_vector(dve, "e0")
            counts_vector(dve)

            mask("e0.mask")
            dve.wait_ge(degrees_here, 32)
            for b, c, _ in turns(dve, "msg_out"):
                nc.vector.scalar_tensor_tensor(A[:, c], C[:, c], w("b_msg"), PN[:, c], ALU.mult, ALU.add).then_inc(
                    part_done[b], 1)
            for b, c, _ in turns(dve, "hn_out"):
                nc.vector.scalar_tensor_tensor(B[:, c], PN[:, c], w("b_hh", 2, 1), B[:, c], ALU.add,
                                               ALU.mult).then_inc(part_done[b], 1)
            two("in_out", B, PN, B, ALU.add)
            two("h1", S1, X, B, ALU.subtract)
            two("h2", S1, S1, C, ALU.mult)
            two("h3", B, S1, B, ALU.add)
            norm_vector(dve, "ln0", B, S1, C, B)
            two("y0b", A, A, B, ALU.add)
            two("y0c", A, A, X, ALU.add)
            norm_vector(dve, "n0", A, S1, C, X)
            for b, c, tiles in turns(dve, "k_row"):
                nc.vector.tensor_copy(R[:, tiles, 0:D], PN[:, c].rearrange("p (t d) -> p t d", d=D)).then_inc(
                    part_done[b], 1)

            edges_vector(dve, "e1")
            for b, _, tiles in turns(dve, "a.den"):
                nc.vector.tensor_scalar(s8[:, 0, tiles, :], R[:, tiles, D:D + HEADS1], 1e-16, None,
                                        ALU.add).then_inc(part_done[b], 1)
            for b, _, tiles in turns(dve, "a.rden"):
                nc.vector.reciprocal(s8[:, 1, tiles, :], s8[:, 0, tiles, :]).then_inc(part_done[b], 1)
            for b, _, tiles in turns(dve, "a.live"):
                nc.vector.tensor_tensor(s8[:, 0, tiles, :], s8[:, 1, tiles, :], live_rows(tiles, HEADS1),
                                        ALU.mult).then_inc(part_done[b], 1)
            over_heads("a.norm", R, 0, HEADS1)
            two("a.diff", C, A, B, ALU.subtract)
            two("a.mix", C, C, S1, ALU.mult)
            two("a.att", A, A, C, ALU.subtract)
            two("a.h", A, A, X, ALU.add)

            def sum_nodes(name, k, x):
                for b, c, _ in turns(dve, name):
                    nc.vector.tensor_reduce(part_sum[:, k, b:b + 1], x[:, c.start:min(c.stop, NODES)], AX,
                                            ALU.add).then_inc(part_done[b], 1)

            def step(name):
                turn(dve, name)
                return nc.vector

            sum_nodes("gn.sum", 0, A)
            step("gn.all").tensor_reduce(col[:, 4:5], part_sum[:, 0, :], AX, ALU.add).then_inc(whole_done, 1)
            step("gn.mean").tensor_scalar(col[:, 5:6], col[:, 4:5], 1.0 / NODES, w("gn_ms"), ALU.mult,
                                          ALU.mult).then_inc(whole_done, 1)
            for b, c, _ in turns(dve, "gn.center"):
                nc.vector.tensor_scalar(S1[:, c], A[:, c], col[:, 5:6], None, ALU.subtract).then_inc(part_done[b], 1)
            sum_nodes("gn.sqsum", 1, B)
            step("gn.var").tensor_reduce(col[:, 6:7], part_sum[:, 1, :], AX, ALU.add).then_inc(whole_done, 1)
            step("gn.inv").reciprocal(col[:, 8:9], col[:, 7:8]).then_inc(whole_done, 1)
            step("gn.gain").tensor_tensor(col[:, 9:10], col[:, 8:9], w("gn_w"), ALU.mult).then_inc(whole_done, 1)
            for b, c, _ in turns(dve, "gn.out"):
                nc.vector.tensor_scalar(C[:, c], S1[:, c], col[:, 9:10], w("gn_b"), ALU.mult, ALU.add).then_inc(
                    part_done[b], 1)
            for b, c, _ in turns(dve, "ffn_out"):
                nc.vector.scalar_tensor_tensor(A[:, c], PN[:, c], w("fb2"), C[:, c], ALU.add, ALU.add).then_inc(
                    part_done[b], 1)
            two("y1", A, A, X, ALU.add)
            norm_vector(dve, "n1", A, S1, C, X)

            edges_vector(dve, "e2")
            for b, _, tiles in turns(dve, "c.norm"):
                nc.vector.tensor_tensor(R[:, tiles, 0:D], R[:, tiles, 0:D], R[:, tiles, D:2 * D],
                                        ALU.mult).then_inc(part_done[b], 1)
            mask("c.mask")
            for b, c, _ in turns(dve, "c.maxa"):
                nc.vector.tensor_scalar(B[:, c], PN[:, c], 1e-24, None, ALU.max).then_inc(part_done[b], 1)
            two("c.unit", A, A, S1, ALU.mult)
            two("c.scaled", A, A, C, ALU.mult)
            two("c.feat", A, A, X, ALU.add)
            for b, c, _ in turns(dve, "y2"):
                nc.vector.scalar_tensor_tensor(A[:, c], PN[:, c], w("mlp_b"), X[:, c], ALU.add, ALU.add).then_inc(
                    part_done[b], 1)
            norm_vector(dve, "n2", A, S1, C, X)

            H2 = HEADS3
            small = [s8[:, k, :, 0:H2] for k in range(8)]
            hrow = S1[:, :].rearrange("p (t d) -> p t d", d=D)
            for e in ("e3", "e4"):
                step(f"{e}.terms_out").tensor_copy(terms[:, :, :], PM[:, 0:TILES * 2 * H2].rearrange(
                    "p (t k) -> p t k", k=2 * H2)).then_inc(whole_done, 1)
                for name, out, at, k in (("ad_row", C_rows, 0, H2), ("as_row", R, D, 0)):
                    for b, _, tiles in turns(dve, f"{e}.{name}"):
                        n = tiles.stop - tiles.start
                        nc.vector.tensor_copy(
                            out[:, tiles, at:at + D].rearrange("p t (h c) -> p t h c", h=H2),
                            terms[:, tiles, k:k + H2].rearrange("p t (h o) -> p t h o", o=1).to_broadcast(
                                [P, n, H2, D // H2])).then_inc(part_done[b], 1)
                for b, c, _ in turns(dve, f"{e}.h_out"):
                    nc.vector.tensor_copy(S1[:, c], PN[:, c]).then_inc(part_done[b], 1)
                step(f"{e}.self_z").tensor_tensor(small[0], terms[:, :, 0:H2], terms[:, :, H2:], ALU.add).then_inc(
                    whole_done, 1)
                step(f"{e}.self").scalar_tensor_tensor(small[1], small[0], 0.2, small[0], ALU.mult,
                                                       ALU.max).then_inc(whole_done, 1)
                edges_vector(dve, e)
                dn, un, sn = (R[:, :, D + k * H2:D + (k + 1) * H2] for k in range(3))
                live2 = live_rows(slice(0, TILES), H2)
                step(f"{e}.m").tensor_tensor(small[2], un, sn, ALU.max).then_inc(whole_done, 1)
                step(f"{e}.m_live").tensor_tensor(small[3], small[2], live2, ALU.mult).then_inc(whole_done, 1)
                step(f"{e}.m_mask").tensor_scalar(small[4], live2, 1.0, -LOW, ALU.subtract, ALU.mult).then_inc(
                    whole_done, 1)
                step(f"{e}.m_all").tensor_tensor(small[2], small[3], small[4], ALU.add).then_inc(whole_done, 1)
                step(f"{e}.we_x").tensor_tensor(small[3], small[2], small[1], ALU.max).then_inc(whole_done, 1)
                turn(dve, f"{e}.ws_x")
                nc.vector.tensor_tensor(small[4], small[2], small[3], ALU.subtract)
                nc.vector.tensor_tensor(small[5], small[1], small[3], ALU.subtract).then_inc(whole_done, 1)
                step(f"{e}.we_live").tensor_tensor(small[3], small[6], live2, ALU.mult).then_inc(whole_done, 1)
                step(f"{e}.den").tensor_tensor(small[4], dn, small[3], ALU.mult).then_inc(whole_done, 1)
                step(f"{e}.den2").tensor_tensor(small[5], small[4], small[7], ALU.add).then_inc(whole_done, 1)
                step(f"{e}.den3").tensor_scalar(small[4], small[5], 1e-16, None, ALU.add).then_inc(whole_done, 1)
                step(f"{e}.rden").reciprocal(small[5], small[4]).then_inc(whole_done, 1)
                step(f"{e}.we_n").tensor_tensor(small[4], small[3], small[5], ALU.mult).then_inc(whole_done, 1)
                step(f"{e}.ws_n").tensor_tensor(small[6], small[7], small[5], ALU.mult).then_inc(whole_done, 1)
                over_heads(f"{e}.num", R, 4, H2)
                over_heads(f"{e}.hs", hrow, 6, H2)
                for b, _, tiles in turns(dve, f"{e}.agg"):
                    nc.vector.tensor_tensor(R[:, tiles, 0:D], R[:, tiles, 0:D], hrow[:, tiles, :],
                                            ALU.add).then_inc(part_done[b], 1)
                if e == "e4":
                    for b, c, _ in turns(dve, f"{e}.act"):
                        nc.vector.scalar_tensor_tensor(A[:, c], PN[:, c], gat_bias[:, 1:2], X[:, c], ALU.add,
                                                       ALU.add).then_inc(part_done[b], 1)
            norm_vector(dve, "n3", A, S1, C, X)

        @block.scalar
        def _(act):
            def one(name, out, x, func=ACT.Copy, **k):
                for b, c, _ in turns(act, name):
                    nc.scalar.activation(out[:, c], x[:, c], func, **k).then_inc(part_done[b], 1)

            def rows_of(name, out, at):
                for b, c, tiles in turns(act, name):
                    nc.scalar.activation(out[:, tiles, at:at + D], PN[:, c].rearrange("p (t d) -> p t d", d=D),
                                         ACT.Copy).then_inc(part_done[b], 1)

            def norm_scalar(p, c, q):
                one(f"{p}.square", q, c, ACT.Square)
                one(f"{p}.inv", q, PN, ACT.Abs_reciprocal_sqrt, bias=eps[:, 0:1])

            edges_scalar(act, "e0")
            one("e0.turned", A, PN)
            one("msg_mean", S1, A, ACT.Identity, bias=col[:, 1:2])
            one("r_out", B, PN, ACT.Sigmoid, bias=col[:, 2:3])
            one("z_out", C, PN, ACT.Sigmoid, bias=col[:, 3:4])
            one("n", B, B, ACT.Tanh, bias=w("b_ih", 2, 1))
            norm_scalar("ln0", S1, C)
            one("y0a", B, B, ACT.Identity, scale=w("gamma0"), bias=w("beta0"))
            norm_scalar("n0", S1, C)
            rows_of("q_row", C_rows, 0)
            rows_of("v_row", R, D)

            edges_scalar(act, "e1")
            one("a.turned", A, PN)
            one("skip_out", B, PN, ACT.Identity, bias=w("bskip"))
            one("a.gate_out", S1, PN, ACT.Sigmoid)
            one("gn.sq", B, S1, ACT.Square)
            turn(act, "gn.std")
            nc.scalar.activation(col[:, 7:8], col[:, 6:7], ACT.Sqrt, bias=eps[:, 0:1], scale=1.0 / NODES).then_inc(
                whole_done, 1)
            for c in range(4):
                one(f"ffn{c}_out", G4[c], PN, ACT.Gelu, bias=w("fb1", c, 1))
            norm_scalar("n1", S1, C)
            rows_of("x2_row", R, 0)

            edges_scalar(act, "e2")
            for b, _, tiles in turns(act, "c.den2"):
                nc.scalar.activation(R[:, tiles, D:2 * D], R[:, tiles, D:2 * D], ACT.Square).then_inc(
                    part_done[b], 1)
            for b, _, tiles in turns(act, "c.rden"):
                nc.scalar.activation(R[:, tiles, D:2 * D], R[:, tiles, D:2 * D], ACT.Abs_reciprocal_sqrt).then_inc(
                    part_done[b], 1)
            one("c.turned", A, PN)
            one("c.sqa", B, A, ACT.Square)
            one("c.inva", S1, B, ACT.Abs_reciprocal_sqrt)
            one("c.sqx", C, X, ACT.Square)
            one("c.rootx", C, PN, ACT.Sqrt)
            norm_scalar("n2", S1, C)

            for e in ("e3", "e4"):
                rows_of(f"{e}.h_row", R, 0)
                edges_scalar(act, e)
                for name, to, x in (("we", 6, 4), ("ws", 7, 5)):
                    turn(act, f"{e}.{name}")
                    nc.scalar.activation(s8[:, to, :, 0:HEADS3], s8[:, x, :, 0:HEADS3], ACT.Exp).then_inc(
                        whole_done, 1)
                if e == "e3":
                    one(f"{e}.act", B, PN, ACT.Relu, bias=gat_bias[:, 0:1])
            norm_scalar("n3", S1, C)
            rows_of("y_row", R, 0)


def host_arrays(a):
    f = np.float32

    def padded(x, n):
        return np.concatenate([x, np.zeros((n - x.shape[0],) + x.shape[1:], x.dtype)])

    def fill(n, value):
        return np.full(n, value, np.int32)

    x = padded(a["x"], NP)
    dst = np.concatenate([a["dst"], fill(EP - EDGES, NP - 1)])
    k = np.arange(P)

    def same(heads):
        return (k[:, None] * heads // D == k[None, :] * heads // D).astype(f)

    parts = {
        "w_msg": a["L0_gnn_W_msg"].T, "w_ih": a["L0_gnn_w_ih"].T, "w_hh": a["L0_gnn_w_hh"].T,
        "wq": a["L1_gnn_Wq"], "wk": a["L1_gnn_Wk"], "wv": a["L1_gnn_Wv"], "wskip": a["L1_gnn_Wskip"],
        "ffn1": a["L1_gnn_W1"], "ffn2": a["L1_gnn_W2"].reshape(4, D, D).transpose(1, 0, 2).reshape(D, 4 * D),
        "mlp": a["L2_gnn_mlp_w"],
        "g1": a["L3_gnn_W1"], "g1s": a["L3_gnn_Wsk1"], "g1T": a["L3_gnn_W1"].T,
        "g2": a["L3_gnn_W2"], "g2s": a["L3_gnn_Wsk2"], "g2T": a["L3_gnn_W2"].T,
        "ident": np.eye(P, dtype=f), "ones": np.ones((P, P), f), "avg": np.full((P, P), 1.0 / D, f),
        "upper": np.triu(np.ones((P, P), f)), "strict": np.triu(np.ones((P, P), f), 1),
        "heads8": same(HEADS1) * f((D // HEADS1) ** -0.5),
        "head2": (k[:, None] * HEADS3 // D == np.arange(HEADS3)[None, :]).astype(f),
        "iota": np.tile(k.astype(f), (P, 1)), "part": k.astype(f)[:, None],
        "node": (np.arange(TILES)[None, :] * P + k[:, None]).astype(f),
        "beta": a["L1_gnn_Wbeta"].reshape(3, D).T,
        "b_ih": a["L0_gnn_b_ih"].reshape(3, D).T, "b_hh": a["L0_gnn_b_hh"].reshape(3, D).T,
        "fb1": a["L1_gnn_b1"].reshape(4, D).T,
    }
    for name, key in (("b_msg", "L0_gnn_b_msg"), ("bq", "L1_gnn_bq"), ("gamma0", "L0_gnn_ln_gamma"), ("beta0", "L0_gnn_ln_beta"), ("bskip", "L1_gnn_bskip"),
                      ("gn_w", "L1_gnn_gn_w"), ("gn_b", "L1_gnn_gn_b"), ("gn_ms", "L1_gnn_gn_ms"),
                      ("fb2", "L1_gnn_b2"), ("mlp_b", "L2_gnn_mlp_b"),
                      ("att_s1", "L3_gnn_att_src1"), ("att_d1", "L3_gnn_att_dst1"), ("g1b", "L3_gnn_b1"),
                      ("g1sb", "L3_gnn_bsk1"), ("att_s2", "L3_gnn_att_src2"), ("att_d2", "L3_gnn_att_dst2"),
                      ("g2b", "L3_gnn_b2"), ("g2sb", "L3_gnn_bsk2")):
        parts[name] = a[key].reshape(D, 1)
    return {
        "weights": np.concatenate([parts[n] for n, _ in WEIGHTS], axis=1),
        "x": x, "xT": np.ascontiguousarray(x.T),
        "src": np.ascontiguousarray(np.concatenate([a["src"], fill(EP - EDGES, 0)]).reshape(CHUNKS, P).T).view(
            np.uint32),
        "dst_line": np.concatenate([fill(1, -1), dst, fill(1, NP)]),
        "dst_col": np.ascontiguousarray(dst.reshape(CHUNKS, P).T),
        "We_k": np.concatenate([a["L1_gnn_We"], a["L1_gnn_bk"][None, :]]),
        "We_v": np.concatenate([a["L1_gnn_We"], a["L1_gnn_bv"][None, :]]),
        "zero": np.zeros((P, D), f),
        "ea11": np.concatenate([padded(a["edge_attr_10"], EP).T, np.ones((1, EP), f)]),
        "ea128": padded(a["edge_attr_128"], EP),
    }


def kernel(**inputs):
    import concourse.bacc as bacc
    from concourse.bass_utils import run_bass_kernel_spmd

    arrays = host_arrays({k: np.asarray(v) for k, v in inputs.items()})
    nc = bacc.Bacc("TRN2", target_bir_lowering=False, num_devices=1)
    t = {k: nc.dram_tensor(f"in_{k}", v.shape, mybir.dt.from_np(v.dtype), kind="ExternalInput").ap()
         for k, v in arrays.items()}
    t["out"] = nc.dram_tensor("out", [NP, D], F32, kind="ExternalOutput").ap()
    gnn(nc, t)
    r = run_bass_kernel_spmd(nc, [{f"in_{k}": v for k, v in arrays.items()}], core_ids=[0])
    return r.results[0]["out"][:NODES]
```

```python
from contextlib import ExitStack

import numpy as np

import concourse.bass as bass
from concourse import mybir

F32 = mybir.dt.float32
BF16 = mybir.dt.bfloat16
I32 = mybir.dt.int32
U32 = mybir.dt.uint32
ALU = mybir.AluOpType
ACT = mybir.ActivationFunctionType
AX = mybir.AxisListType.X

NODES, EDGES, D, EDGE_D = 3125, 50000, 128, 10
P = 128
TILES = -(-NODES // P)
NP = TILES * P
GE = 512
CH = GE // P
GROUPS = -(-EDGES // GE)
EP = GROUPS * GE
CHUNKS = EP // P
PAIRS = GROUPS // 2
RING = 4
ROUNDS = GROUPS // RING
LOW = -3.0e38
BANK = 512

HEADS1, HEADS3 = 8, 2
KINDS = {
    "e0": dict(kind="sum", row=D, out=D),
    "e1": dict(kind="attn", row=2 * D, out=D + HEADS1),
    "e2": dict(kind="soft", row=D, out=2 * D),
    "e3": dict(kind="gat", row=2 * D, out=D + 3 * HEADS3),
    "e4": dict(kind="gat", row=2 * D, out=D + 3 * HEADS3),
}

WEIGHTS = [("w_msg", 128), ("w_ih", 384), ("w_hh", 384), ("wq", 128), ("wk", 128), ("wv", 128), ("wskip", 128),
           ("ffn1", 512), ("ffn2", 512), ("mlp", 128),
           ("g1", 128), ("g1s", 128), ("g1T", 128), ("g2", 128), ("g2s", 128), ("g2T", 128),
           ("ident", 128), ("ones", 128), ("avg", 128), ("upper", 128), ("strict", 128),
           ("heads8", 128), ("head2", HEADS3), ("iota", 128), ("part", 1), ("we_part", 3),
           ("node", TILES), ("beta", 3),
           ("b_ih", 3), ("b_hh", 3), ("b_msg", 1), ("gamma0", 1), ("beta0", 1), ("bq", 1), ("bskip", 1),
           ("gn_w", 1), ("gn_b", 1),
           ("gn_ms", 1), ("fb1", 4), ("fb2", 1), ("mlp_b", 1),
           ("att_s1", 1), ("att_d1", 1), ("g1b", 1), ("g1sb", 1),
           ("att_s2", 1), ("att_d2", 1), ("g2b", 1), ("g2sb", 1)]


def columns(spec):
    at, out = 0, {}
    for name, n in spec:
        out[name] = (at, n)
        at += n
    return out, at


WCOL, WIDTH = columns(WEIGHTS)

PARTS = [(lo, min(lo + BANK // P, TILES)) for lo in range(0, TILES, BANK // P)]
WHOLE = "whole"


def norm_steps(p):
    return [f"{p}.mean", f"{p}.center", f"{p}.square", f"{p}.var", f"{p}.std", f"{p}.inv", f"{p}.spread",
            f"{p}.scale"]


def gat_steps(p):
    return [f"{p}.terms", (f"{p}.terms_out", 1, WHOLE), f"{p}.ad_row", (f"{p}.spread", 0, None),
            f"{p}.as_row", f"{p}.h", f"{p}.h_row",
            (f"{p}.table", 0, None), f"{p}.h_out",
            (f"{p}.self_z", 1, WHOLE), (f"{p}.self", 1, WHOLE), (f"{p}.edges", 0, WHOLE), f"{p}.ends",
            (f"{p}.m", 1, WHOLE), (f"{p}.m_live", 1, WHOLE), (f"{p}.m_mask", 1, WHOLE), (f"{p}.m_all", 1, WHOLE),
            (f"{p}.we_x", 1, WHOLE), (f"{p}.ws_x", 1, WHOLE), (f"{p}.we", 1, WHOLE), (f"{p}.ws", 1, WHOLE),
            (f"{p}.we_live", 1, WHOLE), (f"{p}.den", 1, WHOLE), (f"{p}.den2", 1, WHOLE), (f"{p}.den3", 1, WHOLE),
            (f"{p}.rden", 1, WHOLE), (f"{p}.we_n", 1, WHOLE), (f"{p}.ws_n", 1, WHOLE),
            f"{p}.num", f"{p}.hs", f"{p}.agg", f"{p}.sum", f"{p}.act"]


STEPS = (
    [(n, k, WHOLE) for n, k in (
        ("s.start", 1), ("s.keep", 1), ("s.next", 1), ("s.reset", 1), ("s.count", 1), ("s.before", 1), ("s.rho", 1),
        ("s.first", 1), ("s.rank", 1), ("s.save", 16 * 3), ("s.first_row", 16),
        ("s.lo", 1), ("s.hi", 1), ("s.lof", 1), ("s.hif", 1), ("e0.edges", 0),
        ("s.deg_out", 1), ("s.live", 1),
        ("s.within", 2), ("s.total", 2), ("s.total_out", 1), ("s.run", 1), ("s.end", 1), ("s.end2", 1), ("s.end3", 1),
        ("s.nrun", 1), ("s.nlive", 1), ("s.nlive2", 1), ("s.nlive3", 1), ("s.empty", 1), ("s.empty2", 1),
        ("s.slot", 1), ("s.slot2", 1), ("s.slot3", 1),
        ("mean", 1), ("mean2", 1), ("gb", 1), ("a.wb", 4),
        ("g.att", 4), ("g.comp", 1), ("g.comp_out", 1),
        ("w.hi", 1), ("w.rest", 1), ("w.mid", 1), ("w.rest2", 1), ("w.lo", 1), ("w.a", 1), ("w.b", 1), ("w.c", 1),
        ("g.bias", 2))]
    + ["e0.ends", "e0.mask", "e0.turn", "e0.turned", "msg", "msg_out", "msg_mean", "r", "r_out", "z", "z_out",
       "hn", "hn_out", "in", "in_out", "n", "h1", "h2", "h3"]
    + norm_steps("ln0") + ["y0a", "y0b", "y0c"] + norm_steps("n0")
    + ["q", "q_row", ("q_spread", 0, None), "k", "k_row", "v", "v_row", ("kv_table", 0, None),
       "skip", "skip_out", ("e1.edges", 0, WHOLE), "e1.ends",
       "a.den", "a.rden", "a.live", "a.norm", "a.turn", "a.turned", "a.gate", "a.gate_out", "a.diff",
       "a.mix", "a.att", "a.h", "gn.sum", ("gn.all", 1, WHOLE), ("gn.mean", 1, WHOLE), "gn.center", "gn.sq",
       "gn.sqsum", ("gn.var", 1, WHOLE), ("gn.std", 1, WHOLE), ("gn.inv", 1, WHOLE), ("gn.gain", 1, WHOLE), "gn.out"]
    + [f"ffn{c}{o}" for c in range(4) for o in ("", "_out")]
    + ["ffn", "ffn_out", "y1"] + norm_steps("n1")
    + ["x2", "x2_row", ("x2_table", 0, None), "c.sqx", "c.nx", "c.rootx", ("e2.edges", 0, WHOLE), "e2.ends",
       "c.den2", "c.rden", "c.better", "c.better2", "c.norm", "c.mask", "c.turn", "c.turned", "c.sqa", "c.na", "c.roota",
       "c.max", "c.inv", "c.ratio", "c.spread", "c.scaled", "c.feat", "c.mlp", "y2"]
    + norm_steps("n2")
    + gat_steps("e3") + gat_steps("e4") + norm_steps("n3") + ["y", "y_row", ("y_save", 0, None)]
)
LOADS = {"src": 16, "dst": 16 * 4, "weights": 16 * 6, "attributes": 16}
PART_BEFORE, WHOLE_BEFORE = {}, {}
_part = _whole = 0
for _s in STEPS:
    _name, _n, _kind = (_s, 1, None) if isinstance(_s, str) else _s
    assert _name not in PART_BEFORE, _name
    PART_BEFORE[_name], WHOLE_BEFORE[_name] = _part, _whole
    if _kind == WHOLE:
        _whole += _n
    else:
        _part += _n


ATTR_PART = ("hi", "hi", "mid", "mid", "hi", "lo")
WE_PART = ("hi", "mid", "hi", "mid", "lo", "hi")
BIAS_PART = ("hi", "mid", "lo")
K_ATTR = EDGE_D * len(WE_PART) + len(BIAS_PART)
FLAT = EDGE_D * EP // P


class Group:

    def __init__(self, g, place=None, round_=None):
        self.g = g
        self.r = g % RING if place is None else place
        self.v = g // RING if round_ is None else round_
        self.s = self.r % 2
        self.u = RING // 2 * self.v + self.r // 2

    def by(self, n):
        return Group(self.g + n, (self.r + n) % RING, self.v + (self.r + n) // RING)


def gnn(nc, t):
    with ExitStack() as ctx:
        def sb(name, shape, dt=F32):
            return ctx.enter_context(nc.sbuf_tensor(name, shape, dt))

        def sem(name):
            return ctx.enter_context(nc.semaphore(name))

        def dram(name, shape, dt=F32):
            return nc.dram_tensor(name, shape, dt, kind="Internal").ap()

        marks_d = dram("marks_d", [GROUPS * 2 * GE], BF16)
        keep_d = dram("keep_d", [EP], BF16)
        first_d = dram("first_d", [1, CHUNKS], I32)
        deg_d = dram("deg_d", [NP])
        attr_d = dram("attr_d", [K_ATTR, EP], BF16)
        window_d = {e: dram(f"{e}_window", [NP + P, D]) for e in ("e1", "e3", "e4")}
        table_d = {"e0": t["x"]}
        for e in ("e1", "e2", "e3", "e4"):
            table_d[e] = dram(f"{e}_table", [NP, KINDS[e]["row"]])
        out_d = {e: dram(f"{e}_out", [EP, KINDS[e]["out"]]) for e in KINDS}

        W = sb("W", [P, WIDTH])

        def w(name, lo=0, n=None, p=P):
            a, k = WCOL[name]
            return W[0:p, a + lo:a + (k if n is None else lo + n)]

        src = sb("src", [P, CHUNKS], U32)
        live = sb("live", [P, TILES])
        slot = sb("slot", [P, TILES], U32)
        last = sb("last", [P, TILES], U32)
        X = sb("X", [P, NP])
        A = sb("A", [P, NP])
        B = sb("B", [P, NP])
        C = sb("C", [P, NP])
        S1 = sb("S1", [P, NP])
        R = sb("R", [P, TILES, 2 * D])
        R2 = R[:, :, :].rearrange("p t d -> p (t d)")
        G4 = [A, B, R2[:, 0:NP], R2[:, NP:2 * NP]]
        s8 = sb("s8", [P, 8, TILES, HEADS1])
        eps = sb("eps", [P, 1])
        col = sb("col", [P, 16])
        ns = sb("ns", [P, 5, TILES])
        part_sum = sb("part_sum", [P, 2, len(PARTS)])
        gate_w = sb("gate_w", [P, 2, P])
        beta_sum = sb("beta_sum", [P, 2])
        att = sb("att", [P, 2, 2 * HEADS3])
        comp = sb("comp", [P, 2, 2 * HEADS3])
        terms = sb("terms", [P, TILES, 2 * HEADS3])
        gat_bias = sb("gat_bias", [P, 2])

        MAXROW = 2 * D
        rows_in = sb("rows_in", [P, RING, CH, MAXROW])
        idx = sb("idx", [P, RING, CH], U32)
        marks_b = sb("marks_b", [P, RING, 2 * GE], BF16)
        rank_b, flag_b = marks_b[:, :, 0:GE], marks_b[:, :, GE:]
        ea = A[:, 0:RING * GE].rearrange("p (r e) -> p r e", r=RING)
        ea_parts = A[0:K_ATTR, 0:RING * GE // 2].bitcast(BF16).rearrange("p (r e) -> p r e", r=RING)
        win = sb("win", [P, RING, CH, D])
        one_hot = sb("one_hot", [P, 2, GE])
        qx = sb("qx", [P, 2, GE])
        prod = sb("prod", [P, GE])
        score = sb("score", [P, 2, GE])
        U = sb("U", [P, 2, GE + 1])
        xd = sb("xd", [P, 2, GE])
        clip = sb("clip", [P, 2, GE])
        pw = sb("pw", [P, 2, GE])
        rw = sb("rw", [P, 2, GE])
        pv = sb("pv", [P, GE])
        den = sb("den", [P, 2, GE])
        num = sb("num", [P, 2, GE])
        rows_out = sb("rows_out", [P, 2, CH, MAXROW])

        PS = ctx.enter_context(nc.psum_tensor("PS", [P, 8 * BANK], F32))
        PN = PS[:, 0:NP]
        PM = PS[:, 7 * BANK:8 * BANK]

        def bank(b, n=BANK):
            return PS[:, b * BANK:b * BANK + n]

        V_BANK, Q_BANK, A_BANK = 0, 3, 4
        K_BANKS = {"attn": (2, 7), "gat": (2, 2)}
        OUT_BANK = {"sum": 5, "attn": 5, "soft": 5, "gat": 3}
        MAX_BANK = 5

        loaded = {n: sem(f"loaded_{n}") for n in ("src", "dst", "weights", "attributes")}
        part_done = [sem(f"part_done{b}") for b in range(len(PARTS))]
        whole_done = sem("whole_done")
        moved = [sem(f"moved{b}") for b in range(len(PARTS))]
        moves = [0]
        table_saved = sem("table_saved")
        split_done = sem("split_done")
        attr_saved = sem("attr_saved")
        ATTR_SAVED = 16 * (len(ATTR_PART) + 1)
        degrees_here = sem("degrees_here")
        out_saved = sem("out_saved")
        TABLES = len(PARTS) * 16

        gate_pool = sem("gate_pool")
        gate_sp = sem("gate_sp")
        gate_act = sem("gate_act")
        deg_hot = sem("deg_hot")
        deg_mm = sem("deg_mm")
        SEM = {}
        SOFTMAX = ["scored", "u", "u_head", "x", "clipped", "weights", "pv", "den"]
        QUERY = ["q_ready", "one_hot", "q_copied"]
        USED = {"sum": [], "attn": ["k_ready", "product"] + QUERY + SOFTMAX, "soft": SOFTMAX,
                "gat": QUERY + SOFTMAX + ["max_turned", "max_evac"]}
        LOADS_OF = {"sum": 1, "attn": 1 + CH, "soft": 2, "gat": 1 + CH}
        for e in KINDS:
            kind = KINDS[e]["kind"]
            for n in ["idx_here", "expanded", "num", "turned", "evac"] + USED[kind]:
                SEM[e, n] = sem(f"{e}_{n}")
            for s in range(RING):
                SEM[e, "rows_here", s] = sem(f"{e}_rows_here{s}")
                SEM[e, "loads_here", s] = sem(f"{e}_loads_here{s}")
                if kind == "attn":
                    SEM[e, "attr_here", s] = sem(f"{e}_attr_here{s}")
            for s in range(2):
                SEM[e, "stored", s] = sem(f"{e}_stored{s}")

        def turn(eng, name, b=None):
            if WHOLE_BEFORE[name]:
                eng.wait_ge(whole_done, WHOLE_BEFORE[name])
            if PART_BEFORE[name]:
                for s in part_done if b is None else part_done[b:b + 1]:
                    eng.wait_ge(s, PART_BEFORE[name])

        def turns(eng, name):
            for b, (lo, hi) in enumerate(PARTS):
                turn(eng, name, b)
                yield b, slice(lo * P, hi * P), slice(lo, hi)

        def past(g, n):
            return not isinstance(g, int) or g >= n

        def below(g, n):
            return not isinstance(g, int) or g < n

        def stream(eng, body):
            for g in range(RING):
                body(Group(g))
            with eng.Fori(1, ROUNDS - 1) as i:
                for place in range(RING):
                    body(Group(RING * i + place, place, i))
            for g in range(RING * (ROUNDS - 1), GROUPS):
                body(Group(g))

        L = GROUPS
        dst_i = A[0:L, 0:3 * GE].bitcast(I32).rearrange("p (n e) -> p n e", n=3)
        dst_line = [dst_i[:, n, :] for n in range(3)]
        start_l = B[0:L, 0:GE]
        count_l = B[0:L, GE:2 * GE]
        rho_l = B[0:L, 2 * GE:3 * GE]
        next_l = B[0:L, 3 * GE:4 * GE]
        one_l = B[0:L, 4 * GE:5 * GE]
        marks_l = one_hot[0:L, 0, :].bitcast(BF16)
        rank_l = one_hot[0:L, 0, 0:GE // 2].bitcast(BF16)
        reset_l = one_hot[0:L, 0, GE // 2:GE].bitcast(BF16)
        keep_l = one_hot[0:L, 1, 0:GE // 2].bitcast(BF16)
        first_l = one_hot[0:L, 1, GE // 2:GE // 2 + CH].bitcast(I32)
        dst_col = S1[:, 0:CHUNKS].bitcast(I32)
        lo_i = S1[:, CHUNKS:2 * CHUNKS].bitcast(I32)
        hi_i = S1[:, 2 * CHUNKS:3 * CHUNKS].bitcast(I32)
        lo_f = S1[:, 3 * CHUNKS:4 * CHUNKS]
        hi_f = S1[:, 4 * CHUNKS:5 * CHUNKS]
        lo_hot = [pw[:, s, 0:CH * P // 2].bitcast(BF16).rearrange("p (c n) -> p c n", c=CH) for s in range(2)]
        hi_hot = [rw[:, s, 0:CH * 16].bitcast(BF16).rearrange("p (c n) -> p c n", c=CH)[:, :, 0:TILES]
                  for s in range(2)]
        DEG_BANK = 7
        deg = sb("deg", [P, TILES])
        first_s = sb("first_s", [1, CHUNKS], I32)
        z = [sb(f"z{k}", [P, TILES]) for k in range(8)]
        We_f = sb("We_f", [K_ATTR, 2 * D])
        We_hi, We_mid, We_lo = (sb(f"We_{n}", [K_ATTR, 2 * D], BF16) for n in BIAS_PART)
        We_kv = sb("We_kv", [K_ATTR, 2 * D], BF16)
        ea_f = R2[:, 0:FLAT]
        ea_lo = R2[:, FLAT:FLAT + FLAT // 2].bitcast(BF16)
        ea_hi = C[:, 0:FLAT // 2].bitcast(BF16)
        ea_mid = A[:, 0:FLAT // 2].bitcast(BF16)
        ea_ones = den[:, :, :].rearrange("p s e -> p (s e)").bitcast(BF16)[:, 0:len(BIAS_PART) * EP // P]
        A_rows, S1_rows, C_rows = (x[:, :].rearrange("p (t d) -> p t d", d=D) for x in (A, S1, C))


        def edges_sync(sp, e):
            kind = KINDS[e]["kind"]
            if kind == "sum":
                turn(sp, "s.first_row")
            if kind in ("attn", "gat"):
                for b, (lo, hi) in enumerate(PARTS):
                    sp.wait_ge(moved[b], 16 * (hi - lo) * (2, 5, 7)[("e1", "e3", "e4").index(e)])
            turn(sp, f"{e}.edges" if kind != "sum" else "s.first_row")

            def body(x):
                g, r = x.g, x.r
                here = SEM[e, "loads_here", r]
                before = g - RING + 1
                if past(g, RING):
                    sp.wait_ge(SEM[e, "num" if kind == "sum" else "u"], before)
                    if kind in ("attn", "gat"):
                        sp.wait_ge(SEM[e, "one_hot"], before)
                sp.sem_inc(gate_sp, 1)
                to, from_ = {"sum": (flag_b[:, r, :], keep_d[bass.ds(g * GE, GE)]),
                             "soft": (flag_b[:, r, :], marks_d[bass.ds(g * (2 * GE) + GE, GE)])}.get(
                    kind, (marks_b[:, r, :], marks_d[bass.ds(g * (2 * GE), 2 * GE)]))
                sp.dma_start(to, from_.partition_broadcast(P)).then_inc(here, 16)
                if kind in ("attn", "gat"):
                    if past(g, RING):
                        sp.wait_ge(SEM[e, "q_ready"], before)
                    sp.sem_inc(gate_sp, 1)
                    _, firsts = nc.values_load_multi_w_load_instructions(
                        first_s[0:1, bass.ds(g * CH, CH)], engines=[mybir.EngineType.SP], min_val=0, max_val=NP - 1)
                    for j in range(CH):
                        sp.dma_start(win[:, r, j, :], window_d[e][bass.ds(firsts[j], P), :]).then_inc(here, 16)
                if kind == "soft":
                    if past(g, RING):
                        sp.wait_ge(SEM[e, "expanded"], before)
                    sp.sem_inc(gate_sp, 1)
                    sp.dma_start(ea[:, r, :].rearrange("p (c d) -> p c d", c=CH),
                                 t["ea128"][bass.ds(g * GE, GE), :].rearrange("(c p) d -> p c d", p=P)).then_inc(
                        here, 16)

            stream(sp, body)

        def spread(pool, e, name):
            for b, c, tiles in turns(pool, name):
                for i in range(tiles.start, tiles.stop):
                    pool.indirect_dma_start(window_d[e], bass.IndirectOffsetOnAxis(ap=slot[:, i:i + 1], axis=0),
                                            C_rows[:, i, :], None).then_inc(moved[b], 16)
            moves[0] += 1

        def gather_ends(pool, e):
            for s in range(2):
                pool.wait_ge(SEM[e, "stored", s], 16 * PAIRS)
            if e == "e0":
                pool.wait_ge(attr_saved, ATTR_SAVED)
            k = KINDS[e]["out"]
            for b, c, tiles in turns(pool, f"{e}.ends" if e != "e0" else "s.nrun"):
                for i in range(tiles.start, tiles.stop):
                    pool.indirect_dma_start(R[:, i, 0:k], None, out_d[e], bass.IndirectOffsetOnAxis(
                        ap=last[:, i:i + 1], axis=0)).then_inc(moved[b], 16)
            moves[0] += 1
            for b, (lo, hi) in enumerate(PARTS):
                pool.wait_ge(moved[b], 16 * (hi - lo) * moves[0])
                pool.sem_inc(part_done[b], 1)

        def edges_gpsimd(pool, e):
            k = KINDS[e]["row"]

            def body(x):
                g, s = x.g, x.s
                if past(g, RING):
                    pool.wait_ge(SEM[e, "expanded"], g - RING + 1)
                pool.wait_ge(SEM[e, "idx_here"], g + 1)
                pool.sem_inc(gate_pool, 1)
                for j in range(CH):
                    pool.indirect_dma_start(rows_in[:, x.r, j, 0:k], None, table_d[e], bass.IndirectOffsetOnAxis(
                        ap=idx[:, x.r, j:j + 1], axis=0)).then_inc(SEM[e, "rows_here", x.r], 16)

            stream(pool, body)

        def linear(pe, name, terms_):
            for b, c, tiles in turns(pe, name):
                for k, (lhsT, rhs) in enumerate(terms_):
                    mm = pe.matmul(PN[:, c], lhsT, rhs[:, c], start=k == 0, stop=k == len(terms_) - 1)
                mm.then_inc(part_done[b], 1)

        def row_linear(pe, name, xT, weight):
            for b, c, tiles in turns(pe, name):
                for i in range(tiles.start, tiles.stop):
                    mm = pe.matmul(PN[:, i * P:(i + 1) * P], xT[:, i * P:(i + 1) * P], weight, start=True, stop=True)
                mm.then_inc(part_done[b], 1)

        def rows_to_features(pe, name, R_):
            for b, c, tiles in turns(pe, name):
                for i in range(tiles.start, tiles.stop):
                    mm = pe.transpose(PN[:, i * P:(i + 1) * P], R_[:, i, :], w("ident"))
                mm.then_inc(part_done[b], 1)

        def features_to_rows(pe, name, x):
            rows_to_features(pe, name, x[:, :].rearrange("p (t d) -> p t d", d=P))

        def node_sums(pe, name, x, weight):
            for b, c, tiles in turns(pe, name):
                for k, i in enumerate(range(tiles.start, tiles.stop)):
                    mm = pe.matmul(PN[:, c.start + k:c.start + k + 1], x[:, i * P:(i + 1) * P], weight, start=True,
                                   stop=True)
                mm.then_inc(part_done[b], 1)

        def spread_nodes(pe, name, k):
            for b, c, tiles in turns(pe, name):
                for i in range(tiles.start, tiles.stop):
                    mm = pe.transpose(PN[:, i * P:(i + 1) * P], ns[:, k, i:i + 1].to_broadcast([P, P]), w("ident"))
                mm.then_inc(part_done[b], 1)

        def norm_tensor(pe, p, x, c, q):
            linear(pe, f"{p}.mean", [(w("avg"), x)])
            node_sums(pe, f"{p}.var", q, w("avg", 0, 1))
            spread_nodes(pe, f"{p}.spread", 1)

        def structure_tensor(pe):
            pe.wait_ge(loaded["weights"], LOADS["weights"])
            turn(pe, "s.before")
            pe.matmul(PM[0:GROUPS, 0:1], w("strict", 0, GROUPS, GROUPS), count_l[:, GE - 1:GE], start=True,
                      stop=True).then_inc(whole_done, 1)

        def counts_tensor(pe):
            turn(pe, "s.within")
            pe.matmul(PS[:, BANK:BANK + TILES], w("upper"), deg[:, :], start=True, stop=True).then_inc(whole_done, 1)
            pe.matmul(PS[:, 2 * BANK:2 * BANK + TILES], w("upper"), live[:, :], start=True, stop=True).then_inc(
                whole_done, 1)
            turn(pe, "s.total")
            pe.matmul(PS[:, 3 * BANK:3 * BANK + TILES], w("ones"), deg[:, :], start=True, stop=True).then_inc(
                whole_done, 1)
            pe.matmul(PS[:, 4 * BANK:4 * BANK + TILES], w("ones"), live[:, :], start=True, stop=True).then_inc(
                whole_done, 1)
            turn(pe, "g.comp")
            for n, g in enumerate(("g1T", "g2T")):
                mm = pe.matmul(PM[:, n * 2 * HEADS3:(n + 1) * 2 * HEADS3], w(g), att[:, n, :], start=True, stop=True)
            mm.then_inc(whole_done, 1)

        def edges_tensor(pe, e):
            kind = KINDS[e]["kind"]
            turn(pe, f"{e}.edges")

            def sources(x):
                g, s, u = x.g, x.s, x.u
                pe.wait_ge(SEM[e, "rows_here", x.r], 16 * CH * (x.v + 1))
                if past(g, 2):
                    pe.wait_ge(SEM[e, "num" if kind == "sum" else "scored"], g - 1)
                V = bank(V_BANK + s)
                if kind == "sum":
                    for j in range(CH):
                        mm = pe.transpose(V[:, j * P:(j + 1) * P], rows_in[:, x.r, j, 0:D], w("ident"))
                else:
                    pe.wait_ge(SEM[e, "loads_here", x.r], 16 * LOADS_OF[kind] * (x.v + 1))
                    for j in range(CH):
                        o = V[:, j * P:(j + 1) * P]
                        pe.matmul(o, rows_in[:, x.r, j, 0:D], w("ident"), start=True, stop=False, is_transpose=True)
                        mm = pe.matmul(o, ea[:, x.r, j * P:(j + 1) * P], w("ident"), start=False, stop=True)
                mm.then_inc(SEM[e, "expanded"], 1)

            def queries(x):
                g, s, u = x.g, x.s, x.u
                pe.wait_ge(SEM[e, "loads_here", x.r], 16 * LOADS_OF[kind] * (x.v + 1))
                pe.wait_ge(SEM[e, "one_hot"], g + 1)
                if past(g, 1):
                    pe.wait_ge(SEM[e, "q_copied"], g)
                for j in range(CH):
                    mm = pe.matmul(bank(Q_BANK)[:, j * P:(j + 1) * P], win[:, x.r, j, :],
                                   one_hot[:, s, j * P:(j + 1) * P], start=True, stop=True)
                mm.then_inc(SEM[e, "q_ready"], 1)

            def with_attributes(out, x, at):
                for j in range(CH):
                    o = out[:, j * P:(j + 1) * P]
                    pe.matmul(o, rows_in[:, x.r, j, at:at + D], w("ident"), start=True, stop=False, is_transpose=True)
                    mm = pe.matmul(o, We_kv[:, at:at + D], ea_parts[:, x.r, j * P:(j + 1) * P], start=False,
                                   stop=True)
                return mm

            def keys(x):
                g, s, u = x.g, x.s, x.u
                pe.wait_ge(SEM[e, "rows_here", x.r], 16 * CH * (x.v + 1))
                if kind == "attn" and past(g, 2):
                    pe.wait_ge(SEM[e, "product"], g - 1)
                if kind == "gat" and past(g, 1):
                    pe.wait_ge(SEM[e, "scored"], g)
                K = bank(K_BANKS[kind][x.s])
                if kind == "attn":
                    pe.wait_ge(SEM[e, "attr_here", x.r], 16 * (x.v + 1))
                    with_attributes(K, x, 0).then_inc(SEM[e, "k_ready"], 1)
                    return
                pe.wait_ge(SEM[e, "loads_here", x.r], 16 * LOADS_OF[kind] * (x.v + 1))
                pe.wait_ge(SEM[e, "one_hot"], g + 1)
                for j in range(CH):
                    o = K[:, j * P:(j + 1) * P]
                    pe.matmul(o, rows_in[:, x.r, j, D:2 * D], w("ident"), start=True, stop=False, is_transpose=True)
                    mm = pe.matmul(o, win[:, x.r, j, :], one_hot[:, s, j * P:(j + 1) * P], start=False, stop=True)
                mm.then_inc(SEM[e, "q_ready"], 1)

            def values(x):
                g, s = x.g, x.s
                if past(g, 2):
                    pe.wait_ge(SEM[e, "pv"], g - 1)
                V = bank(V_BANK + s)
                if kind == "attn":
                    mm = with_attributes(V, x, D)
                else:
                    for j in range(CH):
                        mm = pe.transpose(V[:, j * P:(j + 1) * P], rows_in[:, x.r, j, 0:D], w("ident"))
                mm.then_inc(SEM[e, "expanded"], 1)

            def heads(x):
                g = x.g
                pe.wait_ge(SEM[e, "product"], g + 1)
                if past(g, 1):
                    pe.wait_ge(SEM[e, "x"], g)
                pe.matmul(bank(A_BANK), w("heads8"), prod[:, :], start=True, stop=True).then_inc(SEM[e, "scored"], 1)

            def turn_back(x):
                g, s = x.g, x.s
                pe.wait_ge(SEM[e, "num"], g + 1)
                if kind != "sum":
                    pe.wait_ge(SEM[e, "den"], g + 1)
                if past(g, 1):
                    pe.wait_ge(SEM[e, "evac"], 2 * g if kind != "sum" else g)
                back = [num[:, s, :]] + ([den[:, s, :]] if kind != "sum" else [])
                mm = transposes(OUT_BANK[kind], back)
                mm.then_inc(SEM[e, "turned"], 1)

            def transposes(first_bank, xs):
                for k, x in enumerate(xs):
                    for j in range(CH):
                        mm = pe.transpose(bank(first_bank + k)[:, j * P:(j + 1) * P], x[:, j * P:(j + 1) * P],
                                          w("ident"))
                return mm

            def turn_max(x):
                g, s, u = x.g, x.s, x.u
                pe.wait_ge(SEM[e, "scored"], g + 1)
                pe.wait_ge(SEM[e, "u"], g + 1)
                if past(g, 1):
                    pe.wait_ge(SEM[e, "max_evac"], g)
                transposes(MAX_BANK, [U[:, s, 0:GE], score[:, s, :]]).then_inc(SEM[e, "max_turned"], 1)

            if kind == "attn":
                queries(Group(0))
                keys(Group(0))
                heads(Group(0))
                values(Group(0))
                keys(Group(1))
                queries(Group(1))
            elif kind == "gat":
                keys(Group(0))
                values(Group(0))
            else:
                sources(Group(0))

            def body(x):
                g, s = x.g, x.s
                more = below(g, GROUPS - 1)
                if kind == "attn":
                    if below(g, GROUPS - 2):
                        queries(x.by(2))
                        keys(x.by(2))
                    if more:
                        heads(x.by(1))
                        values(x.by(1))
                if kind == "gat" and more:
                    keys(x.by(1))
                if kind == "gat" and past(g, 1):
                    turn_max(x.by(-1))
                if kind == "gat" and more:
                    values(x.by(1))
                if kind in ("sum", "soft") and more:
                    sources(x.by(1))
                if kind != "sum" and past(g, 2):
                    turn_back(x.by(-2))
                if kind == "sum" and past(g, 1):
                    turn_back(x.by(-1))
                if kind == "sum":
                    pe.wait_ge(deg_hot, g + 1)
                    for j in range(CH):
                        mm = pe.matmul(bank(DEG_BANK, TILES), lo_hot[s][:, j, :], hi_hot[s][:, j, :],
                                       start=not past(g, 1) and j == 0,
                                       stop=isinstance(g, int) and g == GROUPS - 1 and j == CH - 1,
                                       skip_group_check=True)
                    mm.then_inc(deg_mm, 1)

            stream(pe, body)
            if kind == "gat":
                turn_max(Group(GROUPS - 1))
            if kind != "sum":
                turn_back(Group(GROUPS - 2))
            turn_back(Group(GROUPS - 1))

        def norm_vector(dve, p, x, c, out):
            for b, n, _ in turns(dve, f"{p}.center"):
                nc.vector.tensor_tensor(c[:, n], x[:, n], PN[:, n], ALU.subtract).then_inc(part_done[b], 1)
            for b, _, tiles in turns(dve, f"{p}.inv"):
                nc.vector.reciprocal(ns[:, 1, tiles], ns[:, 0, tiles]).then_inc(part_done[b], 1)
            for b, n, _ in turns(dve, f"{p}.scale"):
                nc.vector.tensor_tensor(out[:, n], c[:, n], PN[:, n], ALU.mult).then_inc(part_done[b], 1)

        def structure_vector(dve):
            def step(name):
                turn(dve, name)
                return nc.vector

            nc.vector.memset(eps[:, :], 1e-5)
            nc.vector.memset(one_l, 1.0)
            nc.vector.memset(ea_ones, 1.0).then_inc(split_done, 1)
            dve.wait_ge(loaded["src"], LOADS["src"])
            for s in range(RING - 1):
                nc.vector.tensor_copy(idx[:, s, :], src[:, s * CH:(s + 1) * CH]).then_inc(SEM["e0", "idx_here"], 1)
            dve.wait_ge(loaded["dst"], LOADS["dst"])
            step("s.start").tensor_tensor(start_l, dst_line[1], dst_line[0], ALU.not_equal).then_inc(whole_done, 1)
            step("s.keep").tensor_tensor(keep_l, dst_line[1], dst_line[0], ALU.is_equal).then_inc(whole_done, 1)
            step("s.next").tensor_tensor(next_l, dst_line[1], dst_line[2], ALU.not_equal).then_inc(whole_done, 1)
            step("s.reset").tensor_scalar(reset_l, next_l, LOW, None, ALU.mult).then_inc(whole_done, 1)
            step("s.count").tensor_tensor_scan(count_l, one_l, start_l, 0.0, ALU.mult, ALU.add).then_inc(
                whole_done, 1)
            step("s.rho").tensor_scalar(rho_l, count_l, PM[0:L, 0:1], -1.0, ALU.add, ALU.add).then_inc(whole_done, 1)
            rho_c = rho_l.rearrange("p (c e) -> p c e", c=CH)
            step("s.first").tensor_copy(first_l, rho_c[:, :, 0]).then_inc(whole_done, 1)
            step("s.rank").tensor_tensor(rank_l.rearrange("p (c e) -> p c e", c=CH), rho_c,
                                         rho_c[:, :, 0:1].to_broadcast([L, CH, P]), ALU.subtract).then_inc(
                whole_done, 1)
            step("s.lo").tensor_scalar(lo_i, dst_col, P - 1, None, ALU.bitwise_and).then_inc(whole_done, 1)
            step("s.hi").tensor_scalar(hi_i, dst_col, 7, None, ALU.logical_shift_right).then_inc(whole_done, 1)
            step("s.lof").tensor_copy(lo_f, lo_i).then_inc(whole_done, 1)
            step("s.hif").tensor_copy(hi_f, hi_i).then_inc(whole_done, 1)

        def weights_vector(dve):
            def step(name):
                turn(dve, name)
                return nc.vector

            step("mean").tensor_reduce(col[:, 0:1], X[:, 0:NODES], AX, ALU.add).then_inc(whole_done, 1)
            step("mean2").tensor_scalar(col[:, 1:2], col[:, 0:1], 1.0 / NODES, None, ALU.mult).then_inc(
                whole_done, 1)
            step("gb").tensor_tensor(col[:, 2:4], w("b_ih", 0, 2), w("b_hh", 0, 2), ALU.add).then_inc(whole_done, 1)
            turn(dve, "a.wb")
            nc.vector.tensor_tensor(beta_sum[:, 0:1], w("beta", 0, 1), w("beta", 2, 1), ALU.add).then_inc(
                whole_done, 1)
            nc.vector.tensor_tensor(beta_sum[:, 1:2], w("beta", 1, 1), w("beta", 2, 1), ALU.subtract).then_inc(
                whole_done, 1)
            dve.wait_ge(whole_done, WHOLE_BEFORE["a.wb"] + 2)
            for n in range(2):
                nc.vector.tensor_scalar(gate_w[:, n, :], w("ones"), beta_sum[:, n:n + 1], None, ALU.mult).then_inc(
                    whole_done, 1)
            turn(dve, "g.att")
            for n in range(2):
                for k, a in enumerate((f"att_s{n + 1}", f"att_d{n + 1}")):
                    nc.vector.tensor_scalar(att[:, n, k * HEADS3:(k + 1) * HEADS3], w("head2"), w(a), None,
                                            ALU.mult).then_inc(whole_done, 1)
            step("g.comp_out").tensor_copy(comp[:, :, :], PM[:, 0:4 * HEADS3].rearrange(
                "p (n k) -> p n k", n=2)).then_inc(whole_done, 1)
            step("w.hi").tensor_copy(We_hi[:, :], We_f[:, :]).then_inc(whole_done, 1)
            step("w.rest").tensor_tensor(We_f[:, :], We_f[:, :], We_hi[:, :], ALU.subtract).then_inc(whole_done, 1)
            step("w.mid").tensor_copy(We_mid[:, :], We_f[:, :]).then_inc(whole_done, 1)
            step("w.rest2").tensor_tensor(We_f[:, :], We_f[:, :], We_mid[:, :], ALU.subtract).then_inc(whole_done, 1)
            step("w.lo").tensor_copy(We_lo[:, :], We_f[:, :]).then_inc(whole_done, 1)
            step("w.a").tensor_scalar(We_f[:, :], We_hi[:, :], w("we_part", 0, 1, K_ATTR), None, ALU.mult).then_inc(
                whole_done, 1)
            step("w.b").scalar_tensor_tensor(We_f[:, :], We_mid[:, :], w("we_part", 1, 1, K_ATTR), We_f[:, :],
                                             ALU.mult, ALU.add).then_inc(whole_done, 1)
            step("w.c").scalar_tensor_tensor(We_kv[:, :], We_lo[:, :], w("we_part", 2, 1, K_ATTR), We_f[:, :],
                                             ALU.mult, ALU.add).then_inc(whole_done, 1)
            turn(dve, "g.bias")
            for n in range(2):
                nc.vector.tensor_tensor(gat_bias[:, n:n + 1], w(f"g{n + 1}b"), w(f"g{n + 1}sb"), ALU.add).then_inc(
                    whole_done, 1)

        def counts_vector(dve):
            def step(name):
                turn(dve, name)
                return nc.vector

            dve.wait_ge(deg_mm, GROUPS)
            step("s.deg_out").tensor_copy(deg[:, :], bank(DEG_BANK, TILES)).then_inc(whole_done, 1)
            step("s.live").tensor_scalar(live[:, :], deg[:, :], 0.0, None, ALU.is_gt).then_inc(whole_done, 1)
            ones = w("ones", 0, TILES)
            step("s.total_out").tensor_copy(z[0][:, :], PS[:, 3 * BANK:3 * BANK + TILES]).then_inc(whole_done, 1)
            step("s.run").tensor_tensor_scan(z[1][:, :], ones, z[0][:, :], 0.0, ALU.mult, ALU.add).then_inc(
                whole_done, 1)
            step("s.end").tensor_tensor(z[2][:, :], z[1][:, :], z[0][:, :], ALU.subtract).then_inc(whole_done, 1)
            step("s.end2").scalar_tensor_tensor(z[3][:, :], PS[:, BANK:BANK + TILES], -1.0, z[2][:, :], ALU.add,
                                                ALU.add).then_inc(whole_done, 1)
            step("s.end3").tensor_scalar(last[:, :], z[3][:, :], 0.0, None, ALU.max).then_inc(whole_done, 1)
            step("s.nrun").tensor_copy(z[4][:, :], PS[:, 4 * BANK:4 * BANK + TILES]).then_inc(whole_done, 1)
            step("s.nlive").tensor_tensor_scan(z[5][:, :], ones, z[4][:, :], 0.0, ALU.mult, ALU.add).then_inc(
                whole_done, 1)
            step("s.nlive2").tensor_tensor(z[6][:, :], z[5][:, :], z[4][:, :], ALU.subtract).then_inc(whole_done, 1)
            step("s.nlive3").tensor_tensor(z[7][:, :], PS[:, 2 * BANK:2 * BANK + TILES], z[6][:, :],
                                           ALU.add).then_inc(whole_done, 1)
            step("s.empty").tensor_tensor(z[6][:, :], z[7][:, :], live[:, :], ALU.subtract).then_inc(whole_done, 1)
            step("s.empty2").scalar_tensor_tensor(z[7][:, :], w("node"), z[5][:, TILES - 1:TILES], z[6][:, :],
                                                  ALU.add, ALU.subtract).then_inc(whole_done, 1)
            step("s.slot").tensor_tensor(z[6][:, :], z[6][:, :], z[7][:, :], ALU.subtract).then_inc(whole_done, 1)
            step("s.slot2").tensor_tensor(z[6][:, :], z[6][:, :], live[:, :], ALU.mult).then_inc(whole_done, 1)
            step("s.slot3").tensor_tensor(slot[:, :], z[6][:, :], z[7][:, :], ALU.add).then_inc(whole_done, 1)

        def edges_vector(dve, e):
            kind = KINDS[e]["kind"]
            turn(dve, f"{e}.edges")

            def copy_idx(x):
                g, s, u = x.g, x.s, x.u
                if past(g, RING):
                    dve.wait_ge(SEM[e, "rows_here", x.r], 16 * CH * x.v)
                nc.vector.tensor_copy(idx[:, x.r, :], src[:, bass.ds(g * CH, CH)]).then_inc(SEM[e, "idx_here"], 1)

            def sums(x):
                g, s, u = x.g, x.s, x.u
                dve.wait_ge(SEM[e, "expanded"], g + 1)
                dve.wait_ge(SEM[e, "loads_here", x.r], 16 * LOADS_OF[kind] * (x.v + 1))
                if past(g, 1):
                    dve.wait_ge(SEM[e, "num"], g)
                if past(g, 2):
                    dve.wait_ge(SEM[e, "turned"], g - 1)
                init = num[:, 1 - s, GE - 1:GE] if past(g, 1) else 0.0
                nc.vector.tensor_tensor_scan(num[:, s, :], flag_b[:, x.r, :], bank(V_BANK + s), init, ALU.mult,
                                             ALU.add).then_inc(SEM[e, "num"], 1)

            def hot(x):
                g, s, u = x.g, x.s, x.u
                dve.wait_ge(SEM[e, "loads_here", x.r], 16 * LOADS_OF[kind] * (x.v + 1))
                if past(g, 2):
                    dve.wait_ge(SEM[e, "q_ready"], g - 1)
                nc.vector.tensor_scalar(one_hot[:, s, :], rank_b[:, x.r, :], w("part"), None, ALU.is_equal).then_inc(
                    SEM[e, "one_hot"], 1)

            def product(x):
                g, s = x.g, x.s
                dve.wait_ge(SEM[e, "q_copied"], g + 1)
                dve.wait_ge(SEM[e, "k_ready"], g + 1)
                if past(g, 1):
                    dve.wait_ge(SEM[e, "scored"], g)
                nc.vector.tensor_tensor(prod[:, :], bank(K_BANKS[kind][s]), qx[:, s, :], ALU.mult).then_inc(
                    SEM[e, "product"], 1)

            def messages(x):
                g, s = x.g, x.s
                dve.wait_ge(SEM[e, "expanded"], g + 1)
                if past(g, 2):
                    dve.wait_ge(SEM[e, "x"], g - 1)
                    dve.wait_ge(SEM[e, "pv"], g - 1)
                nc.vector.tensor_scalar(score[:, s, :], bank(V_BANK + s), 0.0, 1e-7, ALU.max, ALU.add).then_inc(
                    SEM[e, "scored"], 1)

            def leaky(x):
                g, s = x.g, x.s
                dve.wait_ge(SEM[e, "q_ready"], g + 1)
                if past(g, 2):
                    dve.wait_ge(SEM[e, "max_turned"], g - 1)
                dve.wait_ge(SEM[e, "q_copied"], g + 1)
                nc.vector.tensor_tensor(score[:, s, :], bank(K_BANKS[kind][s]), qx[:, s, :], ALU.max).then_inc(
                    SEM[e, "scored"], 1)

            def running_max(x):
                g, s, u = x.g, x.s, x.u
                dve.wait_ge(SEM[e, "scored"], g + 1)
                dve.wait_ge(SEM[e, "loads_here", x.r], 16 * LOADS_OF[kind] * (x.v + 1))
                a = bank(A_BANK) if kind == "attn" else score[:, s, :]
                if past(g, 1):
                    dve.wait_ge(SEM[e, "u"], g)
                    dve.wait_ge(SEM[e, "x"], g)
                if past(g, 2):
                    if kind == "gat":
                        dve.wait_ge(SEM[e, "max_turned"], g - 1)
                if past(g, 1):
                    nc.vector.tensor_copy(U[:, s, 0:1], U[:, 1 - s, GE:GE + 1]).then_inc(SEM[e, "u_head"], 1)
                else:
                    nc.vector.memset(U[:, s, 0:1], LOW).then_inc(SEM[e, "u_head"], 1)
                init = U[:, 1 - s, GE:GE + 1] if past(g, 1) else LOW
                nc.vector.tensor_tensor_scan(U[:, s, 1:GE + 1], a, flag_b[:, x.r, :], init, ALU.max,
                                             ALU.add).then_inc(SEM[e, "u"], 1)
                dve.wait_ge(SEM[e, "u_head"], g + 1)
                dve.wait_ge(SEM[e, "u"], g + 1)
                if past(g, 2):
                    dve.wait_ge(SEM[e, "clipped"], 2 * (g - 1))
                nc.vector.tensor_tensor(xd[:, s, :], U[:, s, 0:GE], a, ALU.subtract).then_inc(SEM[e, "x"], 1)

            def softmax_sums(x):
                g, s = x.g, x.s
                dve.wait_ge(SEM[e, "weights"], 2 * g + 1)
                dve.wait_ge(SEM[e, "scored" if kind == "soft" else "expanded"], g + 1)
                if past(g, 1):
                    dve.wait_ge(SEM[e, "num"], g)
                value = score[:, s, :] if kind == "soft" else bank(V_BANK + s)
                nc.vector.tensor_tensor(pv[:, :], value, pw[:, s, :], ALU.mult).then_inc(SEM[e, "pv"], 1)
                dve.wait_ge(SEM[e, "weights"], 2 * g + 2)
                if past(g, 1):
                    dve.wait_ge(SEM[e, "den"], g)
                if past(g, 2):
                    dve.wait_ge(SEM[e, "turned"], g - 1)
                for out, x, n in ((den, pw[:, s, :], "den"), (num, pv[:, :], "num")):
                    init = out[:, 1 - s, GE - 1:GE] if past(g, 1) else 0.0
                    if n == "num":
                        dve.wait_ge(SEM[e, "pv"], g + 1)
                    nc.vector.tensor_tensor_scan(out[:, s, :], rw[:, s, :], x, init, ALU.mult, ALU.add).then_inc(
                        SEM[e, n], 1)

            def degrees(g, s):
                if past(g, 2):
                    dve.wait_ge(deg_mm, g - 1)
                for hot_, n, x in ((lo_hot, P, lo_f), (hi_hot, TILES, hi_f)):
                    op = nc.vector.tensor_tensor(
                        hot_[s], w("iota", 0, n).rearrange("p (o n) -> p o n", o=1).to_broadcast([P, CH, n]),
                        x[:, bass.ds(g * CH, CH)].rearrange("p (c o) -> p c o", o=1).to_broadcast([P, CH, n]),
                        ALU.is_equal)
                op.then_inc(deg_hot, 1)

            if kind != "sum":
                for g in range(RING - 1):
                    copy_idx(Group(g))
            if kind in ("attn", "gat"):
                hot(Group(0))
                hot(Group(1))
            if kind == "attn":
                hot(Group(2))
                product(Group(0))

            def body(x):
                g, s, u = x.g, x.s, x.u
                if below(g, GROUPS - RING + 1):
                    copy_idx(x.by(RING - 1))
                if kind == "sum":
                    sums(x)
                    degrees(g, s)
                    if not past(g, 4) and g in (2, 3):
                        dve.wait_ge(split_done, 2 * (g - 1))
                        nc.vector.tensor_tensor(ea_f, ea_f, (ea_hi, ea_mid)[g - 2], ALU.subtract).then_inc(
                            split_done, 1)
                    return
                if kind == "soft":
                    messages(x)
                if kind == "gat":
                    leaky(x)
                running_max(x)
                if kind == "attn" and below(g, GROUPS - 1):
                    product(x.by(1))
                if past(g, 1):
                    softmax_sums(x.by(-1))
                if kind == "gat" and below(g, GROUPS - 2):
                    hot(x.by(2))
                if kind == "attn" and below(g, GROUPS - 3):
                    hot(x.by(3))

            stream(dve, body)
            if kind != "sum":
                softmax_sums(Group(GROUPS - 1))

        def edges_scalar(act, e):
            kind = KINDS[e]["kind"]
            k = KINDS[e]["out"]
            turn(act, f"{e}.edges")

            def copy_q(x):
                g, s = x.g, x.s
                act.wait_ge(SEM[e, "q_ready"], g + 1)
                if past(g, 2):
                    act.wait_ge(SEM[e, "product" if kind == "attn" else "scored"], g - 1)
                if kind == "attn":
                    nc.scalar.activation(qx[:, s, :], bank(Q_BANK), ACT.Identity, bias=w("bq")).then_inc(
                        SEM[e, "q_copied"], 1)
                else:
                    nc.scalar.activation(qx[:, s, :], bank(K_BANKS[kind][s]), ACT.Copy, scale=0.2).then_inc(
                        SEM[e, "q_copied"], 1)

            def weights(x):
                g, s = x.g, x.s
                act.wait_ge(SEM[e, "x"], g + 1)
                if past(g, 2):
                    act.wait_ge(SEM[e, "num"], g - 1)
                    act.wait_ge(SEM[e, "den"], g - 1)
                for n, (out, sign) in enumerate(((pw, 1.0), (rw, -1.0))):
                    if past(g, 1):
                        act.wait_ge(SEM[e, "weights"], 2 * g)
                    nc.scalar.activation(clip[:, n, :], xd[:, s, :], ACT.Relu, scale=sign).then_inc(
                        SEM[e, "clipped"], 1)
                    act.wait_ge(SEM[e, "clipped"], 2 * g + n + 1)
                    nc.scalar.activation(out[:, s, :], clip[:, n, :], ACT.Exp, scale=-1.0).then_inc(
                        SEM[e, "weights"], 1)

            def max_out(x):
                g, s, u = x.g, x.s, x.u
                act.wait_ge(SEM[e, "max_turned"], g + 1)
                if past(g, 2):
                    act.wait_ge(SEM[e, "stored", s], 16 * u)
                small = PS[:, MAX_BANK * BANK:(MAX_BANK + 2) * BANK].rearrange(
                    "p (k c h x) -> p k c h x", k=2, c=CH, h=HEADS3)[:, :, :, :, 0]
                nc.scalar.activation(rows_out[:, s, :, D + HEADS3:k].rearrange("p c (k h) -> p k c h", k=2), small,
                                     ACT.Copy).then_inc(SEM[e, "max_evac"], 1)

            def store(x):
                g, s, u = x.g, x.s, x.u
                act.wait_ge(SEM[e, "turned"], g + 1)
                if past(g, 2):
                    act.wait_ge(SEM[e, "stored", s], 16 * u)
                b = OUT_BANK[kind]
                nc.scalar.activation(rows_out[:, s, :, 0:D], bank(b).rearrange("p (c d) -> p c d", d=D),
                                     ACT.Copy).then_inc(SEM[e, "evac"], 1)
                n = 1 if kind == "sum" else 2
                if kind != "sum":
                    h = {"attn": HEADS1, "soft": D, "gat": HEADS3}[kind]
                    small = bank(b + 1).rearrange("p (c h x) -> p c h x", c=CH, h=h)[:, :, :, 0]
                    nc.scalar.activation(rows_out[:, s, :, D:D + h], small, ACT.Copy).then_inc(SEM[e, "evac"], 1)
                act.wait_ge(SEM[e, "evac"], n * (g + 1))
                if kind == "gat":
                    act.wait_ge(SEM[e, "max_evac"], g + 1)
                act.dma_start(out_d[e][bass.ds(g * GE, GE), :].rearrange("(c p) d -> p c d", p=P),
                              rows_out[:, s, :, 0:k]).then_inc(SEM[e, "stored", s], 16)

            def attribute_part(n):
                if n is None:
                    act.dma_start(ea_f, t["ea10"]).then_inc(loaded["attributes"], 16)
                    return
                if n == 0:
                    act.wait_ge(loaded["attributes"], LOADS["attributes"])
                act.wait_ge(split_done, 1 + 2 * n)
                if n == 0:
                    act.dma_start(attr_d[len(ATTR_PART) * EDGE_D:K_ATTR, :].rearrange("d e -> (d e)").rearrange(
                        "(p n) -> p n", p=P), ea_ones).then_inc(attr_saved, 16)
                name, x = (("hi", ea_hi), ("mid", ea_mid), ("lo", ea_lo))[n]
                nc.scalar.activation(x, ea_f, ACT.Copy).then_inc(split_done, 1)
                act.wait_ge(split_done, 2 + 2 * n)
                for k, p in enumerate(ATTR_PART):
                    if p == name:
                        act.dma_start(attr_d[k * EDGE_D:(k + 1) * EDGE_D, :].rearrange(
                            "d e -> (d e)").rearrange("(p n) -> p n", p=P), x).then_inc(attr_saved, 16)

            def load_attributes(x):
                if past(x.g, RING):
                    act.wait_ge(SEM[e, "expanded"], x.g - RING + 1)
                    act.sem_inc(gate_act, 1)
                act.dma_start(ea_parts[:, x.r, :], attr_d[:, bass.ds(x.g * GE, GE)]).then_inc(
                    SEM[e, "attr_here", x.r], 16)

            def body(x):
                g, s, u = x.g, x.s, x.u
                if kind == "gat" and below(g, GROUPS - 1):
                    copy_q(x.by(1))
                if kind == "attn" and below(g, GROUPS - 2):
                    copy_q(x.by(2))
                if kind != "sum":
                    weights(x)
                if kind == "gat" and past(g, 1):
                    max_out(x.by(-1))
                if past(g, 2):
                    store(x.by(-2))
                if kind == "attn" and below(g, GROUPS - RING):
                    load_attributes(x.by(RING))
                if kind == "sum" and not past(g, 4):
                    attribute_part((None, 0, 1, 2)[g])

            if kind == "attn":
                act.wait_ge(attr_saved, ATTR_SAVED)
                for g in range(RING):
                    load_attributes(Group(g))
            if kind in ("attn", "gat"):
                copy_q(Group(0))
            if kind == "attn":
                copy_q(Group(1))
            stream(act, body)
            if kind == "gat":
                max_out(Group(GROUPS - 1))
            store(Group(GROUPS - 2))
            store(Group(GROUPS - 1))

        block = ctx.enter_context(nc.Block())

        @block.sync
        def _(sp):
            sp.dma_start(src[:, :], t["src"]).then_inc(loaded["src"], 16)
            for n in range(3):
                sp.dma_start(dst_line[n], t["dst_line"][n:n + EP].rearrange("(g e) -> g e", e=GE)).then_inc(
                    loaded["dst"], 16)
            sp.dma_start(dst_col, t["dst_col"]).then_inc(loaded["dst"], 16)
            sp.dma_start(W[:, :], t["weights"]).then_inc(loaded["weights"], 16)
            sp.dma_start(X[:, :], t["xT"]).then_inc(loaded["weights"], 16)
            sp.dma_start(We_f[:, :], t["We"]).then_inc(loaded["weights"], 16)
            for e in ("e1", "e3", "e4"):
                sp.dma_start(window_d[e][NP:NP + P, :], t["zero"]).then_inc(loaded["weights"], 16)
            turn(sp, "s.save")
            sp.dma_start(marks_d.rearrange("(g e) -> g e", e=2 * GE), marks_l[:, :]).then_inc(whole_done, 16)
            sp.dma_start(keep_d.rearrange("(g e) -> g e", e=GE), keep_l[:, :]).then_inc(whole_done, 16)
            sp.dma_start(first_d.rearrange("a (g c) -> (a g) c", c=CH), first_l[:, :]).then_inc(whole_done, 16)
            turn(sp, "s.first_row")
            sp.dma_start(first_s[:, :], first_d).then_inc(whole_done, 16)
            edges_sync(sp, "e0")
            turn(sp, "s.live")
            with nc.allow_non_contiguous_dma(reason="3200 degrees, once"):
                sp.dma_start(deg_d.rearrange("(t p) -> p t", p=P), deg[:, :]).then_inc(degrees_here, 16)
            sp.wait_ge(degrees_here, 16)
            sp.wait_ge(attr_saved, ATTR_SAVED)
            sp.dma_start(C[:, :], deg_d.partition_broadcast(P)).then_inc(degrees_here, 16)

            def save_table(e, name):
                for b, _, tiles in turns(sp, name):
                    lo, hi = tiles.start * P, tiles.stop * P
                    sp.dma_start(table_d[e][lo:hi, :].rearrange("(t p) d -> p t d", p=P),
                                 R[:, tiles, 0:KINDS[e]["row"]]).then_inc(table_saved, 16)

            save_table("e1", "kv_table")
            edges_sync(sp, "e1")
            save_table("e2", "x2_table")
            edges_sync(sp, "e2")
            for e in ("e3", "e4"):
                save_table(e, f"{e}.table")
                edges_sync(sp, e)
            for b, _, tiles in turns(sp, "y_save"):
                sp.dma_start(t["out"][tiles.start * P:tiles.stop * P, :].rearrange("(t p) d -> p t d", p=P),
                             R[:, tiles, 0:D]).then_inc(out_saved, 16)
            sp.wait_ge(out_saved, 16 * len(PARTS))

        @block.gpsimd
        def _(pool):
            for n, e in enumerate(KINDS):
                if e == "e1":
                    spread(pool, "e1", "q_spread")
                if e in ("e3", "e4"):
                    spread(pool, e, f"{e}.spread")
                if e != "e0":
                    turn(pool, f"{e}.edges")
                    pool.wait_ge(table_saved, TABLES * n)
                edges_gpsimd(pool, e)
                gather_ends(pool, e)

        @block.tensor
        def _(pe):
            structure_tensor(pe)
            edges_tensor(pe, "e0")
            counts_tensor(pe)
            rows_to_features(pe, "e0.turn", R[:, :, 0:D])
            linear(pe, "msg", [(w("w_msg"), A)])
            linear(pe, "r", [(w("w_ih", 0, D), S1), (w("w_hh", 0, D), X)])
            linear(pe, "z", [(w("w_ih", D, D), S1), (w("w_hh", D, D), X)])
            linear(pe, "hn", [(w("w_hh", 2 * D, D), X)])
            linear(pe, "in", [(w("w_ih", 2 * D, D), S1)])
            norm_tensor(pe, "ln0", B, S1, C)
            norm_tensor(pe, "n0", A, S1, C)
            row_linear(pe, "q", X, w("wq"))
            row_linear(pe, "k", X, w("wk"))
            row_linear(pe, "v", X, w("wv"))
            linear(pe, "skip", [(w("wskip"), X)])
            edges_tensor(pe, "e1")
            rows_to_features(pe, "a.turn", R[:, :, 0:D])
            linear(pe, "a.gate", [(gate_w[:, 0, :], A), (gate_w[:, 1, :], B)])
            for c in range(4):
                linear(pe, f"ffn{c}", [(w("ffn1", c * D, D), C)])
            linear(pe, "ffn", [(w("ffn2", c * D, D), G4[c]) for c in range(4)])
            norm_tensor(pe, "n1", A, S1, C)
            features_to_rows(pe, "x2", X)
            node_sums(pe, "c.nx", C, w("ones", 0, 1))
            edges_tensor(pe, "e2")
            rows_to_features(pe, "c.turn", R[:, :, 0:D])
            node_sums(pe, "c.na", B, w("ones", 0, 1))
            spread_nodes(pe, "c.spread", 4)
            linear(pe, "c.mlp", [(w("mlp"), A)])
            norm_tensor(pe, "n2", A, S1, C)
            for n, (e, x_in, g, gs) in enumerate((("e3", X, "g1", "g1s"), ("e4", B, "g2", "g2s"))):
                for b, _, tiles in turns(pe, f"{e}.terms"):
                    for i in range(tiles.start, tiles.stop):
                        mm = pe.matmul(PM[:, i * 2 * HEADS3:(i + 1) * 2 * HEADS3], x_in[:, i * P:(i + 1) * P],
                                       comp[:, n, :], start=True, stop=True)
                    mm.then_inc(part_done[b], 1)
                row_linear(pe, f"{e}.h", x_in, w(g))
                edges_tensor(pe, e)
                for b, _, tiles in turns(pe, f"{e}.sum"):
                    for i in range(tiles.start, tiles.stop):
                        o = PN[:, i * P:(i + 1) * P]
                        pe.matmul(o, w(gs), x_in[:, i * P:(i + 1) * P], start=True, stop=False)
                        mm = pe.matmul(o, R[:, i, 0:D], w("ident"), start=False, stop=True)
                    mm.then_inc(part_done[b], 1)
            norm_tensor(pe, "n3", A, S1, C)
            features_to_rows(pe, "y", X)

        @block.vector
        def _(dve):
            def two(name, out, x, y, op):
                for b, c, _ in turns(dve, name):
                    nc.vector.tensor_tensor(out[:, c], x[:, c], y[:, c], op).then_inc(part_done[b], 1)

            def live_rows(tiles, n):
                return live[:, tiles].rearrange("p (t o) -> p t o", o=1).to_broadcast([P, tiles.stop - tiles.start, n])

            def mask(name):
                for b, _, tiles in turns(dve, name):
                    nc.vector.tensor_tensor(R[:, tiles, 0:D], R[:, tiles, 0:D], live_rows(tiles, D),
                                            ALU.mult).then_inc(part_done[b], 1)

            def over_heads(name, rows_, k, heads):
                for b, _, tiles in turns(dve, name):
                    n = tiles.stop - tiles.start
                    x = rows_[:, tiles, 0:D].rearrange("p t (h c) -> p t h c", h=heads)
                    mul = s8[:, k, tiles, 0:heads].rearrange("p t (h o) -> p t h o", o=1).to_broadcast(
                        [P, n, heads, D // heads])
                    nc.vector.tensor_tensor(x, x, mul, ALU.mult).then_inc(part_done[b], 1)

            structure_vector(dve)
            edges_vector(dve, "e0")
            counts_vector(dve)
            weights_vector(dve)

            mask("e0.mask")
            dve.wait_ge(degrees_here, 32)
            for b, c, _ in turns(dve, "msg_out"):
                nc.vector.scalar_tensor_tensor(A[:, c], C[:, c], w("b_msg"), PN[:, c], ALU.mult, ALU.add).then_inc(
                    part_done[b], 1)
            for b, c, _ in turns(dve, "hn_out"):
                nc.vector.scalar_tensor_tensor(B[:, c], PN[:, c], w("b_hh", 2, 1), B[:, c], ALU.add,
                                               ALU.mult).then_inc(part_done[b], 1)
            two("in_out", B, PN, B, ALU.add)
            two("h1", S1, X, B, ALU.subtract)
            two("h2", S1, S1, C, ALU.mult)
            two("h3", B, S1, B, ALU.add)
            norm_vector(dve, "ln0", B, S1, B)
            two("y0b", A, A, B, ALU.add)
            two("y0c", A, A, X, ALU.add)
            norm_vector(dve, "n0", A, S1, X)
            for b, c, tiles in turns(dve, "k_row"):
                nc.vector.tensor_copy(R[:, tiles, 0:D], PN[:, c].rearrange("p (t d) -> p t d", d=D)).then_inc(
                    part_done[b], 1)

            edges_vector(dve, "e1")
            for b, _, tiles in turns(dve, "a.den"):
                nc.vector.tensor_scalar(s8[:, 0, tiles, :], R[:, tiles, D:D + HEADS1], 1e-16, None,
                                        ALU.add).then_inc(part_done[b], 1)
            for b, _, tiles in turns(dve, "a.rden"):
                nc.vector.reciprocal(s8[:, 1, tiles, :], s8[:, 0, tiles, :]).then_inc(part_done[b], 1)
            for b, _, tiles in turns(dve, "a.live"):
                nc.vector.tensor_tensor(s8[:, 0, tiles, :], s8[:, 1, tiles, :], live_rows(tiles, HEADS1),
                                        ALU.mult).then_inc(part_done[b], 1)
            over_heads("a.norm", R, 0, HEADS1)
            two("a.diff", C, A, B, ALU.subtract)
            two("a.mix", C, C, S1, ALU.mult)
            two("a.att", A, A, C, ALU.subtract)
            two("a.h", A, A, X, ALU.add)

            def sum_nodes(name, k, x):
                for b, c, _ in turns(dve, name):
                    nc.vector.tensor_reduce(part_sum[:, k, b:b + 1], x[:, c.start:min(c.stop, NODES)], AX,
                                            ALU.add).then_inc(part_done[b], 1)

            def step(name):
                turn(dve, name)
                return nc.vector

            sum_nodes("gn.sum", 0, A)
            step("gn.all").tensor_reduce(col[:, 4:5], part_sum[:, 0, :], AX, ALU.add).then_inc(whole_done, 1)
            step("gn.mean").tensor_scalar(col[:, 5:6], col[:, 4:5], 1.0 / NODES, w("gn_ms"), ALU.mult,
                                          ALU.mult).then_inc(whole_done, 1)
            for b, c, _ in turns(dve, "gn.center"):
                nc.vector.tensor_scalar(S1[:, c], A[:, c], col[:, 5:6], None, ALU.subtract).then_inc(part_done[b], 1)
            sum_nodes("gn.sqsum", 1, B)
            step("gn.var").tensor_reduce(col[:, 6:7], part_sum[:, 1, :], AX, ALU.add).then_inc(whole_done, 1)
            step("gn.inv").reciprocal(col[:, 8:9], col[:, 7:8]).then_inc(whole_done, 1)
            step("gn.gain").tensor_tensor(col[:, 9:10], col[:, 8:9], w("gn_w"), ALU.mult).then_inc(whole_done, 1)
            for b, c, _ in turns(dve, "gn.out"):
                nc.vector.tensor_scalar(C[:, c], S1[:, c], col[:, 9:10], w("gn_b"), ALU.mult, ALU.add).then_inc(
                    part_done[b], 1)
            for b, c, _ in turns(dve, "ffn_out"):
                nc.vector.scalar_tensor_tensor(A[:, c], PN[:, c], w("fb2"), C[:, c], ALU.add, ALU.add).then_inc(
                    part_done[b], 1)
            two("y1", A, A, X, ALU.add)
            norm_vector(dve, "n1", A, S1, X)

            edges_vector(dve, "e2")
            for b, _, tiles in turns(dve, "c.better"):
                nc.vector.tensor_tensor(A_rows[:, tiles, :], R[:, tiles, D:2 * D], S1_rows[:, tiles, :],
                                        ALU.mult).then_inc(part_done[b], 1)
            for b, _, tiles in turns(dve, "c.better2"):
                nc.vector.scalar_tensor_tensor(A_rows[:, tiles, :], A_rows[:, tiles, :], 2.0, S1_rows[:, tiles, :],
                                               ALU.subtract, ALU.mult).then_inc(part_done[b], 1)
            for b, _, tiles in turns(dve, "c.norm"):
                nc.vector.tensor_tensor(R[:, tiles, 0:D], R[:, tiles, 0:D], A_rows[:, tiles, :],
                                        ALU.mult).then_inc(part_done[b], 1)
            for b, _, tiles in turns(dve, "c.mask"):
                nc.vector.scalar_tensor_tensor(R[:, tiles, 0:D], R[:, tiles, 0:D], -1.0, live_rows(tiles, D),
                                               ALU.mult, ALU.mult).then_inc(part_done[b], 1)
            for b, _, tiles in turns(dve, "c.max"):
                nc.vector.tensor_scalar(ns[:, 2, tiles], ns[:, 2, tiles], 1e-12, None, ALU.max).then_inc(
                    part_done[b], 1)
            for b, _, tiles in turns(dve, "c.inv"):
                nc.vector.reciprocal(ns[:, 4, tiles], ns[:, 2, tiles]).then_inc(part_done[b], 1)
            for b, _, tiles in turns(dve, "c.ratio"):
                nc.vector.tensor_tensor(ns[:, 4, tiles], ns[:, 4, tiles], ns[:, 3, tiles], ALU.mult).then_inc(
                    part_done[b], 1)
            two("c.scaled", A, A, PN, ALU.mult)
            two("c.feat", A, A, X, ALU.add)
            for b, c, _ in turns(dve, "y2"):
                nc.vector.scalar_tensor_tensor(A[:, c], PN[:, c], w("mlp_b"), X[:, c], ALU.add, ALU.add).then_inc(
                    part_done[b], 1)
            norm_vector(dve, "n2", A, S1, X)

            H2 = HEADS3
            small = [s8[:, k, :, 0:H2] for k in range(8)]
            hrow = S1_rows
            for e in ("e3", "e4"):
                step(f"{e}.terms_out").tensor_copy(terms[:, :, :], PM[:, 0:TILES * 2 * H2].rearrange(
                    "p (t k) -> p t k", k=2 * H2)).then_inc(whole_done, 1)
                for name, out, at, k in (("ad_row", C_rows, 0, H2), ("as_row", R, D, 0)):
                    for b, _, tiles in turns(dve, f"{e}.{name}"):
                        n = tiles.stop - tiles.start
                        nc.vector.tensor_copy(
                            out[:, tiles, at:at + D].rearrange("p t (h c) -> p t h c", h=H2),
                            terms[:, tiles, k:k + H2].rearrange("p t (h o) -> p t h o", o=1).to_broadcast(
                                [P, n, H2, D // H2])).then_inc(part_done[b], 1)
                for b, c, _ in turns(dve, f"{e}.h_out"):
                    nc.vector.tensor_copy(S1[:, c], PN[:, c]).then_inc(part_done[b], 1)
                step(f"{e}.self_z").tensor_tensor(small[0], terms[:, :, 0:H2], terms[:, :, H2:], ALU.add).then_inc(
                    whole_done, 1)
                step(f"{e}.self").scalar_tensor_tensor(small[1], small[0], 0.2, small[0], ALU.mult,
                                                       ALU.max).then_inc(whole_done, 1)
                edges_vector(dve, e)
                dn, un, sn = (R[:, :, D + k * H2:D + (k + 1) * H2] for k in range(3))
                live2 = live_rows(slice(0, TILES), H2)
                step(f"{e}.m").tensor_tensor(small[2], un, sn, ALU.max).then_inc(whole_done, 1)
                step(f"{e}.m_live").tensor_tensor(small[3], small[2], live2, ALU.mult).then_inc(whole_done, 1)
                step(f"{e}.m_mask").tensor_scalar(small[4], live2, 1.0, -LOW, ALU.subtract, ALU.mult).then_inc(
                    whole_done, 1)
                step(f"{e}.m_all").tensor_tensor(small[2], small[3], small[4], ALU.add).then_inc(whole_done, 1)
                step(f"{e}.we_x").tensor_tensor(small[3], small[2], small[1], ALU.max).then_inc(whole_done, 1)
                turn(dve, f"{e}.ws_x")
                nc.vector.tensor_tensor(small[4], small[2], small[3], ALU.subtract)
                nc.vector.tensor_tensor(small[5], small[1], small[3], ALU.subtract).then_inc(whole_done, 1)
                step(f"{e}.we_live").tensor_tensor(small[3], small[6], live2, ALU.mult).then_inc(whole_done, 1)
                step(f"{e}.den").tensor_tensor(small[4], dn, small[3], ALU.mult).then_inc(whole_done, 1)
                step(f"{e}.den2").tensor_tensor(small[5], small[4], small[7], ALU.add).then_inc(whole_done, 1)
                step(f"{e}.den3").tensor_scalar(small[4], small[5], 1e-16, None, ALU.add).then_inc(whole_done, 1)
                step(f"{e}.rden").reciprocal(small[5], small[4]).then_inc(whole_done, 1)
                step(f"{e}.we_n").tensor_tensor(small[4], small[3], small[5], ALU.mult).then_inc(whole_done, 1)
                step(f"{e}.ws_n").tensor_tensor(small[6], small[7], small[5], ALU.mult).then_inc(whole_done, 1)
                over_heads(f"{e}.num", R, 4, H2)
                over_heads(f"{e}.hs", hrow, 6, H2)
                for b, _, tiles in turns(dve, f"{e}.agg"):
                    nc.vector.tensor_tensor(R[:, tiles, 0:D], R[:, tiles, 0:D], hrow[:, tiles, :],
                                            ALU.add).then_inc(part_done[b], 1)
                if e == "e4":
                    for b, c, _ in turns(dve, f"{e}.act"):
                        nc.vector.scalar_tensor_tensor(A[:, c], PN[:, c], gat_bias[:, 1:2], X[:, c], ALU.add,
                                                       ALU.add).then_inc(part_done[b], 1)
            norm_vector(dve, "n3", A, S1, X)

        @block.scalar
        def _(act):
            def one(name, out, x, func=ACT.Copy, **k):
                for b, c, _ in turns(act, name):
                    nc.scalar.activation(out[:, c], x[:, c], func, **k).then_inc(part_done[b], 1)

            def rows_of(name, out, at):
                for b, c, tiles in turns(act, name):
                    nc.scalar.activation(out[:, tiles, at:at + D], PN[:, c].rearrange("p (t d) -> p t d", d=D),
                                         ACT.Copy).then_inc(part_done[b], 1)

            def roots(name, k, **bias):
                for b, c, tiles in turns(act, name):
                    n = tiles.stop - tiles.start
                    nc.scalar.activation(ns[:, k, tiles], PN[:, c.start:c.start + n], ACT.Sqrt, **bias).then_inc(
                        part_done[b], 1)

            def norm_scalar(p, c, q):
                one(f"{p}.square", q, c, ACT.Square)
                roots(f"{p}.std", 0, bias=eps[:, 0:1])

            edges_scalar(act, "e0")
            one("e0.turned", A, PN)
            one("msg_mean", S1, A, ACT.Identity, bias=col[:, 1:2])
            one("r_out", B, PN, ACT.Sigmoid, bias=col[:, 2:3])
            one("z_out", C, PN, ACT.Sigmoid, bias=col[:, 3:4])
            one("n", B, B, ACT.Tanh, bias=w("b_ih", 2, 1))
            norm_scalar("ln0", S1, C)
            one("y0a", B, B, ACT.Identity, scale=w("gamma0"), bias=w("beta0"))
            norm_scalar("n0", S1, C)
            rows_of("q_row", C_rows, 0)
            rows_of("v_row", R, D)
            one("skip_out", B, PN, ACT.Identity, bias=w("bskip"))

            edges_scalar(act, "e1")
            one("a.turned", A, PN)
            one("a.gate_out", S1, PN, ACT.Sigmoid)
            one("gn.sq", B, S1, ACT.Square)
            turn(act, "gn.std")
            nc.scalar.activation(col[:, 7:8], col[:, 6:7], ACT.Sqrt, bias=eps[:, 0:1], scale=1.0 / NODES).then_inc(
                whole_done, 1)
            for c in range(4):
                one(f"ffn{c}_out", G4[c], PN, ACT.Gelu, bias=w("fb1", c, 1))
            norm_scalar("n1", S1, C)
            rows_of("x2_row", R, 0)
            one("c.sqx", C, X, ACT.Square)
            roots("c.rootx", 3)

            edges_scalar(act, "e2")
            for b, _, tiles in turns(act, "c.den2"):
                nc.scalar.activation(S1_rows[:, tiles, :], R[:, tiles, D:2 * D], ACT.Square).then_inc(
                    part_done[b], 1)
            one("c.rden", S1, S1, ACT.Abs_reciprocal_sqrt)
            one("c.turned", A, PN)
            one("c.sqa", B, A, ACT.Square)
            roots("c.roota", 2)
            norm_scalar("n2", S1, C)

            for e in ("e3", "e4"):
                rows_of(f"{e}.h_row", R, 0)
                edges_scalar(act, e)
                for name, to, x in (("we", 6, 4), ("ws", 7, 5)):
                    turn(act, f"{e}.{name}")
                    nc.scalar.activation(s8[:, to, :, 0:HEADS3], s8[:, x, :, 0:HEADS3], ACT.Exp).then_inc(
                        whole_done, 1)
                if e == "e3":
                    one(f"{e}.act", B, PN, ACT.Relu, bias=gat_bias[:, 0:1])
            norm_scalar("n3", S1, C)
            rows_of("y_row", R, 0)


def host_arrays(a):
    f = np.float32

    def padded(x, n):
        return np.concatenate([x, np.zeros((n - x.shape[0],) + x.shape[1:], x.dtype)])

    def fill(n, value):
        return np.full(n, value, np.int32)

    x = padded(a["x"], NP)
    dst = np.concatenate([a["dst"], fill(EP - EDGES, NP - 1)])
    k = np.arange(P)

    def same(heads):
        return (k[:, None] * heads // D == k[None, :] * heads // D).astype(f)

    parts = {
        "w_msg": a["L0_gnn_W_msg"].T, "w_ih": a["L0_gnn_w_ih"].T, "w_hh": a["L0_gnn_w_hh"].T,
        "wq": a["L1_gnn_Wq"], "wk": a["L1_gnn_Wk"], "wv": a["L1_gnn_Wv"], "wskip": a["L1_gnn_Wskip"],
        "ffn1": a["L1_gnn_W1"], "ffn2": a["L1_gnn_W2"].reshape(4, D, D).transpose(1, 0, 2).reshape(D, 4 * D),
        "mlp": a["L2_gnn_mlp_w"],
        "g1": a["L3_gnn_W1"], "g1s": a["L3_gnn_Wsk1"], "g1T": a["L3_gnn_W1"].T,
        "g2": a["L3_gnn_W2"], "g2s": a["L3_gnn_Wsk2"], "g2T": a["L3_gnn_W2"].T,
        "ident": np.eye(P, dtype=f), "ones": np.ones((P, P), f), "avg": np.full((P, P), 1.0 / D, f),
        "upper": np.triu(np.ones((P, P), f)), "strict": np.triu(np.ones((P, P), f), 1),
        "heads8": same(HEADS1) * f((D // HEADS1) ** -0.5),
        "head2": (k[:, None] * HEADS3 // D == np.arange(HEADS3)[None, :]).astype(f),
        "we_part": np.concatenate([np.array([[p == q for q in BIAS_PART] for p in WE_PART], f).repeat(EDGE_D, axis=0),
                                   np.eye(3, dtype=f), np.zeros((P - K_ATTR, 3), f)]),
        "iota": np.tile(k.astype(f), (P, 1)), "part": k.astype(f)[:, None],
        "node": (np.arange(TILES)[None, :] * P + k[:, None]).astype(f),
        "beta": a["L1_gnn_Wbeta"].reshape(3, D).T,
        "b_ih": a["L0_gnn_b_ih"].reshape(3, D).T, "b_hh": a["L0_gnn_b_hh"].reshape(3, D).T,
        "fb1": a["L1_gnn_b1"].reshape(4, D).T,
    }
    for name, key in (("b_msg", "L0_gnn_b_msg"), ("bq", "L1_gnn_bq"),
                      ("gamma0", "L0_gnn_ln_gamma"), ("beta0", "L0_gnn_ln_beta"), ("bskip", "L1_gnn_bskip"),
                      ("gn_w", "L1_gnn_gn_w"), ("gn_b", "L1_gnn_gn_b"), ("gn_ms", "L1_gnn_gn_ms"),
                      ("fb2", "L1_gnn_b2"), ("mlp_b", "L2_gnn_mlp_b"),
                      ("att_s1", "L3_gnn_att_src1"), ("att_d1", "L3_gnn_att_dst1"), ("g1b", "L3_gnn_b1"),
                      ("g1sb", "L3_gnn_bsk1"), ("att_s2", "L3_gnn_att_src2"), ("att_d2", "L3_gnn_att_dst2"),
                      ("g2b", "L3_gnn_b2"), ("g2sb", "L3_gnn_bsk2")):
        parts[name] = a[key].reshape(D, 1)
    return {
        "weights": np.concatenate([parts[n] for n, _ in WEIGHTS], axis=1),
        "x": x, "xT": np.ascontiguousarray(x.T),
        "src": np.ascontiguousarray(np.concatenate([a["src"], fill(EP - EDGES, 0)]).reshape(-1, P).T).view(
            np.uint32),
        "dst_line": np.concatenate([fill(1, -1), dst, fill(1, NP)]),
        "dst_col": np.ascontiguousarray(dst.reshape(CHUNKS, P).T),
        "We": np.concatenate([np.concatenate([a["L1_gnn_We"]] * 2, axis=1)] * len(WE_PART) + [np.concatenate(
            [a["L1_gnn_bk"], a["L1_gnn_bv"]])[None, :]] * len(BIAS_PART)),
        "zero": np.zeros((P, D), f),
        "ea10": np.ascontiguousarray(padded(a["edge_attr_10"], EP).T).reshape(P, FLAT),
        "ea128": padded(a["edge_attr_128"], EP),
    }


def kernel(**inputs):
    import concourse.bacc as bacc
    from concourse.bass_utils import run_bass_kernel_spmd

    arrays = host_arrays({k: np.asarray(v) for k, v in inputs.items()})
    nc = bacc.Bacc("TRN2", target_bir_lowering=False, num_devices=1)
    t = {k: nc.dram_tensor(f"in_{k}", v.shape, mybir.dt.from_np(v.dtype), kind="ExternalInput").ap()
         for k, v in arrays.items()}
    t["out"] = nc.dram_tensor("out", [NP, D], F32, kind="ExternalOutput").ap()
    gnn(nc, t)
    r = run_bass_kernel_spmd(nc, [{f"in_{k}": v for k, v in arrays.items()}], core_ids=[0])
    return r.results[0]["out"][:NODES]
```
